# Optimizing a Trainium2 kernel written in Bass

```python
import numpy as np
import jax
import jax.numpy as jnp

def _softmax(x, axis=-1):
    return jax.nn.softmax(x, axis=axis)

def _gelu(x):
    return jax.nn.gelu(x, approximate=True)

def _silu(x):
    return jax.nn.silu(x)

def _sigmoid(x):
    return jax.nn.sigmoid(x)

def _layernorm(x, axis=-1, eps=1e-05):
    m = jnp.mean(x, axis=axis, keepdims=True)
    v = jnp.var(x, axis=axis, keepdims=True)
    return (x - m) / jnp.sqrt(v + eps)

def _scatter_add(tgt, idx, src, axis=0):
    return tgt.at[idx].add(src)

def _segment_sum(src, seg, n):
    return jax.ops.segment_sum(src, seg, n)
kernel_name = 'mk_vit_tower_postln_d1_tok_img768_r4_9e58af'

def setup_inputs(seed: int=0):
    np.random.seed(seed)
    _w = jnp.asarray

    def _rec_inputs():
        import jax
        import jax.numpy as jnp
        _rk = jax.random.key(seed)
        x = 7.57192e-06 + 1.00007 * jax.random.normal(jax.random.fold_in(_rk, 1), (128, 3, 224, 224), jnp.float32)
        return x
    x = _rec_inputs()

    def _L0_tok_setup():
        import jax, jax.numpy as jnp
        import numpy as np
        B, C, H, W_IMG, P, D = (64, 3, 224, 224, 16, 192)
        N_PATCH = H // P * (W_IMG // P)
        SEQ = N_PATCH + 1

        def _patchify(x):
            b = x.shape[0]
            hp, wp = (H // P, W_IMG // P)
            x = x.reshape(b, C, hp, P, wp, P)
            x = x.transpose(0, 2, 4, 1, 3, 5)
            return x.reshape(b, hp * wp, C * P * P)
        key = jax.random.key(seed)
        k1, k2, k3, k4, k5 = jax.random.split(key, 5)
        in_feat = P * P * C
        return {'x': jax.random.normal(k1, (B, C, H, W_IMG), dtype=jnp.float32), 'W': jax.random.normal(k2, (in_feat, D), dtype=jnp.float32) * (1.0 / np.sqrt(in_feat)), 'b': jax.random.normal(k3, (D,), dtype=jnp.float32) * 0.02, 'pos_table': jax.random.normal(k4, (SEQ, D), dtype=jnp.float32) * 0.02, 'class_token': jax.random.normal(k5, (1, 1, D), dtype=jnp.float32)}
    _L0_tok_all = _L0_tok_setup()
    _L0_tok_in = {k: v for k, v in _L0_tok_all.items() if k in ('W', 'b', 'pos_table', 'class_token')}
    del _L0_tok_all

    def _L0_attn_setup():
        import jax, jax.numpy as jnp
        import numpy as np
        NUM_HEADS = 12
        ROPE_THETA = 10000.0

        def _rope_cos_sin(n, hd, dtype):
            inv_freq = 1.0 / ROPE_THETA ** (np.arange(0, hd, 2, dtype=np.float64) / hd)
            freqs = np.outer(np.arange(n, dtype=np.float64), inv_freq)
            emb = np.concatenate([freqs, freqs], axis=-1)
            return (jnp.asarray(np.cos(emb), dtype), jnp.asarray(np.sin(emb), dtype))

        def _apply_rope(t, cos, sin):
            half = t.shape[-1] // 2
            t1, t2 = (t[..., :half], t[..., half:])
            rot = jnp.concatenate([-t2, t1], axis=-1)
            return t * cos + rot * sin
        key = jax.random.key(seed)
        k1, k2, k3 = jax.random.split(key, 3)
        B, N, C = (8, 256, 192)
        x = jax.random.normal(k1, (B, N, C), dtype=jnp.float32)
        w_qkv = jax.random.normal(k2, (C, 3 * C), dtype=jnp.float32) * 0.02
        w_proj = jax.random.normal(k3, (C, C), dtype=jnp.float32) * 0.02
        b_proj = jnp.zeros((C,), dtype=jnp.float32)
        return {'x': x, 'w_qkv': w_qkv, 'w_proj': w_proj, 'b_proj': b_proj}
    _L0_attn_all = _L0_attn_setup()
    _L0_attn_in = {k: v for k, v in _L0_attn_all.items() if k in ('w_qkv', 'w_proj', 'b_proj')}
    del _L0_attn_all

    def _L0_ffn_setup():
        import jax, jax.numpy as jnp
        import numpy as np
        E = 128
        I = 464
        IS = 928
        K = 6
        G = 1
        TG = 1
        SCALE = 2.5
        CAP = 192

        def moe_forward(hidden_states, Wg, e_bias, W_gate_up, W_down, Wsg, Wsu, Wsd):
            B, S, H = hidden_states.shape
            x = hidden_states.reshape(-1, H)
            T = x.shape[0]
            logits = x.astype(jnp.float32) @ Wg.T
            sig = jax.nn.sigmoid(logits)
            choice = sig + e_bias[None, :]
            grp = choice.reshape(T, G, E // G)
            group_scores = jax.lax.top_k(grp, 2)[0].sum(-1)
            gidx = jax.lax.top_k(group_scores, TG)[1]
            gmask = jnp.zeros((T, G), jnp.float32).at[jnp.arange(T)[:, None], gidx].set(1.0)
            smask = jnp.repeat(gmask, E // G, axis=1)
            scores_for_choice = jnp.where(smask > 0, choice, 0.0)
            topk_idx = jax.lax.top_k(scores_for_choice, K)[1]
            topk_w = jnp.take_along_axis(sig, topk_idx, axis=1)
            topk_w = topk_w / (topk_w.sum(-1, keepdims=True) + 1e-20)
            topk_w = topk_w * SCALE
            P = T * K
            flat_e = topk_idx.reshape(-1)
            order = jnp.argsort(flat_e)
            se = flat_e[order]
            counts = jax.ops.segment_sum(jnp.ones(P, jnp.int32), flat_e, num_segments=E)
            starts = jnp.cumsum(counts) - counts
            pos = jnp.arange(P) - starts[se]
            buf_idx = jnp.where(pos < CAP, se * CAP + pos, E * CAP)
            tok_of_pair = (order // K).astype(jnp.int32)
            w_of_pair = topk_w.reshape(-1)[order]
            token_buf = jnp.zeros((E * CAP,), jnp.int32).at[buf_idx].set(tok_of_pair, mode='drop')
            w_buf = jnp.zeros((E * CAP,), x.dtype).at[buf_idx].set(w_of_pair.astype(x.dtype), mode='drop')
            xb = x[token_buf].reshape(E, CAP, H)
            gu = jnp.einsum('ech,ehf->ecf', xb, W_gate_up)
            g, u = jnp.split(gu, 2, axis=-1)
            inter = jax.nn.silu(g) * u
            yb = jnp.einsum('eci,eih->ech', inter, W_down)
            yb = yb * w_buf.reshape(E, CAP, 1)
            routed = jnp.zeros((T, H), x.dtype).at[token_buf].add(yb.reshape(E * CAP, H))
            shared = jax.nn.silu(x @ Wsg) * (x @ Wsu) @ Wsd
            return (routed + shared).reshape(B, S, H)
        key = jax.random.key(seed)
        ks = jax.random.split(key, 8)
        B, S, H = (1, 512, 192)
        sc = 0.02
        return {'hidden_states': jax.random.normal(ks[0], (B, S, H), jnp.float32), 'Wg': jax.random.normal(ks[1], (E, H), jnp.float32) * sc, 'e_bias': jnp.zeros((E,), jnp.float32), 'W_gate_up': jax.random.normal(ks[2], (E, H, 2 * I), jnp.float32) * sc, 'W_down': jax.random.normal(ks[3], (E, I, H), jnp.float32) * sc, 'Wsg': jax.random.normal(ks[4], (H, IS), jnp.float32) * sc, 'Wsu': jax.random.normal(ks[5], (H, IS), jnp.float32) * sc, 'Wsd': jax.random.normal(ks[6], (IS, H), jnp.float32) * sc}
    _L0_ffn_all = _L0_ffn_setup()
    _L0_ffn_in = {k: v for k, v in _L0_ffn_all.items() if k in ('Wg', 'e_bias', 'W_gate_up', 'W_down', 'Wsg', 'Wsu', 'Wsd')}
    del _L0_ffn_all
    return {'x': x, 'L0_tok_W': _L0_tok_in['W'], 'L0_tok_b': _L0_tok_in['b'], 'L0_tok_pos_table': _L0_tok_in['pos_table'], 'L0_tok_class_token': _L0_tok_in['class_token'], 'L0_attn_w_qkv': _L0_attn_in['w_qkv'], 'L0_attn_w_proj': _L0_attn_in['w_proj'], 'L0_attn_b_proj': _L0_attn_in['b_proj'], 'L0_ffn_Wg': _L0_ffn_in['Wg'], 'L0_ffn_e_bias': _L0_ffn_in['e_bias'], 'L0_ffn_W_gate_up': _L0_ffn_in['W_gate_up'], 'L0_ffn_W_down': _L0_ffn_in['W_down'], 'L0_ffn_Wsg': _L0_ffn_in['Wsg'], 'L0_ffn_Wsu': _L0_ffn_in['Wsu'], 'L0_ffn_Wsd': _L0_ffn_in['Wsd']}

def reference(x, L0_tok_W, L0_tok_b, L0_tok_pos_table, L0_tok_class_token, L0_attn_w_qkv, L0_attn_w_proj, L0_attn_b_proj, L0_ffn_Wg, L0_ffn_e_bias, L0_ffn_W_gate_up, L0_ffn_W_down, L0_ffn_Wsg, L0_ffn_Wsu, L0_ffn_Wsd):
    import jax
    import jax.numpy as jnp

    def _L0_tok_ref(x, W, b, pos_table, class_token):
        import jax, jax.numpy as jnp
        import numpy as np
        B, C, H, W_IMG, P, D = (64, 3, 224, 224, 16, 192)
        N_PATCH = H // P * (W_IMG // P)
        SEQ = N_PATCH + 1

        def _patchify(x):
            b = x.shape[0]
            hp, wp = (H // P, W_IMG // P)
            x = x.reshape(b, C, hp, P, wp, P)
            x = x.transpose(0, 2, 4, 1, 3, 5)
            return x.reshape(b, hp * wp, C * P * P)
        patches = _patchify(x)
        tokens = jnp.einsum('bnf,fd->bnd', patches, W) + b
        cls = jnp.broadcast_to(class_token, (x.shape[0], 1, D))
        seq = jnp.concatenate([cls, tokens], axis=1)
        return seq + pos_table[None, :, :]

    def _L0_attn_ref(x, w_qkv, w_proj, b_proj):
        import jax, jax.numpy as jnp
        import numpy as np
        NUM_HEADS = 12
        ROPE_THETA = 10000.0

        def _rope_cos_sin(n, hd, dtype):
            inv_freq = 1.0 / ROPE_THETA ** (np.arange(0, hd, 2, dtype=np.float64) / hd)
            freqs = np.outer(np.arange(n, dtype=np.float64), inv_freq)
            emb = np.concatenate([freqs, freqs], axis=-1)
            return (jnp.asarray(np.cos(emb), dtype), jnp.asarray(np.sin(emb), dtype))

        def _apply_rope(t, cos, sin):
            half = t.shape[-1] // 2
            t1, t2 = (t[..., :half], t[..., half:])
            rot = jnp.concatenate([-t2, t1], axis=-1)
            return t * cos + rot * sin
        B, N, C = x.shape
        H = NUM_HEADS
        hd = C // H
        scale = hd ** (-0.5)
        qkv = (x @ w_qkv).reshape(B, N, 3, H, hd).transpose(0, 3, 2, 1, 4)
        q, k, v = (qkv[:, :, 0], qkv[:, :, 1], qkv[:, :, 2])
        cos, sin = _rope_cos_sin(N, hd, x.dtype)
        q = _apply_rope(q, cos, sin)
        k = _apply_rope(k, cos, sin)
        attn = jax.nn.softmax(jnp.einsum('bhqd,bhkd->bhqk', q, k) * scale, axis=-1)
        out = jnp.einsum('bhqk,bhkd->bhqd', attn, v)
        out = out.transpose(0, 2, 1, 3).reshape(B, N, C)
        return out @ w_proj + b_proj

    def _L0_ffn_ref(hidden_states, Wg, e_bias, W_gate_up, W_down, Wsg, Wsu, Wsd):
        import jax, jax.numpy as jnp
        import numpy as np
        E = 128
        I = 464
        IS = 928
        K = 6
        G = 1
        TG = 1
        SCALE = 2.5
        CAP = 192

        def moe_forward(hidden_states, Wg, e_bias, W_gate_up, W_down, Wsg, Wsu, Wsd):
            B, S, H = hidden_states.shape
            x = hidden_states.reshape(-1, H)
            T = x.shape[0]
            logits = x.astype(jnp.float32) @ Wg.T
            sig = jax.nn.sigmoid(logits)
            choice = sig + e_bias[None, :]
            grp = choice.reshape(T, G, E // G)
            group_scores = jax.lax.top_k(grp, 2)[0].sum(-1)
            gidx = jax.lax.top_k(group_scores, TG)[1]
            gmask = jnp.zeros((T, G), jnp.float32).at[jnp.arange(T)[:, None], gidx].set(1.0)
            smask = jnp.repeat(gmask, E // G, axis=1)
            scores_for_choice = jnp.where(smask > 0, choice, 0.0)
            topk_idx = jax.lax.top_k(scores_for_choice, K)[1]
            topk_w = jnp.take_along_axis(sig, topk_idx, axis=1)
            topk_w = topk_w / (topk_w.sum(-1, keepdims=True) + 1e-20)
            topk_w = topk_w * SCALE
            P = T * K
            flat_e = topk_idx.reshape(-1)
            order = jnp.argsort(flat_e)
            se = flat_e[order]
            counts = jax.ops.segment_sum(jnp.ones(P, jnp.int32), flat_e, num_segments=E)
            starts = jnp.cumsum(counts) - counts
            pos = jnp.arange(P) - starts[se]
            buf_idx = jnp.where(pos < CAP, se * CAP + pos, E * CAP)
            tok_of_pair = (order // K).astype(jnp.int32)
            w_of_pair = topk_w.reshape(-1)[order]
            token_buf = jnp.zeros((E * CAP,), jnp.int32).at[buf_idx].set(tok_of_pair, mode='drop')
            w_buf = jnp.zeros((E * CAP,), x.dtype).at[buf_idx].set(w_of_pair.astype(x.dtype), mode='drop')
            xb = x[token_buf].reshape(E, CAP, H)
            gu = jnp.einsum('ech,ehf->ecf', xb, W_gate_up)
            g, u = jnp.split(gu, 2, axis=-1)
            inter = jax.nn.silu(g) * u
            yb = jnp.einsum('eci,eih->ech', inter, W_down)
            yb = yb * w_buf.reshape(E, CAP, 1)
            routed = jnp.zeros((T, H), x.dtype).at[token_buf].add(yb.reshape(E * CAP, H))
            shared = jax.nn.silu(x @ Wsg) * (x @ Wsu) @ Wsd
            return (routed + shared).reshape(B, S, H)
        return moe_forward(hidden_states, Wg, e_bias, W_gate_up, W_down, Wsg, Wsu, Wsd)
    h = _L0_tok_ref(x, L0_tok_W, L0_tok_b, L0_tok_pos_table, L0_tok_class_token)
    h = _layernorm(h + _L0_attn_ref(h, L0_attn_w_qkv, L0_attn_w_proj, L0_attn_b_proj), axis=-1)
    h = _layernorm(h + _L0_ffn_ref(h, L0_ffn_Wg, L0_ffn_e_bias, L0_ffn_W_gate_up, L0_ffn_W_down, L0_ffn_Wsg, L0_ffn_Wsu, L0_ffn_Wsd), axis=-1)
    return h

_drawn_inputs = setup_inputs


def setup_inputs(seed=0):
    import zlib

    import numpy as np

    out = dict(_drawn_inputs(seed))
    spreads = {'L0_attn_b_proj': (0.0, 0.1), 'L0_ffn_e_bias': (0.0, 0.8)}
    factors = {'L0_tok_b': 2.766,
     'L0_tok_pos_table': 2.85,
     'L0_attn_w_qkv': 8.0,
     'L0_attn_w_proj': 8.0,
     'L0_ffn_Wg': 8.0,
     'L0_ffn_W_gate_up': 8.0,
     'L0_ffn_W_down': 8.0}
    for name, (base, spread) in spreads.items():
        noise = np.random.default_rng([zlib.crc32(name.encode()), seed]).standard_normal(out[name].shape)
        drawn = base * np.exp(spread * noise) if base else spread * noise
        out[name] = jnp.asarray(drawn.astype(out[name].dtype))
    for name, factor in factors.items():
        out[name] = (out[name] * factor).astype(out[name].dtype)
    return out
```

```python
import numpy as np

import concourse.bass as bass
from concourse import mybir

F32 = mybir.dt.float32
BF16 = mybir.dt.bfloat16
I32 = mybir.dt.int32
ALU = mybir.AluOpType
ACT = mybir.ActivationFunctionType
AX_X = mybir.AxisListType.X

P = 128
PATCH = 16
HEADS = 12
HD = 16
TOP_K = 6
CAP = 192
ROUTE_SCALE = 2.5
LN_EPS = 1e-5
ROPE_THETA = 10000.0
BIG = 65536.0
SENTINEL = 3.0e38
TAKEN = -3.0e38
CHUNK = 512


class Shapes:

    def __init__(self, x, tok_w, pos, wg, w_gate_up, wsg):
        self.images, self.chans, self.height, self.width = x.shape
        self.gh, self.gw = self.height // PATCH, self.width // PATCH
        self.patches = self.gh * self.gw
        self.seq = pos.shape[0]
        self.dim = tok_w.shape[1]
        self.half = self.dim // 2
        self.half_heads = HEADS // 2
        self.rows = (self.seq + 1) // 2
        self.second = self.seq - self.rows
        self.tokens = self.images * self.seq
        self.chunks = -(-self.tokens // CHUNK)
        self.padded = self.chunks * CHUNK
        self.experts = wg.shape[0]
        self.slots = self.experts * CAP
        self.all_rows = self.padded + CAP
        self.inner = w_gate_up.shape[2] // 2
        self.shared = wsg.shape[1]
        self.ff_tile = 116
        self.ff = self.inner // self.ff_tile
        self.sff = self.shared // self.ff_tile
        self.row = self.dim + self.experts


def repeat(ap, axis, count):
    dims = [list(d) for d in ap.ap]
    dims.insert(axis, [0, count])
    return bass.AP(ap.tensor, ap.offset, dims)


def at_least(eng, sem, value):
    if isinstance(value, int) and value <= 0:
        return
    eng.wait_ge(sem, value)


def hold(eng, passed, sem, value):
    if isinstance(value, int) and value <= 0:
        return
    eng.wait_ge(sem, value)
    eng.sem_inc(passed, 1)


def attention_phase(nc, S, x, tok_w, tok_b, pos, cls, w_qkv, w_proj, b_proj,
                    t_ident, t_cos, t_sin, t_hmask, t_vmask, hx, acc, slot_token, t_empty):
    from contextlib import ExitStack

    R, HALF, SEQ, SEC, NP = S.rows, S.half, S.seq, S.second, S.patches
    HH, D, B = S.half_heads, S.dim, S.images
    KR = S.chans * PATCH
    PJ = PATCH // 2
    GW, GH = S.gw, S.gh
    DIAG = HALF + HD

    with ExitStack() as ctx:
        def sb(name, shape, dt=F32):
            return ctx.enter_context(nc.sbuf_tensor(name, shape, dt))

        def bank(name):
            return ctx.enter_context(nc.psum_tensor(name, [P, 512], F32))

        def sem(name):
            return ctx.enter_context(nc.semaphore(name))

        ident = sb("a_ident", [P, P])
        cos = sb("a_cos", [R, 2, HD])
        sin = sb("a_sin", [R, 2, HD])
        hmask = sb("a_hmask", [HALF, HH])
        vmask = sb("a_vmask", [R, 2])
        wt = sb("a_wt", [2 * KR, PJ, D])
        wqkv = sb("a_wqkv", [HALF, 2, 3 * D])
        wp = sb("a_wp", [HALF, 2, D])
        bproj = sb("a_bproj", [R, D])
        pos_rows = sb("a_pos_rows", [R, 2, D])
        add_rows = sb("a_add_rows", [R, 2, D])
        addT = sb("a_addT", [HALF, 2, SEQ])
        zeros = sb("a_zeros", [P, S.row])
        empty = sb("a_empty", [P, S.slots // P], I32)
        img = [sb(f"a_img{i}", [2 * KR, GH, S.width]) for i in range(2)]
        hT = [sb(f"a_hT{i}", [HALF, 2, SEQ]) for i in range(2)]
        rope_a = [sb(f"a_rope_a{i}", [R, 2 * D]) for i in range(2)]
        rope_b = [sb(f"a_rope_b{i}", [R, 2 * D]) for i in range(2)]
        qk = sb("a_qk", [R, 2, 2 * D])
        qT = [sb(f"a_qT{i}", [HALF, 2, SEQ]) for i in range(2)]
        kT = sb("a_kT", [HALF, 2, SEQ])
        k_own = [sb(f"a_k_own{i}", [HALF, HEADS, SEQ]) for i in range(2)]
        v_pad = [sb(f"a_v_pad{i}", [R, 2, 2, HH * DIAG]) for i in range(2)]
        neg_max = [sb(f"a_neg_max{i}", [R, HEADS, 2]) for i in range(2)]
        denom = [sb(f"a_denom{i}", [R, HEADS, 2]) for i in range(2)]
        prob = [sb(f"a_prob{i}", [R, 2, SEQ]) for i in range(2)]
        probT = [sb(f"a_probT{i}", [R, 2, SEQ]) for i in range(2)]
        rden = sb("a_rden", [R, HEADS, 2])
        rden_wide = sb("a_rden_wide", [R, 2, HEADS, HD])
        rdenT = sb("a_rdenT", [HALF, 2, SEQ])
        oT = sb("a_oT", [HALF, 2, SEQ])
        res = sb("a_res", [R, 2, D])
        res2 = sb("a_res2", [R, 2, D])
        stats = sb("a_stats", [R, 2, 6])
        moments = sb("a_moments", [R, 2, 2])
        rstd = sb("a_rstd", [R, 2])
        minus_half = sb("a_minus_half", [R, 2])
        h1 = [sb(f"a_h1{i}", [R, 2, D]) for i in range(2)]

        score = [bank("a_score0"), bank("a_score1")]
        turned = [bank("a_turned0"), bank("a_turned1")]
        out_b = bank("a_out")
        fa, fb, gb = bank("a_fa"), bank("a_fb"), bank("a_gb")

        half_set = sem("a_half_set")
        consts_in = sem("a_consts_in")
        zero_set = sem("a_zero_set")
        scratch_set = sem("a_scratch_set")
        add_ready, add_turned, cls_col = sem("a_add_ready"), sem("a_add_turned"), sem("a_cls_col")
        img_in = [sem("a_img_in0"), sem("a_img_in1")]
        tok_done = sem("a_tok_done")
        hT_ready = sem("a_hT_ready")
        qk_done, rope_step, qk_ready = sem("a_qk_done"), sem("a_rope_step"), sem("a_qk_ready")
        v_done, v_ready = sem("a_v_done"), sem("a_v_ready")
        turn_qk, qT_ready, kT_ready, k_own_ready = (sem("a_turn_qk"), sem("a_qT_ready"),
                                                    sem("a_kT_ready"), sem("a_k_own_ready"))
        score_done, max_ready, prob_ready = sem("a_score_done"), sem("a_max_ready"), sem("a_prob_ready")
        turned_done, probT_ready, pv_done = sem("a_turned_done"), sem("a_probT_ready"), sem("a_pv_done")
        rden_ready, wide_ready, rdenT_done, rdenT_ready = (sem("a_rden_ready"), sem("a_wide_ready"),
                                                           sem("a_rdenT_done"), sem("a_rdenT_ready"))
        oT_ready, proj_done, h_turned = sem("a_oT_ready"), sem("a_proj_done"), sem("a_h_turned")
        ln_step, h1_ready = sem("a_ln_step"), sem("a_h1_ready")
        h1_out = [sem("a_h1_out0"), sem("a_h1_out1")]

        CONSTS = 14 * 16
        IMG_DMAS = 2 * S.chans * 16

        x_rows = x.rearrange("b c (hp ph) w -> b c ph hp w", ph=PATCH)
        w_rows = tok_w.rearrange("(r g j) d -> g r j d", g=2, j=PJ)

        pool_passed, dve_passed = sem("a_pool_passed"), sem("a_dve_passed")
        block = ctx.enter_context(nc.Block())

        def images(eng, body):
            body(0, 0, 0, True, False)
            body(1, 0, 1, False, B == 2)
            if B > 4:
                with eng.Fori(1, B // 2 - 1) as k:
                    body(k * 2, k, 0, False, False)
                    body(k * 2 + 1, k, 1, False, False)
            if B > 2:
                k = B // 2 - 1
                body(2 * k, k, 0, False, False)
                body(2 * k + 1, k, 1, False, True)

        @block.sync
        def _(sp):
            for dst, src in ((ident[:], t_ident), (cos[:], t_cos), (sin[:], t_sin), (hmask[:], t_hmask),
                             (vmask[:], t_vmask), (wt[0:KR], w_rows[0]), (wt[KR:2 * KR], w_rows[1]),
                             (wqkv[:], w_qkv.rearrange("(k p) n -> p k n", k=2)),
                             (wp[:], w_proj.rearrange("(k p) n -> p k n", k=2)),
                             (bproj[:], b_proj.partition_broadcast(R)),
                             (pos_rows[:, 0, :], pos[0:R, :]), (pos_rows[:, 1, :], pos[SEC:SEQ, :]),
                             (add_rows[:, 1, :], tok_b.partition_broadcast(R)),
                             (add_rows[1:R, 0, :], tok_b.partition_broadcast(R - 1))):
                sp.dma_start(dst, src).then_inc(consts_in, 16)
            sp.dma_start(add_rows[0:1, 0, :], cls[0]).then_inc(consts_in, 16)

            def load(n, i):
                for g in range(2):
                    for c in range(S.chans):
                        r = g * KR + c * PATCH
                        sp.dma_start(img[i][r:r + PATCH, :, 0:S.width - PJ * g],
                                     x_rows[n, c][:, :, PJ * g:S.width]).then_inc(img_in[i], 16)

            def store(n, i):
                sp.wait_ge(h1_ready, n + 1)
                sp.dma_start(hx[bass.ds(n * SEQ, R), 0:D], h1[i][:, 0, :]).then_inc(h1_out[i], 16)
                sp.dma_start(hx[bass.ds(n * SEQ + R, R - 1), 0:D], h1[i][1:R, 1, :]).then_inc(h1_out[i], 16)

            load(0, 0)
            load(1, 1)
            sp.dma_start(empty[:], t_empty).then_inc(scratch_set, 16)
            sp.wait_ge(scratch_set, 16)
            sp.dma_start(slot_token.rearrange("(p n) a -> p (n a)", p=P), empty[:]).then_inc(scratch_set, 16)
            sp.wait_ge(zero_set, 1)
            r, k = S.tokens, 2
            while r < S.all_rows:
                m = min(P, S.all_rows - r)
                sp.dma_start(hx[r:r + m, :], zeros[0:m, :]).then_inc(scratch_set, 16)
                r, k = r + m, k + 1
            sp.dma_start(acc[S.padded:S.padded + P, :], zeros[:, 0:D]).then_inc(scratch_set, 16)
            sp.dma_start(acc[S.padded + P:S.all_rows, :], zeros[0:CAP - P, 0:D]).then_inc(scratch_set, 16)
            sp.wait_ge(scratch_set, 16 * (k + 2))

            def body(n, k, odd, first, last):
                if not last and not (isinstance(n, int) and n + 2 >= B):
                    sp.wait_ge(tok_done, n + 1)
                    load(n + 2, odd)
                if not first:
                    store(n - 1, 1 - odd)

            images(sp, body)
            store(B - 1, (B - 1) % 2)
            for i in range(2):
                sp.wait_ge(h1_out[i], 32 * (B // 2))

        @block.gpsimd
        def _(pool):
            pool.memset(minus_half[:], -0.5).then_inc(half_set, 1)
            hold(pool, pool_passed, half_set, 1)
            hold(pool, pool_passed, consts_in, CONSTS + 16)

            def own(m, i):
                hold(pool, pool_passed, kT_ready, m + 1)
                hold(pool, pool_passed, score_done, (m - 1) * HEADS)
                for h in range(HEADS):
                    pool.tensor_scalar(k_own[i][:, h, :], kT[:, h // HH, :], hmask[:, h % HH:h % HH + 1], None,
                                       ALU.mult).then_inc(k_own_ready, 1)

            def inverse_deviation(n):
                hold(pool, pool_passed, ln_step, n * 9 + 6)
                pool.tensor_scalar(rstd[:], moments[:, :, 1], LN_EPS, None, ALU.add).then_inc(ln_step, 1)
                hold(pool, pool_passed, ln_step, n * 9 + 7)
                pool.tensor_tensor(rstd[:], rstd[:], minus_half[:], ALU.pow).then_inc(ln_step, 1)

            def body(n, k, odd, first, last):
                if not first:
                    inverse_deviation(n - 1)
                if not last:
                    own(n + 1, 1 - odd)

            own(0, 0)
            images(pool, body)
            inverse_deviation(B - 1)

        @block.tensor
        def _(pe):
            pe.wait_ge(consts_in, CONSTS + 16)
            pe.wait_ge(add_ready, 1)
            for kh in range(2):
                for t in range(2):
                    mm = pe.transpose(fb[0:HALF, kh * SEQ + t * SEC:kh * SEQ + t * SEC + R],
                                      add_rows[:, t, kh * HALF:(kh + 1) * HALF], ident[0:R, 0:R])
            mm.then_inc(add_turned, 1)

            def embed(m, mk, i, f, prologue=False):
                if f == 0:
                    pe.wait_ge(img_in[i], (mk + 1) * IMG_DMAS)
                    if not prologue:
                        pe.wait_ge(qT_ready, m)
                for j in range(PJ):
                    mm = pe.matmul(fa[0:HALF, f * NP:(f + 1) * NP], wt[:, j, f * HALF:(f + 1) * HALF],
                                   img[i][:, :, j:j + PATCH * (GW - 1) + 1:PATCH], start=(j == 0), stop=(j == PJ - 1))
                if f == 1:
                    mm.then_inc(tok_done, 1)

            def project_qk(m, i, t, prologue=False):
                if t == 0:
                    pe.wait_ge(hT_ready, m + 1)
                    if not prologue:
                        pe.wait_ge(qk_ready, 2 * m)
                else:
                    if not prologue:
                        pe.wait_ge(kT_ready, m)
                        at_least(pe, ln_step, (m - 2) * 9 + 1)
                for kh in range(2):
                    mm = pe.matmul((fa, fb)[t][0:R, 0:2 * D], hT[i][:, kh, t * SEC:t * SEC + R], wqkv[:, kh, 0:2 * D],
                                   start=(kh == 0), stop=(kh == 1))
                mm.then_inc(qk_done, 1)

            def project_v(m, i, prologue=False):
                at_least(pe, ln_step, (m - 2) * 9 + 2)
                for t in range(2):
                    for kh in range(2):
                        mm = pe.matmul(gb[0:R, t * D:(t + 1) * D], hT[i][:, kh, t * SEC:t * SEC + R],
                                       wqkv[:, kh, 2 * D:3 * D], start=(kh == 0), stop=(kh == 1))
                mm.then_inc(v_done, 1)

            def turn(m):
                pe.wait_ge(qk_ready, 2 * (m + 1))
                for w, b in ((0, fa), (1, fb)):
                    for kh in range(2):
                        for t in range(2):
                            c = w * D + kh * HALF
                            mm = pe.transpose(b[0:HALF, kh * SEQ + t * SEC:kh * SEQ + t * SEC + R],
                                              qk[:, t, c:c + HALF], ident[0:R, 0:R])
                    mm.then_inc(turn_qk, 1)

            def scores(n, i, h, g):
                if h == 0:
                    pe.wait_ge(qT_ready, n + 1)
                pe.wait_ge(k_own_ready, g + 1)
                at_least(pe, prob_ready, g - 1)
                for t in range(2):
                    mm = pe.matmul(score[h % 2][0:R, t * SEQ:(t + 1) * SEQ], qT[i][:, h // HH, t * SEC:t * SEC + R],
                                   k_own[i][:, h, :], start=True, stop=True)
                mm.then_inc(score_done, 1)

            def turn_probs(h, g):
                pe.wait_ge(prob_ready, g + 1)
                at_least(pe, probT_ready, g - 1)
                for kt in range(2):
                    for t in range(2):
                        mm = pe.transpose(turned[h % 2][0:R, kt * SEQ + t * SEC:kt * SEQ + t * SEC + R],
                                          prob[h % 2][:, t, kt * SEC:kt * SEC + R], ident[0:R, 0:R])
                mm.then_inc(turned_done, 1)

            def attend(n, i, h, g):
                pe.wait_ge(probT_ready, g + 1)
                if h == 0:
                    pe.wait_ge(v_ready, n + 1)
                    at_least(pe, oT_ready, n)
                half, j = h // HH, h % HH
                for kt in range(2):
                    mm = pe.matmul(out_b[0:HALF, half * SEQ:(half + 1) * SEQ],
                                   v_pad[i][:, kt, half, j * HALF:(j + 1) * HALF], probT[h % 2][:, kt, :],
                                   start=(j == 0 and kt == 0), stop=(j == HH - 1 and kt == 1))
                mm.then_inc(pv_done, 1)

            def turn_denoms(n):
                pe.wait_ge(wide_ready, n + 1)
                at_least(pe, v_ready, n + 2 if not isinstance(n, int) or n + 2 <= B else B)
                for kh in range(2):
                    for t in range(2):
                        src = rden_wide[:, t, kh * HH:(kh + 1) * HH, :].rearrange("p h d -> p (h d)")
                        mm = pe.transpose(gb[0:HALF, kh * SEQ + t * SEC:kh * SEQ + t * SEC + R], src, ident[0:R, 0:R])
                mm.then_inc(rdenT_done, 1)

            def project_out(n, i, last):
                pe.wait_ge(kT_ready, n + 1 if last else n + 2)
                for t in range(2):
                    for kh in range(2):
                        mm = pe.transpose(fb[0:R, t * D + kh * HALF:t * D + (kh + 1) * HALF],
                                          hT[i][:, kh, t * SEC:t * SEC + R], ident[0:HALF, 0:HALF])
                mm.then_inc(h_turned, 1)
                pe.wait_ge(oT_ready, n + 1)
                for t in range(2):
                    for kh in range(2):
                        mm = pe.matmul(gb[0:R, t * D:(t + 1) * D], oT[:, kh, t * SEC:t * SEC + R], wp[:, kh, :],
                                       start=(kh == 0), stop=(kh == 1))
                mm.then_inc(proj_done, 1)

            pe.wait_ge(cls_col, 1)
            embed(0, 0, 0, 0, True)
            embed(0, 0, 0, 1, True)
            project_qk(0, 0, 0, True)
            project_qk(0, 0, 1, True)
            project_v(0, 0, True)
            turn(0)
            scores(0, 0, 0, 0)
            scores(0, 0, 1, 1)

            def body(n, k, odd, first, last):
                mk = k + odd
                for h in range(HEADS):
                    g = n * HEADS + h
                    turn_probs(h, g)
                    if h + 2 < HEADS:
                        scores(n, odd, h + 2, g + 2)
                    elif not last:
                        scores(n + 1, 1 - odd, h + 2 - HEADS, g + 2)
                    if h == 0 and not first:
                        attend(n - 1, 1 - odd, HEADS - 1, g - 1)
                        turn_denoms(n - 1)
                    if not last:
                        if h == 1:
                            embed(n + 1, mk, 1 - odd, 0)
                        if h == 3:
                            embed(n + 1, mk, 1 - odd, 1)
                        if h in (4, 5):
                            project_qk(n + 1, 1 - odd, h - 4)
                        if h == 6:
                            project_v(n + 1, 1 - odd)
                        if h == 8:
                            turn(n + 1)
                    if h == 2 and not first:
                        project_out(n - 1, 1 - odd, False)
                    if h > 0:
                        attend(n, odd, h - 1, g - 1)

            images(pe, body)
            attend(B - 1, (B - 1) % 2, HEADS - 1, B * HEADS - 1)
            turn_denoms(B - 1)
            project_out(B - 1, (B - 1) % 2, True)

        @block.scalar
        def _(act):
            act.wait_ge(consts_in, CONSTS + 16)

            def turn_copy(m, i):
                act.wait_ge(turn_qk, 2 * m + 1)
                at_least(act, score_done, (m - 1) * HEADS)
                act.activation(qT[i].rearrange("p k s -> p (k s)"), fa[0:HALF, 0:2 * SEQ], ACT.Copy,
                               scale=HD ** -0.5).then_inc(qT_ready, 1)
                act.wait_ge(turn_qk, 2 * m + 2)
                at_least(act, k_own_ready, m * HEADS)
                act.activation(kT.rearrange("p k s -> p (k s)"), fb[0:HALF, 0:2 * SEQ], ACT.Copy).then_inc(kT_ready, 1)

            def softmax(i, h, g):
                act.wait_ge(max_ready, g + 1)
                at_least(act, turned_done, g - 1)
                for t in range(2):
                    op = act.activation(prob[h % 2][:, t, :], score[h % 2][0:R, t * SEQ:(t + 1) * SEQ], ACT.Exp,
                                        bias=neg_max[i][:, h, t:t + 1], accum_out=denom[i][:, h, t:t + 1])
                op.then_inc(prob_ready, 1)

            def denom_copy(n):
                act.wait_ge(rdenT_done, n + 1)
                at_least(act, oT_ready, n)
                act.activation(rdenT.rearrange("p k s -> p (k s)"), gb[0:HALF, 0:2 * SEQ], ACT.Copy)\
                   .then_inc(rdenT_ready, 1)

            turn_copy(0, 0)
            softmax(0, 0, 0)
            softmax(0, 1, 1)

            def body(n, k, odd, first, last):
                for h in range(HEADS):
                    g = n * HEADS + h
                    if h + 2 < HEADS:
                        softmax(odd, h + 2, g + 2)
                    elif not last:
                        softmax(1 - odd, h + 2 - HEADS, g + 2)
                    if h == 0 and not first:
                        denom_copy(n - 1)
                    if h == 8 and not last:
                        turn_copy(n + 1, 1 - odd)

            images(act, body)
            denom_copy(B - 1)

        @block.vector
        def _(dve):
            dve.memset(zeros[:], 0.0).then_inc(zero_set, 1)
            for i in range(2):
                dve.memset(v_pad[i].rearrange("p a b c -> p (a b c)"), 0.0).then_inc(zero_set, 1)
            dve.wait_ge(consts_in, CONSTS + 16)
            dve.tensor_tensor(add_rows[:], add_rows[:], pos_rows[:], ALU.add).then_inc(add_ready, 1)
            dve.wait_ge(add_turned, 1)
            dve.tensor_copy(addT.rearrange("p k s -> p (k s)"), fb[0:HALF, 0:2 * SEQ]).then_inc(add_ready, 1)
            dve.wait_ge(add_ready, 2)
            for i in range(2):
                op = dve.tensor_copy(hT[i][:, :, 0:1], addT[:, :, 0:1])
            op.then_inc(cls_col, 1)
            dve.wait_ge(zero_set, 3)

            def add_position(m, i):
                dve.wait_ge(tok_done, m + 1)
                at_least(dve, h_turned, m - 1)
                dve.tensor_tensor(hT[i][:, :, 1:SEQ], fa[0:HALF, 0:2 * NP].rearrange("p (k s) -> p k s", k=2),
                                  addT[:, :, 1:SEQ], ALU.add).then_inc(hT_ready, 1)

            def rope(m, t):
                dve.wait_ge(qk_done, 2 * m + t + 1)
                at_least(dve, qk_ready, 2 * m + t - 1)
                b = (fa, fb)[t]
                src = b[0:R, 0:2 * D]
                heads = src.rearrange("p (h d) -> p h d", d=HD)
                dims = [list(d) for d in src.ap]
                swap = bass.AP(src.tensor, src.offset + HD // 2, [dims[0], [HD, 2 * HEADS], [-(HD // 2), 2], [1, HD // 2]])
                c = repeat(cos[:, t, :], 1, 2 * HEADS)
                s = repeat(sin[:, t, :].rearrange("p (a b) -> p a b", a=2), 1, 2 * HEADS)
                dve.tensor_tensor(rope_a[t].rearrange("p (h d) -> p h d", d=HD), heads, c, ALU.mult).then_inc(rope_step, 1)
                dve.tensor_tensor(rope_b[t].rearrange("p (h a b) -> p h a b", a=2, b=HD // 2), swap, s, ALU.mult)\
                   .then_inc(rope_step, 1)
                dve.wait_ge(rope_step, (2 * m + t) * 2 + 2)
                at_least(dve, turn_qk, 2 * m)
                dve.tensor_tensor(qk[:, t, :], rope_a[t][:], rope_b[t][:], ALU.add).then_inc(qk_ready, 1)

            def place_values(m, i):
                dve.wait_ge(v_done, m + 1)
                at_least(dve, pv_done, (m - 1) * HEADS)
                for t in range(2):
                    own = v_pad[i][:, t, :, :].rearrange("p a (h w) -> p a h w", w=DIAG)[:, :, :, 0:HD]
                    src = gb[0:R, t * D:(t + 1) * D].rearrange("p (a h d) -> p a h d", a=2, d=HD)
                    op = dve.tensor_scalar(own, src, vmask[:, t:t + 1], None, ALU.mult)
                op.then_inc(v_ready, 1)

            def maxima(i, h, g):
                dve.wait_ge(score_done, g + 1)
                dve.tensor_reduce(neg_max[i][:, h, :], score[h % 2][0:R, 0:2 * SEQ].rearrange("p (t s) -> p t s", t=2),
                                  AX_X, ALU.max, negate=True).then_inc(max_ready, 1)

            def probs_copy(h, g):
                dve.wait_ge(turned_done, g + 1)
                at_least(dve, pv_done, g - 1)
                dve.tensor_copy(probT[h % 2].rearrange("p k s -> p (k s)"), turned[h % 2][0:R, 0:2 * SEQ])\
                   .then_inc(probT_ready, 1)

            def denoms(n, i):
                dve.wait_ge(prob_ready, (n + 1) * HEADS)
                dve.reciprocal(rden.rearrange("p h t -> p (h t)"), denom[i].rearrange("p h t -> p (h t)"))\
                   .then_inc(rden_ready, 1)
                dve.wait_ge(rden_ready, n + 1)
                at_least(dve, rdenT_done, n)
                dve.tensor_copy(rden_wide[:], repeat(rden.rearrange("p h t -> p t h"), 3, HD)).then_inc(wide_ready, 1)

            def normalise_heads(n):
                dve.wait_ge(rdenT_ready, n + 1)
                dve.wait_ge(pv_done, (n + 1) * HEADS)
                dve.tensor_tensor(oT.rearrange("p k s -> p (k s)"), out_b[0:HALF, 0:2 * SEQ],
                                  rdenT.rearrange("p k s -> p (k s)"), ALU.mult).then_inc(oT_ready, 1)

            def layernorm(n, k_out, i):
                dve.wait_ge(h_turned, n + 1)
                dve.tensor_tensor(res[:], fb[0:R, 0:2 * D].rearrange("p (t d) -> p t d", t=2),
                                  repeat(bproj[:], 1, 2), ALU.add).then_inc(ln_step, 1)
                dve.wait_ge(proj_done, n + 1)
                dve.wait_ge(ln_step, n * 9 + 1)
                dve.tensor_tensor(res2[:], gb[0:R, 0:2 * D].rearrange("p (t d) -> p t d", t=2), res[:], ALU.add)\
                   .then_inc(ln_step, 1)
                dve.wait_ge(ln_step, n * 9 + 2)
                for t in range(2):
                    dve.bn_stats(stats[:, t, :], res2[:, t, :]).then_inc(ln_step, 1)
                hold(dve, dve_passed, ln_step, n * 9 + 4)
                for t in range(2):
                    dve.bn_aggr(moments[:, t, :], stats[:, t, :]).then_inc(ln_step, 1)
                dve.wait_ge(ln_step, n * 9 + 8)
                at_least(dve, h1_out[i], k_out * 32)
                for t in range(2):
                    op = dve.tensor_scalar(h1[i][:, t, :], res2[:, t, :], moments[:, t, 0:1], rstd[:, t:t + 1],
                                           ALU.subtract, ALU.mult)
                    op.then_inc((ln_step, h1_ready)[t], 1)

            add_position(0, 0)
            rope(0, 0)
            rope(0, 1)
            place_values(0, 0)
            maxima(0, 0, 0)
            maxima(0, 1, 1)

            def body(n, k, odd, first, last):
                for h in range(HEADS):
                    g = n * HEADS + h
                    if h == 0 and not first:
                        denoms(n - 1, 1 - odd)
                    probs_copy(h, g)
                    if h + 2 < HEADS:
                        maxima(odd, h + 2, g + 2)
                    elif not last:
                        maxima(1 - odd, h + 2 - HEADS, g + 2)
                    if not first:
                        if h == 0:
                            normalise_heads(n - 1)
                        if h == 2:
                            layernorm(n - 1, k - 1 + odd, 1 - odd)
                    if not last:
                        if h == 3:
                            add_position(n + 1, 1 - odd)
                        if h == 4:
                            rope(n + 1, 0)
                        if h == 5:
                            rope(n + 1, 1)
                        if h == 6:
                            place_values(n + 1, 1 - odd)

            images(dve, body)
            denoms(B - 1, (B - 1) % 2)
            normalise_heads(B - 1)
            layernorm(B - 1, (B - 1) // 2, (B - 1) % 2)


def tables(S):
    inv_freq = 1.0 / ROPE_THETA ** (np.arange(0, HD, 2, dtype=np.float64) / HD)
    freqs = np.outer(np.arange(S.seq, dtype=np.float64), inv_freq)
    cos = np.cos(np.concatenate([freqs, freqs], axis=-1)).astype(np.float32)
    sin = np.sin(np.concatenate([-freqs, freqs], axis=-1)).astype(np.float32)
    tiles = [slice(0, S.rows), slice(S.second, S.seq)]
    hmask = np.kron(np.eye(S.half_heads, dtype=np.float32), np.ones((HD, 1), np.float32))
    vmask = np.ones((S.rows, 2), np.float32)
    vmask[0, 1] = 0.0
    before = np.triu(np.ones((P, P), np.float32), 1)
    first_slot = np.arange(S.experts, dtype=np.float32) * CAP
    return {
        "ident": np.eye(P, dtype=np.float32),
        "cos": np.stack([cos[t] for t in tiles], axis=1),
        "sin": np.stack([sin[t] for t in tiles], axis=1),
        "hmask": hmask,
        "vmask": vmask,
        "before": before,
        "slot_base": np.tile(BIG - first_slot, (P, 1)).astype(np.float32),
        "slot_limit": np.tile(BIG - first_slot - CAP, (P, 1)).astype(np.float32),
        "token_id": (np.arange(CHUNK // P)[None, :] * P + np.arange(P)[:, None]).astype(np.float32),
        "empty": (S.padded + np.arange(S.slots) % CAP).astype(np.int32).reshape(P, -1),
    }


def routing_phase(nc, S, wg, e_bias, wsg, wsu, wsd, t_ident, t_before, t_base, t_limit, t_token, hx, acc, slot_token):
    from contextlib import ExitStack

    HALF, D, E, NC, FT, SFF = S.half, S.dim, S.experts, S.chunks, S.ff_tile, S.sff
    T = CHUNK // P
    STEPS = 28

    with ExitStack() as ctx:
        def sb(name, shape, dt=F32):
            return ctx.enter_context(nc.sbuf_tensor(name, shape, dt))

        def bank(name):
            return ctx.enter_context(nc.psum_tensor(name, [P, 512], F32))

        def sem(name):
            return ctx.enter_context(nc.semaphore(name))

        ident = sb("b_ident", [P, P])
        before_f = sb("b_before_f", [P, P])
        before = sb("b_before", [P, P], BF16)
        ones = sb("b_ones", [P, P], BF16)
        base = sb("b_base", [P, E])
        limit = sb("b_limit", [P, E])
        bias = sb("b_bias", [P, E])
        wg_rows = sb("b_wg_rows", [E, D])
        wgT = sb("b_wgT", [HALF, 2, E])
        w_g = sb("b_w_g", [HALF, 2, S.shared])
        w_u = sb("b_w_u", [HALF, 2, S.shared])
        w_d = sb("b_w_d", [FT, SFF, D])
        token_f = [sb(f"b_token_f{i}", [P, T]) for i in range(2)]
        token_i = [sb(f"b_token_i{i}", [P, T], I32) for i in range(2)]
        rows = [sb(f"b_rows{i}", [P, T, D]) for i in range(2)]
        xT = sb("b_xT", [HALF, 2, CHUNK])
        sig = sb("b_sig", [P, T, E])
        choice = sb("b_choice", [P, T, E + 2])
        top = sb("b_top", [P, T, 8])
        replaced = sb("b_replaced", [P, T, E + 2])
        mask = sb("b_mask", [P, T, E], BF16)
        place = sb("b_place", [P, T, E])
        place_m = sb("b_place_m", [P, T, E])
        in_cap = sb("b_in_cap", [P, T, E])
        place_v = sb("b_place_v", [P, T, E])
        slots8 = sb("b_slots8", [P, T, 8])
        slot_i = [sb(f"b_slot_i{i}", [P, T, 8], I32) for i in range(2)]
        wsel = sb("b_wsel", [P, T, E])
        wsum = sb("b_wsum", [P, T])
        wden = sb("b_wden", [P, T])
        winv = sb("b_winv", [P, T])
        weight = [sb(f"b_weight{i}", [P, T, E]) for i in range(2)]
        silu_g = [sb(f"b_silu{i}", [FT, CHUNK]) for i in range(2)]
        inter = sb("b_inter", [FT, SFF, CHUNK])
        total = [sb(f"b_total{i}", [P, T, D]) for i in range(2)]

        t0, t1, gate_b, down_b = bank("b_t0"), bank("b_t1"), bank("b_gate"), bank("b_down")
        g_b = [bank("b_g0"), bank("b_g1")]
        u_b = [bank("b_u0"), bank("b_u1")]

        consts_in, setup = sem("b_consts_in"), sem("b_setup")
        wg_turned, wgT_ready = sem("b_wg_turned"), sem("b_wgT_ready")
        rows_in = [sem("b_rows_in0"), sem("b_rows_in1")]
        x_turned, xT0_ready, xT1_ready = sem("b_x_turned"), sem("b_xT0_ready"), sem("b_xT1_ready")
        gate_done, sig_ready = sem("b_gate_done"), sem("b_sig_ready")
        route_step, mask_ready, prefix_done = sem("b_route_step"), sem("b_mask_ready"), sem("b_prefix_done")
        slots_ready, weight_ready = sem("b_slots_ready"), sem("b_weight_ready")
        up_done, silu_ready, inter_ready = sem("b_up_done"), sem("b_silu_ready"), sem("b_inter_ready")
        down_done, total_ready = sem("b_down_done"), sem("b_total_ready")
        weight_out = [sem("b_weight_out0"), sem("b_weight_out1")]
        total_out = [sem("b_total_out0"), sem("b_total_out1")]
        scattered = [sem("b_scattered0"), sem("b_scattered1")]
        token_step = sem("b_token_step")

        SCATTERS = T * TOP_K * 16
        CONSTS = 11 * 16

        pool_passed, dve_passed = sem("b_pool_passed"), sem("b_dve_passed")
        block = ctx.enter_context(nc.Block())

        def chunks(eng, body):
            body(0, 0, 0, True, NC == 1)
            if NC == 1:
                return
            body(1, 0, 1, False, NC == 2)
            full = (NC - 3) // 2
            if full > 0:
                with eng.Fori(1, 1 + full) as k:
                    body(k * 2, k, 0, False, False)
                    body(k * 2 + 1, k, 1, False, False)
            for c in range(2 + 2 * max(full, 0), NC):
                body(c, c // 2, c % 2, False, c == NC - 1)

        def tile_rows(c, lo, width, handle):
            v = handle[bass.ds(c * CHUNK, CHUNK), lo:lo + width]
            return v.rearrange("(t p) d -> p t d", p=P)

        @block.sync
        def _(sp):
            for dst, src in ((ident[:], t_ident), (before_f[:], t_before), (base[:], t_base), (limit[:], t_limit),
                             (bias[:], e_bias.partition_broadcast(P)), (wg_rows[:], wg),
                             (w_g[:], wsg.rearrange("(k p) n -> p k n", k=2)),
                             (w_u[:], wsu.rearrange("(k p) n -> p k n", k=2)),
                             (w_d[:], wsd.rearrange("(j p) n -> p j n", p=FT)),
                             (token_f[0][:], t_token), (token_f[1][:], t_token)):
                sp.dma_start(dst, src).then_inc(consts_in, 16)

            def load(c, i):
                sp.dma_start(rows[i][:], tile_rows(c, 0, D, hx)).then_inc(rows_in[i], 16)

            load(0, 0)
            if NC > 1:
                load(1, 1)

            def body(c, k, odd, first, last):
                sp.wait_ge(weight_ready, c + 1)
                sp.dma_start(tile_rows(c, D, E, hx), weight[odd][:]).then_inc(weight_out[odd], 16)
                sp.wait_ge(total_ready, 2 * (c + 1))
                sp.dma_start(tile_rows(c, 0, D, acc), total[odd][:]).then_inc(total_out[odd], 16)
                if not (isinstance(c, int) and c + 2 >= NC):
                    load(c + 2, odd)

            chunks(sp, body)
            for i in range(2):
                n = (NC + 1 - i) // 2
                if n:
                    sp.wait_ge(weight_out[i], 16 * n)
                    sp.wait_ge(total_out[i], 16 * n)
                    sp.wait_ge(scattered[i], SCATTERS * n)

        @block.gpsimd
        def _(pool):
            pool.memset(ones[:], 1.0).then_inc(setup, 1)
            hold(pool, pool_passed, consts_in, CONSTS)
            pool.tensor_scalar(token_f[1][:], token_f[1][:], float(CHUNK), None, ALU.add).then_inc(token_step, 1)

            def body(c, k, odd, first, last):
                hold(pool, pool_passed, token_step, 2 * c + 1 if not first else 1)
                hold(pool, pool_passed, scattered[odd], k * SCATTERS)
                pool.tensor_copy(token_i[odd][:], token_f[odd][:]).then_inc(token_step, 1)
                hold(pool, pool_passed, token_step, 2 * c + 2)
                pool.tensor_scalar(token_f[odd][:], token_f[odd][:], float(2 * CHUNK), None, ALU.add)\
                    .then_inc(token_step, 1)
                hold(pool, pool_passed, slots_ready, c + 1)
                for t in range(T):
                    for j in range(TOP_K):
                        pool.indirect_dma_start(
                            slot_token, bass.IndirectOffsetOnAxis(ap=slot_i[odd][:, t, j:j + 1], axis=0),
                            token_i[odd][:, t:t + 1], None, bounds_check=S.slots - 1, oob_is_err=False,
                        ).then_inc(scattered[odd], 16)

            chunks(pool, body)

        @block.tensor
        def _(pe):
            pe.wait_ge(consts_in, CONSTS)
            for kh in range(2):
                mm = pe.transpose(gate_b[0:HALF, kh * P:kh * P + E], wg_rows[:, kh * HALF:(kh + 1) * HALF], ident[0:E, 0:E])
            mm.then_inc(wg_turned, 1)
            pe.wait_ge(setup, 2)
            pe.wait_ge(wgT_ready, 1)

            def turn(c, k, i):
                pe.wait_ge(rows_in[i], (k + 1) * 16)
                at_least(pe, route_step, (c - 1) * STEPS + 12)
                for kh in range(2):
                    for t in range(T):
                        mm = pe.transpose((t0, t1)[kh][0:HALF, t * P:(t + 1) * P], rows[i][:, t, kh * HALF:(kh + 1) * HALF],
                                          ident[:])
                mm.then_inc(x_turned, 1)

            def gate(c):
                pe.wait_ge(xT0_ready, c + 1)
                pe.wait_ge(xT1_ready, c + 1)
                at_least(pe, total_ready, 2 * c)
                for t in range(T):
                    for kh in range(2):
                        mm = pe.matmul(gate_b[:, t * E:(t + 1) * E], xT[:, kh, t * P:(t + 1) * P], wgT[:, kh, :],
                                       start=(kh == 0), stop=(kh == 1))
                mm.then_inc(gate_done, 1)

            def up(c, j):
                at_least(pe, inter_ready, c * SFF + j - 1)
                for w, b in ((w_g, g_b), (w_u, u_b)):
                    for kh in range(2):
                        mm = pe.matmul(b[j % 2][0:FT, :], w[:, kh, j * FT:(j + 1) * FT], xT[:, kh, :],
                                       start=(kh == 0), stop=(kh == 1))
                mm.then_inc(up_done, 1)

            def prefix(c):
                pe.wait_ge(mask_ready, c + 1)
                for t in range(T):
                    for u in range(t + 1):
                        pe.matmul(t0[:, t * E:(t + 1) * E], before[:] if u == t else ones[:], mask[:, u, :],
                                  start=(u == 0), stop=(u == t))
                for t in range(T):
                    mm = pe.matmul(t1[:, 0:E], ones[:], mask[:, t, :], start=(t == 0), stop=(t == T - 1))
                mm.then_inc(prefix_done, 1)

            def down(c):
                pe.wait_ge(inter_ready, (c + 1) * SFF)
                for q in range(T // 2):
                    if q == 0:
                        at_least(pe, total_ready, 2 * c - 1)
                    else:
                        pe.wait_ge(sig_ready, c + 1)
                    for t in range(2):
                        for j in range(SFF):
                            s = (2 * q + t) * P
                            mm = pe.matmul((down_b, gate_b)[q][:, t * D:(t + 1) * D], inter[:, j, s:s + P], w_d[:, j, :],
                                           start=(j == 0), stop=(j == SFF - 1))
                    mm.then_inc(down_done, 1)

            turn(0, 0, 0)

            def body(c, k, odd, first, last):
                gate(c)
                for j in range(SFF):
                    up(c, j)
                    if j == SFF // 2:
                        prefix(c)
                if not last:
                    turn(c + 1, k + odd, 1 - odd)
                down(c)

            chunks(pe, body)

        @block.scalar
        def _(act):
            def body(c, k, odd, first, last):
                if first:
                    copy_x(act, 0)
                act.wait_ge(gate_done, c + 1)
                at_least(act, weight_ready, c)
                act.activation(sig.rearrange("p t e -> p (t e)"), gate_b[:, 0:T * E], ACT.Sigmoid).then_inc(sig_ready, 1)
                for j in range(SFF):
                    act.wait_ge(up_done, c * SFF + j + 1)
                    at_least(act, inter_ready, c * SFF + j - 1)
                    act.activation(silu_g[j % 2][:], g_b[j % 2][0:FT, :], ACT.Silu).then_inc(silu_ready, 1)
                if not last:
                    copy_x(act, c + 1)

            def copy_x(act, c):
                act.wait_ge(x_turned, c + 1)
                act.activation(xT[:, 0, :], t0[0:HALF, :], ACT.Copy).then_inc(xT0_ready, 1)

            chunks(act, body)

        @block.vector
        def _(dve):
            dve.memset(choice[:, :, E:E + 2], SENTINEL).then_inc(setup, 1)
            dve.wait_ge(consts_in, CONSTS)
            dve.tensor_copy(before[:], before_f[:]).then_inc(wgT_ready, 1)
            dve.wait_ge(wg_turned, 1)
            dve.tensor_copy(wgT[:], gate_b[0:HALF, 0:2 * P].rearrange("p (k e) -> p k e", k=2)[:, :, 0:E])\
               .then_inc(wgT_ready, 1)

            def copy_x(c):
                dve.wait_ge(x_turned, c + 1)
                dve.tensor_copy(xT[:, 1, :], t1[0:HALF, :]).then_inc(xT1_ready, 1)

            def choose(c):
                z = c * STEPS
                dve.wait_ge(sig_ready, c + 1)
                dve.tensor_tensor(choice[:, :, 0:E], sig[:], repeat(bias[:], 1, T), ALU.add).then_inc(route_step, 1)
                hold(dve, dve_passed, route_step, z + 1)
                for t in range(T):
                    dve.max(top[:, t, :], choice[:, t, 0:E]).then_inc(route_step, 1)
                dve.wait_ge(route_step, z + 5)
                dve.memset(top[:, :, TOP_K:8], SENTINEL).then_inc(route_step, 1)
                hold(dve, dve_passed, route_step, z + 6)
                for t in range(T):
                    dve.match_replace(replaced[:, t, :], top[:, t, :], choice[:, t, :], TAKEN).then_inc(route_step, 1)
                dve.wait_ge(route_step, z + 10)
                at_least(dve, prefix_done, c)
                dve.tensor_scalar(mask[:], replaced[:, :, 0:E], TAKEN / 2, None, ALU.is_le).then_inc(mask_ready, 1)

            def queue(c, k, i):
                z = c * STEPS
                dve.wait_ge(prefix_done, c + 1)
                dve.tensor_tensor(place[:], repeat(base[:], 1, T), t0[:, 0:T * E].rearrange("p (t e) -> p t e", t=T),
                                  ALU.subtract).then_inc(route_step, 1)
                dve.wait_ge(route_step, z + 11)
                dve.tensor_tensor(base[:], base[:], t1[:, 0:E], ALU.subtract).then_inc(route_step, 1)
                dve.wait_ge(mask_ready, c + 1)
                dve.tensor_tensor(place_m[:], place[:], mask[:], ALU.mult).then_inc(route_step, 1)
                dve.wait_ge(route_step, z + 13)
                dve.tensor_tensor(in_cap[:], place_m[:], repeat(limit[:], 1, T), ALU.is_gt).then_inc(route_step, 1)
                dve.wait_ge(route_step, z + 14)
                dve.tensor_tensor(place_v[:], place_m[:], in_cap[:], ALU.mult).then_inc(route_step, 1)
                hold(dve, dve_passed, route_step, z + 15)
                for t in range(T):
                    dve.max(slots8[:, t, :], place_v[:, t, :]).then_inc(route_step, 1)
                dve.wait_ge(route_step, z + 19)
                at_least(dve, scattered[i], k * SCATTERS)
                dve.tensor_scalar(slot_i[i][:], slots8[:], -1.0, BIG, ALU.mult, ALU.add).then_inc(slots_ready, 1)

            def weights(c, k, i):
                z = c * STEPS
                for t in range(T):
                    dve.tensor_tensor_reduce(wsel[:, t, :], sig[:, t, :], mask[:, t, :], 1.0, 0.0, ALU.mult, ALU.add,
                                             wsum[:, t:t + 1]).then_inc(route_step, 1)
                dve.wait_ge(route_step, z + 23)
                dve.tensor_scalar(wden[:], wsum[:], 1e-20, None, ALU.add).then_inc(route_step, 1)
                dve.wait_ge(route_step, z + 24)
                dve.reciprocal(winv[:], wden[:]).then_inc(route_step, 1)
                dve.wait_ge(route_step, z + 25)
                at_least(dve, weight_out[i], k * 16)
                for t in range(T):
                    op = dve.tensor_scalar(weight[i][:, t, :], wsel[:, t, :], winv[:, t:t + 1], ROUTE_SCALE,
                                           ALU.mult, ALU.mult)
                    op.then_inc(weight_ready if t == T - 1 else route_step, 1)

            def gated(c, j):
                dve.wait_ge(silu_ready, c * SFF + j + 1)
                dve.tensor_tensor(inter[:, j, :], silu_g[j % 2][:], u_b[j % 2][0:FT, :], ALU.mult).then_inc(inter_ready, 1)

            def add_shared(c, k, i):
                at_least(dve, total_out[i], k * 16)
                for q in range(T // 2):
                    dve.wait_ge(down_done, 2 * c + q + 1)
                    dve.tensor_tensor(total[i][:, 2 * q:2 * q + 2, :],
                                      (down_b, gate_b)[q][:, 0:2 * D].rearrange("p (t d) -> p t d", t=2),
                                      rows[i][:, 2 * q:2 * q + 2, :], ALU.add).then_inc(total_ready, 1)

            copy_x(0)

            def body(c, k, odd, first, last):
                choose(c)
                for j in range(SFF):
                    gated(c, j)
                    if j == SFF // 2:
                        queue(c, k, odd)
                    if j == SFF // 2 + 1:
                        weights(c, k, odd)
                if not last:
                    copy_x(c + 1)
                add_shared(c, k, odd)

            dve.wait_ge(setup, 2)
            chunks(dve, body)


def experts_phase(nc, S, w_gate_up, w_down, t_ident, hx, acc, slot_token):
    from contextlib import ExitStack

    HALF, D, E, FT, FF = S.half, S.dim, S.experts, S.ff_tile, S.ff
    ST = CAP // 2

    with ExitStack() as ctx:
        def sb(name, shape, dt=F32):
            return ctx.enter_context(nc.sbuf_tensor(name, shape, dt))

        def bank(name):
            return ctx.enter_context(nc.psum_tensor(name, [P, 512], F32))

        def sem(name):
            return ctx.enter_context(nc.semaphore(name))

        ident = sb("c_ident", [P, P])
        w_gu = [sb(f"c_w_gu{i}", [HALF, 2, 2 * S.inner]) for i in range(2)]
        w_d = [sb(f"c_w_d{i}", [FT, FF, D]) for i in range(2)]
        token = [sb(f"c_token{i}", [ST, 2], I32) for i in range(4)]
        rows = [sb(f"c_rows{i}", [ST, 2, S.row]) for i in range(2)]
        xT = sb("c_xT", [HALF, 2 * CAP])
        silu_g = [sb(f"c_silu{i}", [FT, CAP]) for i in range(2)]
        inter = sb("c_inter", [FT, FF, CAP])
        y = [sb(f"c_y{i}", [ST, 2, D]) for i in range(2)]

        x_b = bank("c_x")
        gu_b = [bank(f"c_gu{i}") for i in range(4)]
        y_b = [bank("c_down0"), bank("c_down1")]

        ident_in = sem("c_ident_in")
        gu_in = [sem("c_gu_in0"), sem("c_gu_in1")]
        d_in = [sem("c_d_in0"), sem("c_d_in1")]
        token_in = [sem(f"c_token_in{i}") for i in range(4)]
        gathered = [sem("c_gathered0"), sem("c_gathered1")]
        x_turned, xT_ready = sem("c_x_turned"), sem("c_xT_ready")
        up_done, silu_ready, inter_ready = sem("c_up_done"), sem("c_silu_ready"), sem("c_inter_ready")
        down_done, y_ready = sem("c_down_done"), sem("c_y_ready")
        added = [sem(f"c_added{i}") for i in range(4)]

        pool_passed, dve_passed = sem("c_pool_passed"), sem("c_dve_passed")
        block = ctx.enter_context(nc.Block())

        def experts(eng, body):
            for i in range(4):
                body(i, 0, i, i == 0, E == i + 1)
            if E > 8:
                with eng.Fori(1, E // 4 - 1) as k:
                    for i in range(4):
                        body(k * 4 + i, k, i, False, False)
            k = E // 4 - 1
            for i in range(4):
                body(4 * k + i, k, i, False, i == 3)

        def beyond(e, ahead):
            return isinstance(e, int) and e + ahead >= E

        def wait_added(eng, k, i, back, passed=None):
            j = i - back
            if passed is None:
                at_least(eng, added[j % 4], 32 * (k + 1 + j // 4))
            else:
                hold(eng, passed, added[j % 4], 32 * (k + 1 + j // 4))

        @block.sync
        def _(sp):
            sp.dma_start(ident[:], t_ident).then_inc(ident_in, 16)

            def load_token(e, i):
                sp.dma_start(token[i][:], slot_token[bass.ds(e * CAP, CAP), :].rearrange("(p t) a -> p (t a)", t=2))\
                  .then_inc(token_in[i], 16)

            def load_weights(e, i):
                sp.dma_start(w_gu[i][:], w_gate_up[e].rearrange("(k p) n -> p k n", k=2)).then_inc(gu_in[i], 16)
                sp.dma_start(w_d[i][:], w_down[e].rearrange("(j p) n -> p j n", p=FT)).then_inc(d_in[i], 16)

            for e in range(3):
                load_token(e, e)
            load_weights(0, 0)
            load_weights(1, 1)

            def body(e, k, i, first, last):
                if not beyond(e, 3):
                    wait_added(sp, k, i, 1)
                    load_token(e + 3, (i + 3) % 4)
                if not beyond(e, 2):
                    sp.wait_ge(down_done, e + 1)
                    load_weights(e + 2, i % 2)

            experts(sp, body)
            for i in range(4):
                sp.wait_ge(added[i], 32 * (E // 4))

        @block.gpsimd
        def _(pool):
            def gather(e, k, i):
                hold(pool, pool_passed, token_in[i], 16 * (k + 1))
                hold(pool, pool_passed, y_ready, e - 1)
                for t in range(2):
                    pool.indirect_dma_start(rows[i % 2][:, t, :], None, hx,
                                            bass.IndirectOffsetOnAxis(ap=token[i][:, t:t + 1], axis=0))\
                        .then_inc(gathered[i % 2], 16)

            gather(0, 0, 0)

            def body(e, k, i, first, last):
                if not last:
                    gather(e + 1, k + (i + 1) // 4, (i + 1) % 4)
                hold(pool, pool_passed, y_ready, e + 1)
                wait_added(pool, k, i, 1, pool_passed)
                for t in range(2):
                    pool.indirect_dma_start(acc, bass.IndirectOffsetOnAxis(ap=token[i][:, t:t + 1], axis=0),
                                            y[i % 2][:, t, :], None, compute_op=ALU.add).then_inc(added[i], 16)

            experts(pool, body)

        @block.tensor
        def _(pe):
            pe.wait_ge(ident_in, 16)

            def turn(e, k2, i):
                pe.wait_ge(gathered[i % 2], 32 * (k2 + 1))
                for kh in range(2):
                    for t in range(2):
                        mm = pe.transpose(x_b[0:HALF, kh * CAP + t * ST:kh * CAP + (t + 1) * ST],
                                          rows[i % 2][:, t, kh * HALF:(kh + 1) * HALF], ident[0:ST, 0:ST])
                mm.then_inc(x_turned, 1)

            turn(0, 0, 0)

            def body(e, k, i, first, last):
                k2 = k * 2 + i // 2
                pe.wait_ge(xT_ready, e + 1)
                pe.wait_ge(gu_in[i % 2], 16 * (k2 + 1))
                for j in range(FF):
                    at_least(pe, inter_ready, (e - 1) * FF + j + 1)
                    for w in range(2):
                        for kh in range(2):
                            c = w * S.inner + j * FT
                            mm = pe.matmul(gu_b[j][0:FT, w * CAP:(w + 1) * CAP], w_gu[i % 2][:, kh, c:c + FT],
                                           xT[:, kh * CAP:(kh + 1) * CAP], start=(kh == 0), stop=(kh == 1))
                    mm.then_inc(up_done, 1)
                if not last:
                    turn(e + 1, k * 2 + (i + 1) // 2, (i + 1) % 4)
                pe.wait_ge(d_in[i % 2], 16 * (k2 + 1))
                pe.wait_ge(inter_ready, (e + 1) * FF)
                at_least(pe, y_ready, e - 1)
                for t in range(2):
                    for j in range(FF):
                        mm = pe.matmul(y_b[i % 2][0:ST, t * D:(t + 1) * D], inter[:, j, t * ST:(t + 1) * ST],
                                       w_d[i % 2][:, j, :], start=(j == 0), stop=(j == FF - 1))
                mm.then_inc(down_done, 1)

            experts(pe, body)

        @block.scalar
        def _(act):
            def copy_x(e):
                act.wait_ge(x_turned, e + 1)
                act.activation(xT[:], x_b[0:HALF, 0:2 * CAP], ACT.Copy).then_inc(xT_ready, 1)

            copy_x(0)

            def body(e, k, i, first, last):
                for j in range(FF):
                    act.wait_ge(up_done, e * FF + j + 1)
                    at_least(act, inter_ready, e * FF + j - 1)
                    act.activation(silu_g[j % 2][:], gu_b[j][0:FT, 0:CAP], ACT.Silu).then_inc(silu_ready, 1)
                if not last:
                    copy_x(e + 1)

            experts(act, body)

        @block.vector
        def _(dve):
            def body(e, k, i, first, last):
                for j in range(FF):
                    dve.wait_ge(silu_ready, e * FF + j + 1)
                    at_least(dve, down_done, e)
                    dve.tensor_tensor(inter[:, j, :], silu_g[j % 2][:], gu_b[j][0:FT, CAP:2 * CAP], ALU.mult)\
                       .then_inc(inter_ready, 1)
                dve.wait_ge(down_done, e + 1)
                wait_added(dve, k, i, 2)
                for t in range(2):
                    op = dve.tensor_scalar(y[i % 2][:, t, :], y_b[i % 2][0:ST, t * D:(t + 1) * D],
                                           rows[i % 2][:, t, bass.ds(e + D, 1)], None, ALU.mult)
                op.then_inc(y_ready, 1)

            experts(dve, body)


def final_phase(nc, S, acc, out):
    from contextlib import ExitStack

    D, B, J = S.dim, S.images, 14
    STEPS = S.seq // J
    REST = S.seq - STEPS * J

    with ExitStack() as ctx:
        def sb(name, shape, dt=F32):
            return ctx.enter_context(nc.sbuf_tensor(name, shape, dt))

        def sem(name):
            return ctx.enter_context(nc.semaphore(name))

        rows = [sb(f"d_rows{i}", [B, J, D]) for i in range(2)]
        norm = [sb(f"d_norm{i}", [B, J, D]) for i in range(2)]
        stats = sb("d_stats", [B, J, 6])
        moments = [sb(f"d_moments{i}", [B, J, 2]) for i in range(2)]
        rstd = [sb(f"d_rstd{i}", [B, J]) for i in range(2)]
        minus_half = sb("d_minus_half", [B, J])

        half_set = sem("d_half_set")
        rows_in = [sem("d_rows_in0"), sem("d_rows_in1")]
        out_done = [sem("d_out0"), sem("d_out1")]
        stats_ready, moments_ready, rstd_step = sem("d_stats_ready"), sem("d_moments_ready"), sem("d_rstd_step")
        norm_ready = sem("d_norm_ready")

        pool_passed, dve_passed = sem("d_pool_passed"), sem("d_dve_passed")
        block = ctx.enter_context(nc.Block())
        acc_v = acc[0:S.tokens, :].rearrange("(b s) d -> b s d", s=S.seq)

        def groups(eng, body):
            body(0, 0, 0, J)
            body(1, 0, 1, J)
            with eng.Fori(1, STEPS // 2 - 1) as k:
                body(k * 2, k, 0, J)
                body(k * 2 + 1, k, 1, J)
            k = STEPS // 2 - 1
            body(2 * k, k, 0, J)
            body(2 * k + 1, k, 1, J)
            body(STEPS, STEPS // 2, 0, REST)

        @block.sync
        def _(sp):
            def load(s, i, count):
                sp.dma_start(rows[i][:, 0:count, :], acc_v[:, bass.ds(s * J, count), :]).then_inc(rows_in[i], 16)

            load(0, 0, J)
            load(1, 1, J)

            def body(s, k, odd, count):
                sp.wait_ge(norm_ready, s + 1)
                sp.dma_start(out[:, bass.ds(s * J, count), :], norm[odd][:, 0:count, :]).then_inc(out_done[odd], 16)
                if not (isinstance(s, int) and s + 2 > STEPS):
                    load(s + 2, odd, REST if isinstance(s, int) and s + 2 == STEPS else J)

            groups(sp, body)
            sp.wait_ge(out_done[0], 16 * (STEPS // 2 + 1))
            sp.wait_ge(out_done[1], 16 * (STEPS // 2))

        @block.gpsimd
        def _(pool):
            pool.memset(minus_half[:], -0.5).then_inc(half_set, 1)
            hold(pool, pool_passed, half_set, 1)

            def body(s, k, odd, count):
                hold(pool, pool_passed, moments_ready, s + 1)
                hold(pool, pool_passed, norm_ready, s - 1)
                pool.tensor_scalar(rstd[odd][:, 0:count], moments[odd][:, 0:count, 1], LN_EPS, None, ALU.add)\
                    .then_inc(rstd_step, 1)
                hold(pool, pool_passed, rstd_step, 2 * s + 1)
                pool.tensor_tensor(rstd[odd][:, 0:count], rstd[odd][:, 0:count], minus_half[:, 0:count], ALU.pow)\
                    .then_inc(rstd_step, 1)

            groups(pool, body)

        @block.vector
        def _(dve):
            def measure(s, k, odd, count):
                dve.wait_ge(rows_in[odd], 16 * (k + 1))
                at_least(dve, moments_ready, s)
                for j in range(count):
                    op = dve.bn_stats(stats[:, j, :], rows[odd][:, j, :])
                op.then_inc(stats_ready, 1)
                hold(dve, dve_passed, stats_ready, s + 1)
                for j in range(count):
                    op = dve.bn_aggr(moments[odd][:, j, :], stats[:, j, :])
                op.then_inc(moments_ready, 1)

            def apply(s, k, odd, count):
                dve.wait_ge(rstd_step, 2 * s + 2)
                at_least(dve, out_done[odd], 16 * k)
                for j in range(count):
                    op = dve.tensor_scalar(norm[odd][:, j, :], rows[odd][:, j, :], moments[odd][:, j, 0:1],
                                           rstd[odd][:, j:j + 1], ALU.subtract, ALU.mult)
                op.then_inc(norm_ready, 1)

            def body(s, k, odd, count):
                measure(s, k, odd, count)
                apply(s, k, odd, count)

            groups(dve, body)


def vit_tower_moe_kernel(nc, S, x, tok_w, tok_b, pos, cls, w_qkv, w_proj, b_proj, wg, e_bias, w_gate_up, w_down,
                         wsg, wsu, wsd, t, out):
    hx = nc.dram_tensor("hx_scratch", [S.all_rows, S.row], F32, kind="Internal").ap()
    acc = nc.dram_tensor("acc_scratch", [S.all_rows, S.dim], F32, kind="Internal").ap()
    slot_token = nc.dram_tensor("slot_token_scratch", [S.slots, 1], I32, kind="Internal").ap()
    attention_phase(nc, S, x, tok_w, tok_b, pos, cls, w_qkv, w_proj, b_proj, t["ident"], t["cos"], t["sin"],
                    t["hmask"], t["vmask"], hx, acc, slot_token, t["empty"])
    routing_phase(nc, S, wg, e_bias, wsg, wsu, wsd, t["ident"], t["before"], t["slot_base"], t["slot_limit"],
                  t["token_id"], hx, acc, slot_token)
    experts_phase(nc, S, w_gate_up, w_down, t["ident"], hx, acc, slot_token)
    final_phase(nc, S, acc, out)


_INS = ['x', 'L0_tok_W', 'L0_tok_b', 'L0_tok_pos_table', 'L0_tok_class_token', 'L0_attn_w_qkv', 'L0_attn_w_proj',
        'L0_attn_b_proj', 'L0_ffn_Wg', 'L0_ffn_e_bias', 'L0_ffn_W_gate_up', 'L0_ffn_W_down', 'L0_ffn_Wsg',
        'L0_ffn_Wsu', 'L0_ffn_Wsd']


def kernel(**inputs):
    import numpy as _np
    import concourse.bacc as _bacc
    from concourse import mybir as _mybir
    from concourse.bass_utils import run_bass_kernel_spmd as _run

    nc = _bacc.Bacc("TRN2", target_bir_lowering=False, num_devices=1)
    arrays, args = {}, []
    for name in _INS:
        a = _np.ascontiguousarray(inputs[name])
        arrays[f"in_{name}_dram"] = a
        args.append(nc.dram_tensor(f"in_{name}_dram", a.shape, _mybir.dt.from_np(a.dtype), kind="ExternalInput").ap())
    S = Shapes(inputs["x"], inputs["L0_tok_W"], inputs["L0_tok_pos_table"], inputs["L0_ffn_Wg"],
               inputs["L0_ffn_W_gate_up"], inputs["L0_ffn_Wsg"])
    consts = {}
    for name, a in tables(S).items():
        arrays[f"const_{name}_dram"] = a
        consts[name] = nc.dram_tensor(f"const_{name}_dram", a.shape, _mybir.dt.from_np(a.dtype),
                                      kind="ExternalInput").ap()
    out = nc.dram_tensor("out_0_dram", (S.images, S.seq, S.dim), F32, kind="ExternalOutput").ap()
    vit_tower_moe_kernel(nc, S, *args, consts, out)
    r = _run(nc, [arrays], core_ids=[0])
    return r.results[0]["out_0_dram"]
```

```python
import numpy as np

import concourse.bass as bass
from concourse import mybir

F32 = mybir.dt.float32
F32R = mybir.dt.float32r
BF16 = mybir.dt.bfloat16
I32 = mybir.dt.int32
ALU = mybir.AluOpType
ACT = mybir.ActivationFunctionType
AX_X = mybir.AxisListType.X

P = 128
PATCH = 16
HEADS = 12
HD = 16
TOP_K = 6
CAP = 192
ROUTE_SCALE = 2.5
LN_EPS = 1e-5
ROPE_THETA = 10000.0
BIG = 65536.0
SENTINEL = 3.0e38
TAKEN = -3.0e38
CHUNK = 512


PRODUCTS = [(0, 0, 0), (0, 0, 1), (2, 0, 0), (1, 1, 0), (1, 1, 1)]


class Shapes:

    def __init__(self, x, tok_w, pos, wg, w_gate_up, wsg):
        self.images, self.chans, self.height, self.width = x.shape
        self.gh, self.gw = self.height // PATCH, self.width // PATCH
        self.patches = self.gh * self.gw
        self.seq = pos.shape[0]
        self.dim = tok_w.shape[1]
        self.half = self.dim // 2
        self.half_heads = HEADS // 2
        self.rows = (self.seq + 1) // 2
        self.second = self.seq - self.rows
        self.tokens = self.images * self.seq
        self.chunks = -(-self.tokens // CHUNK)
        self.padded = self.chunks * CHUNK
        self.experts = wg.shape[0]
        self.slots = self.experts * CAP
        self.all_rows = self.padded + CAP
        self.inner = w_gate_up.shape[2] // 2
        self.shared = wsg.shape[1]
        self.ff_tile = 116
        self.ff = self.inner // self.ff_tile
        self.sff = self.shared // self.ff_tile
        self.third = self.dim - P
        self.wide = self.dim + self.third
        self.row = self.dim + self.experts
        self.even = self.seq + 1
        self.group = 4
        self.groups = HEADS // self.group


def repeat(ap, axis, count):
    dims = [list(d) for d in ap.ap]
    dims.insert(axis, [0, count])
    return bass.AP(ap.tensor, ap.offset, dims)


def at_least(eng, sem, value):
    if isinstance(value, int) and value <= 0:
        return
    eng.wait_ge(sem, value)


def hold(eng, passed, sem, value):
    if isinstance(value, int) and value <= 0:
        return
    eng.wait_ge(sem, value)
    eng.sem_inc(passed, 1)


def attention_phase(nc, S, x, tok_w, tok_b, pos, cls, w_qkv, w_proj, b_proj,
                    t_ident, t_cos, t_sin, t_split, t_vmask, hx, acc, slot_token, t_empty):
    from contextlib import ExitStack

    R, SEQ, SEC, NP = S.rows, S.seq, S.second, S.patches
    D, B, W2 = S.dim, S.images, S.wide
    KR = S.chans * PATCH
    PJ = PATCH // 2
    GW, GH = S.gw, S.gh
    EV, G4, NG = S.even, S.group, S.groups
    SUB = 2 * HD
    DIAG = P + SUB
    COPIES = 4
    PAIRS = HEADS // 2
    ROUNDS = 2 * NG
    DEN = P * 2
    LN = 6

    with ExitStack() as ctx:
        def sb(name, shape, dt=F32):
            return ctx.enter_context(nc.sbuf_tensor(name, shape, dt))

        def bank(name):
            return ctx.enter_context(nc.psum_tensor(name, [P, 512], F32))

        def sem(name):
            return ctx.enter_context(nc.semaphore(name))

        ident = sb("a_ident", [P, P])
        cos = sb("a_cos", [R, 2, HD])
        sin = sb("a_sin", [R, 2, HD])
        split = sb("a_split", [P, 6])
        vmask = sb("a_vmask", [R, 2])
        wt = sb("a_wt", [2 * KR, PJ, W2])
        raw_qkv = sb("a_raw_qkv", [P, 2, 3 * D])
        wqkv = sb("a_wqkv", [P, 2, 2, 3 * D], F32R)
        wp = sb("a_wp", [P, NG, D])
        bproj = sb("a_bproj", [R, D])
        pos_rows = sb("a_pos_rows", [R, 2, D])
        add_rows = sb("a_add_rows", [R, 2, W2])
        addT = sb("a_addT", [P, 2, SEQ])
        zeros = sb("a_zeros", [P, S.row])
        empty = sb("a_empty", [P, S.slots // P], I32)
        img = [sb(f"a_img{i}", [2 * KR, GH, S.width]) for i in range(2)]
        hT = sb("a_hT", [P, 2, SEQ])
        hT_high = sb("a_hT_high", [P, SEQ])
        hT_parts = sb("a_hT_parts", [P, 3, SEQ], F32R)
        rope_a = [sb(f"a_rope_a{i}", [R, 2 * D]) for i in range(2)]
        rope_b = [sb(f"a_rope_b{i}", [R, 2 * D]) for i in range(2)]
        qk = sb("a_qk", [R, 2, 2 * HEADS, COPIES * HD])
        high = [sb(f"a_high{i}", [P, 2, SEQ]) for i in range(2)]
        raw = sb("a_raw", [P, 2, SEQ])
        qT = sb("a_qT", [P, PAIRS, SEQ], F32R)
        k_own = sb("a_k_own", [P, HEADS, EV], F32R)
        v_own = [sb(f"a_v_own{i}", [R, 2, HEADS * DIAG], F32R) for i in range(2)]
        neg_max = [sb(f"a_neg_max{i}", [R, HEADS, 2]) for i in range(2)]
        denom = [sb(f"a_denom{i}", [R, HEADS, 2]) for i in range(2)]
        prob = [sb(f"a_prob{i}", [R, 2, SEQ]) for i in range(2)]
        probT_hi = [sb(f"a_probT_hi{i}", [R, 2, EV], F32R) for i in range(3)]
        probT_lo = [sb(f"a_probT_lo{i}", [R, 2, EV], F32R) for i in range(3)]
        rden = sb("a_rden", [R, G4, 2])
        rden_wide = sb("a_rden_wide", [R, 2, G4, SUB])
        rdenT = [sb(f"a_rdenT{i}", [P, SEQ]) for i in range(2)]
        oT = sb("a_oT", [P, NG, SEQ])
        h_rows = sb("a_h_rows", [R, 2, D])
        res = [sb(f"a_res{i}", [R, 2, D]) for i in range(2)]
        res2 = sb("a_res2", [R, 2, D])
        stats = sb("a_stats", [R, 2, 6])
        moments = sb("a_moments", [R, 2, 2])
        rstd = sb("a_rstd", [R, 2])
        minus_half = sb("a_minus_half", [R, 2])
        h1 = [sb(f"a_h1{i}", [R, 2, D]) for i in range(2)]

        score = [bank("a_score0"), bank("a_score1")]
        turned = [bank("a_turned0"), bank("a_turned1")]
        out_b = [bank("a_out0"), bank("a_out1")]
        fa, fb = bank("a_fa"), bank("a_fb")

        half_set = sem("a_half_set")
        consts_in, wp_in = sem("a_consts_in"), sem("a_wp_in")
        zero_set = sem("a_zero_set")
        scratch_set = sem("a_scratch_set")
        add_step = sem("a_add_step")
        add_ready, add_turned, cls_col = sem("a_add_ready"), sem("a_add_turned"), sem("a_cls_col")
        img_in = [sem("a_img_in0"), sem("a_img_in1")]
        tok_done = sem("a_tok_done")
        hT_ready, hT_high_ready, hT_split = sem("a_hT_ready"), sem("a_hT_high_ready"), sem("a_hT_split")
        qkv_split = sem("a_qkv_split")
        qk_done, rope_step, qk_ready = sem("a_qk_done"), sem("a_rope_step"), sem("a_qk_ready")
        v_done, v_high, v_ready = sem("a_v_done"), sem("a_v_high"), sem("a_v_ready")
        turn_qk, high_ready, raw_ready = sem("a_turn_qk"), sem("a_high_ready"), sem("a_raw_ready")
        q_ready, k_ready = sem("a_q_ready"), sem("a_k_ready")
        score_done, max_ready, prob_ready = sem("a_score_done"), sem("a_max_ready"), sem("a_prob_ready")
        turned_done, hi_ready, probT_ready, pv_done = (sem("a_turned_done"), sem("a_hi_ready"),
                                                       sem("a_probT_ready"), sem("a_pv_done"))
        rden_ready, wide_ready, rdenT_done, rdenT_ready = (sem("a_rden_ready"), sem("a_wide_ready"),
                                                           sem("a_rdenT_done"), sem("a_rdenT_ready"))
        oT_ready, proj_done = sem("a_oT_ready"), sem("a_proj_done")
        h_turned, h_rows_ready, res_ready = sem("a_h_turned"), sem("a_h_rows_ready"), sem("a_res_ready")
        ln_step, h1_ready = sem("a_ln_step"), sem("a_h1_ready")
        h1_out = [sem("a_h1_out0"), sem("a_h1_out1")]

        CONSTS = 18 * 16
        WP_DMAS = 2 * HEADS * 16
        IMG_DMAS = 2 * S.chans * 16

        x_rows = x.rearrange("b c (hp ph) w -> b c ph hp w", ph=PATCH)
        w_rows = tok_w.rearrange("(r g j) d -> g r j d", g=2, j=PJ)

        pool_passed, dve_passed = sem("a_pool_passed"), sem("a_dve_passed")
        block = ctx.enter_context(nc.Block())

        def images(eng, body):
            body(0, 0, 0, True, False)
            body(1, 0, 1, False, B == 2)
            if B > 4:
                with eng.Fori(1, B // 2 - 1) as k:
                    body(k * 2, k, 0, False, False)
                    body(k * 2 + 1, k, 1, False, False)
            if B > 2:
                k = B // 2 - 1
                body(2 * k, k, 0, False, False)
                body(2 * k + 1, k, 1, False, True)

        def beyond(n, ahead):
            return isinstance(n, int) and n + ahead >= B

        @block.sync
        def _(sp):
            for dst, src in ((ident[:], t_ident), (split[:], t_split),
                             (pos_rows[:, 0, :], pos[0:R, :]), (pos_rows[:, 1, :], pos[SEC:SEQ, :]),
                             (add_rows[:, 1, 0:D], tok_b.partition_broadcast(R)),
                             (add_rows[1:R, 0, 0:D], tok_b.partition_broadcast(R - 1)),
                             (add_rows[0:1, 0, 0:D], cls[0]),
                             (wt[0:KR, :, 0:D], w_rows[0]), (wt[KR:2 * KR, :, 0:D], w_rows[1]),
                             (wt[0:KR, :, D:W2], w_rows[0][:, :, P:D]), (wt[KR:2 * KR, :, D:W2], w_rows[1][:, :, P:D])):
                sp.dma_start(dst, src).then_inc(consts_in, 16)

            def load(n, i):
                for g in range(2):
                    for c in range(S.chans):
                        r = g * KR + c * PATCH
                        sp.dma_start(img[i][r:r + PATCH, :, 0:S.width - PJ * g],
                                     x_rows[n, c][:, :, PJ * g:S.width]).then_inc(img_in[i], 16)

            def store(n, i):
                sp.wait_ge(h1_ready, n + 1)
                sp.dma_start(hx[bass.ds(n * SEQ, R), 0:D], h1[i][:, 0, :]).then_inc(h1_out[i], 16)
                sp.dma_start(hx[bass.ds(n * SEQ + R, R - 1), 0:D], h1[i][1:R, 1, :]).then_inc(h1_out[i], 16)

            load(0, 0)
            load(1, 1)
            for h in range(HEADS):
                for part in range(2):
                    r = h % G4 * SUB + part * HD
                    sp.dma_start(wp[r:r + HD, h // G4, :], w_proj[h * HD:(h + 1) * HD, :]).then_inc(wp_in, 16)
            sp.wait_ge(wp_in, WP_DMAS)
            sp.dma_start(empty[:], t_empty).then_inc(scratch_set, 16)
            sp.wait_ge(scratch_set, 16)
            sp.dma_start(slot_token.rearrange("(p n) a -> p (n a)", p=P), empty[:]).then_inc(scratch_set, 16)
            sp.wait_ge(zero_set, 1)
            r, k = S.tokens, 2
            while r < S.all_rows:
                m = min(P, S.all_rows - r)
                sp.dma_start(hx[r:r + m, :], zeros[0:m, :]).then_inc(scratch_set, 16)
                r, k = r + m, k + 1
            sp.dma_start(acc[S.padded:S.padded + P, :], zeros[:, 0:D]).then_inc(scratch_set, 16)
            sp.dma_start(acc[S.padded + P:S.all_rows, :], zeros[0:CAP - P, 0:D]).then_inc(scratch_set, 16)
            sp.wait_ge(scratch_set, 16 * (k + 2))

            def body(n, k, odd, first, last):
                if not beyond(n, 2):
                    sp.wait_ge(tok_done, n + 1)
                    load(n + 2, odd)
                if not first:
                    store(n - 1, 1 - odd)

            images(sp, body)
            store(B - 1, (B - 1) % 2)
            for i in range(2):
                sp.wait_ge(h1_out[i], 32 * (B // 2))

        @block.gpsimd
        def _(pool):
            pool.memset(minus_half[:], -0.5).then_inc(half_set, 1)
            hold(pool, pool_passed, half_set, 1)
            hold(pool, pool_passed, consts_in, CONSTS)

            def rope_sum(m, group, t):
                hold(pool, pool_passed, rope_step, m * 4 + 4 - 2 * t)
                hold(pool, pool_passed, turn_qk, ROUNDS * m - ROUNDS + 2 * (group + 1))
                lo = group * G4
                a, b = (repeat(x.rearrange("p (s h d) -> p s h d", s=2, d=HD)[:, :, lo:lo + G4, :], 3, COPIES)
                        for x in (rope_a[t], rope_b[t]))
                out = qk[:, t, :, :].rearrange("p (s h) (c d) -> p s h c d", s=2, d=HD)[:, :, lo:lo + G4]
                for s in range(2):
                    pool.tensor_tensor(out[:, s], a[:, s], b[:, s], ALU.add).then_inc(qk_ready, 1)

            def rope_sums(m):
                for group in range(NG):
                    for t in (1, 0):
                        rope_sum(m, group, t)

            def add_bias(m, i):
                hold(pool, pool_passed, h_rows_ready, m + 1)
                hold(pool, pool_passed, ln_step, (m - 2) * LN + 1)
                pool.tensor_tensor(res[i][:], h_rows[:], repeat(bproj[:], 1, 2), ALU.add).then_inc(res_ready, 1)

            def normalise(n, k_out, i):
                hold(pool, pool_passed, ln_step, n * LN + 4)
                pool.tensor_scalar(rstd[:], moments[:, :, 1], LN_EPS, None, ALU.add).then_inc(ln_step, 1)
                hold(pool, pool_passed, ln_step, n * LN + 5)
                pool.tensor_tensor(rstd[:], rstd[:], minus_half[:], ALU.pow).then_inc(ln_step, 1)
                hold(pool, pool_passed, ln_step, n * LN + 6)
                hold(pool, pool_passed, h1_out[i], k_out * 32)
                for t in range(2):
                    op = pool.tensor_scalar(h1[i][:, t, :], res2[:, t, :], moments[:, t, 0:1], rstd[:, t:t + 1],
                                            ALU.subtract, ALU.mult)
                op.then_inc(h1_ready, 1)

            def body(n, k, odd, first, last):
                if not last:
                    rope_sums(n + 1)
                if not first:
                    normalise(n - 1, k - 1 + odd, 1 - odd)
                if not last:
                    add_bias(n + 1, 1 - odd)

            rope_sums(0)
            add_bias(0, 0)
            images(pool, body)
            normalise(B - 1, (B - 1) // 2, (B - 1) % 2)

        @block.tensor
        def _(pe):
            pe.wait_ge(consts_in, CONSTS)
            pe.wait_ge(add_ready, 1)
            for kh in range(2):
                for t in range(2):
                    mm = pe.transpose(fb[:, kh * SEQ + t * SEC:kh * SEQ + t * SEC + R],
                                      add_rows[:, t, kh * P:(kh + 1) * P], ident[0:R, 0:R])
            mm.then_inc(add_turned, 1)

            EMBED = [(f, j) for f in range(2) for j in range(PJ)]
            EMBED_CUTS = [0, 4, 7, 10, 13, 16]

            def embed(m, mk, i, lo, hi):
                if lo == 0:
                    pe.wait_ge(img_in[i], (mk + 1) * IMG_DMAS)
                    at_least(pe, h_rows_ready, m)
                for f, j in EMBED[lo:hi]:
                    mm = pe.matmul(fb[:, f * NP:(f + 1) * NP], wt[:, j, f * P:(f + 1) * P],
                                   img[i][:, :, j:j + PATCH * (GW - 1) + 1:PATCH], start=(j == 0), stop=(j == PJ - 1))
                if hi == len(EMBED):
                    mm.then_inc(tok_done, 1)

            def project_qk(m, t):
                pe.wait_ge(hT_split, 2 * (m + 1))
                if t == 0:
                    at_least(pe, raw_ready, NG * m)
                for n, (x, kt, part) in enumerate(PRODUCTS):
                    mm = pe.matmul((fa, fb)[t][0:R, 0:2 * D], hT_parts[:, x, t * SEC:t * SEC + R],
                                   wqkv[:, kt, part, 0:2 * D], start=(n == 0), stop=(n == len(PRODUCTS) - 1))
                mm.then_inc(qk_done, 1)

            def project_v(m):
                pe.wait_ge(rope_step, m * 4 + 2)
                for t in range(2):
                    for n, (x, kt, part) in enumerate(PRODUCTS):
                        mm = pe.matmul(fb[0:R, t * D:(t + 1) * D], hT_parts[:, x, t * SEC:t * SEC + R],
                                       wqkv[:, kt, part, 2 * D:3 * D], start=(n == 0), stop=(n == len(PRODUCTS) - 1))
                mm.then_inc(v_done, 1)

            def turn_h(m):
                pe.wait_ge(v_ready, m + 1)
                for t in range(2):
                    for kt, w in ((0, P), (1, D - P)):
                        mm = pe.transpose(fb[0:R, t * D + kt * P:t * D + kt * P + w],
                                          hT[0:w, kt, t * SEC:t * SEC + R], ident[0:w, 0:w])
                mm.then_inc(h_turned, 1)

            def turn(m, r):
                if r % 2 == 0:
                    pe.wait_ge(qk_ready, 4 * NG * m + 4 * (r // 2 + 1))
                if r == 0:
                    at_least(pe, ln_step, (m - 2) * LN + 1)
                elif r % 2 == 1:
                    pe.wait_ge(q_ready, NG * m + r // 2 + 1)
                else:
                    pe.wait_ge(raw_ready, NG * m + r // 2)
                for c in range(2):
                    h = r % 2 * HEADS + r // 2 * G4 + 2 * c
                    for t in range(2):
                        mm = pe.transpose(fa[:, c * SEQ + t * SEC:c * SEQ + t * SEC + R],
                                          qk[:, t, h:h + 2, :].rearrange("p h d -> p (h d)"), ident[0:R, 0:R])
                mm.then_inc(turn_qk, 1)

            def scores(n, h, g):
                if h % G4 == 0:
                    pe.wait_ge(q_ready, NG * n + h // G4 + 1)
                    pe.wait_ge(k_ready, NG * n + h // G4 + 1)
                at_least(pe, prob_ready, g - 1)
                for t in range(2):
                    mm = pe.matmul(score[h % 2][0:R, t * EV:(t + 1) * EV], qT[:, h // 2, t * SEC:t * SEC + R],
                                   k_own[:, h, :], start=True, stop=True)
                mm.then_inc(score_done, 1)

            def turn_probs(h, g):
                pe.wait_ge(prob_ready, g + 1)
                at_least(pe, probT_ready, g - 1)
                for kt in range(2):
                    for t in range(2):
                        mm = pe.transpose(turned[h % 2][0:R, kt * SEQ + t * SEC:kt * SEQ + t * SEC + R],
                                          prob[h % 2][:, t, kt * SEC:kt * SEC + R], ident[0:R, 0:R])
                mm.then_inc(turned_done, 1)

            def attend(n, i, h, g):
                pe.wait_ge(probT_ready, g + 1)
                group, j = h // G4, h % G4
                out = out_b[(i + group) % 2]
                if h == 0:
                    pe.wait_ge(v_ready, n + 1)
                if j == 0:
                    at_least(pe, oT_ready, NG * n + group - 1)
                last = 0
                for kt in range(2):
                    for part in (probT_hi, probT_lo):
                        last += 1
                        mm = pe.matmul(out[:, 0:EV], v_own[i][:, kt, h * DIAG - j * SUB:h * DIAG - j * SUB + P],
                                       part[h % 3][:, kt, :], start=(j == 0 and last == 1), stop=(j == G4 - 1 and last == 4))
                mm.then_inc(pv_done, 1)
                if j == G4 - 1:
                    pe.wait_ge(wide_ready, NG * n + group + 1)
                    for t in range(2):
                        mm = pe.transpose(out[:, DEN + t * SEC:DEN + t * SEC + R],
                                          rden_wide[:, t, :, :].rearrange("p h d -> p (h d)"), ident[0:R, 0:R])
                    mm.then_inc(rdenT_done, 1)

            def project_out(n, t):
                if t == 0:
                    if isinstance(n, int) and n == 0:
                        pe.wait_ge(wp_in, WP_DMAS)
                    pe.wait_ge(oT_ready, NG * (n + 1))
                    if not beyond(n, 2):
                        pe.wait_ge(rope_step, (n + 2) * 4 + 4)
                    elif n == B - 2:
                        pe.wait_ge(raw_ready, NG * B)
                    else:
                        pe.wait_ge(ln_step, (n - 1) * LN + 1)
                for group in range(NG):
                    mm = pe.matmul(fa[0:R, t * D:(t + 1) * D], oT[:, group, t * SEC:t * SEC + R], wp[:, group, :],
                                   start=(group == 0), stop=(group == NG - 1))
                if t == 1:
                    mm.then_inc(proj_done, 1)

            pe.wait_ge(cls_col, 1)
            pe.wait_ge(qkv_split, 2)
            embed(0, 0, 0, 0, len(EMBED))
            project_qk(0, 1)
            project_qk(0, 0)
            project_v(0)
            turn_h(0)
            embed(1, 0, 1, 0, len(EMBED))
            for r in range(ROUNDS):
                turn(0, r)
            scores(0, 0, 0)
            scores(0, 1, 1)

            def body(n, k, odd, first, last):
                for h in range(HEADS):
                    g = n * HEADS + h
                    turn_probs(h, g)
                    if h + 2 < HEADS:
                        scores(n, h + 2, g + 2)
                    elif not last:
                        scores(n + 1, h + 2 - HEADS, g + 2)
                    if h >= 2:
                        attend(n, odd, h - 2, g - 2)
                    elif not first:
                        attend(n - 1, 1 - odd, h + HEADS - 2, g - 2)
                    if h in (1, 2) and not last:
                        project_qk(n + 1, 2 - h)
                    if h == 3 and not last:
                        project_v(n + 1)
                    if h in (4, 5) and not first:
                        project_out(n - 1, h - 4)
                    if h == 5 and not last:
                        turn_h(n + 1)
                    if 6 <= h < 11 and not beyond(n, 2):
                        embed(n + 2, k + 1, odd, EMBED_CUTS[h - 6], EMBED_CUTS[h - 5])
                    if h >= 6 and not last:
                        turn(n + 1, h - 6)

            images(pe, body)
            for h in (HEADS - 2, HEADS - 1):
                attend(B - 1, (B - 1) % 2, h, (B - 1) * HEADS + h)
            project_out(B - 1, 0)
            project_out(B - 1, 1)

        @block.scalar
        def _(act):
            for dst, src in ((raw_qkv[:, 0, :], w_qkv[0:P, :]), (raw_qkv[0:P // 2, 1, :], w_qkv[P:D, :]),
                             (raw_qkv[P // 2:P, 1, :], w_qkv[P:D, :]), (cos[:], t_cos), (sin[:], t_sin),
                             (vmask[:], t_vmask), (bproj[:], b_proj.partition_broadcast(R))):
                act.dma_start(dst, src).then_inc(consts_in, 16)
            act.wait_ge(consts_in, CONSTS)

            def high_parts(m, r):
                act.wait_ge(turn_qk, ROUNDS * m + r + 1)
                at_least(act, (q_ready, k_ready)[r % 2], NG * m + r // 2)
                act.activation(high[r % 2].bitcast(F32R).rearrange("p c s -> p (c s)"), fa[:, 0:2 * SEQ], ACT.Copy,
                               scale=split[:, 2 * (r % 2):2 * (r % 2) + 1]).then_inc(high_ready, 1)
                if r % 2 == 1:
                    act.activation(raw.rearrange("p c s -> p (c s)"), fa[:, 0:2 * SEQ], ACT.Copy).then_inc(raw_ready, 1)

            def h_high(m):
                act.wait_ge(hT_ready, m + 1)
                at_least(act, v_done, m)
                act.activation(hT_parts[:, 0, :], hT[:, 0, :], ACT.Copy).then_inc(hT_high_ready, 1)
                act.activation(hT_high.bitcast(F32R)[:], hT[:, 1, :], ACT.Copy, scale=split[:, 4:5])\
                   .then_inc(hT_high_ready, 1)

            def values_high(m, i):
                act.wait_ge(v_done, m + 1)
                at_least(act, pv_done, (m - 1) * HEADS)
                if isinstance(m, int) and m < 2:
                    act.wait_ge(zero_set, 3)
                for t in range(2):
                    own = v_own[i][:, t, :].rearrange("p (h w) -> p h w", w=DIAG)
                    act.activation(own[:, :, 0:HD], fb[0:R, t * D:(t + 1) * D].rearrange("p (h d) -> p h d", d=HD),
                                   ACT.Copy, scale=vmask[:, t:t + 1]).then_inc(v_high, 1)

            def copy_h(m):
                act.wait_ge(h_turned, m + 1)
                at_least(act, res_ready, m)
                act.activation(h_rows.rearrange("p t d -> p (t d)"), fb[0:R, 0:2 * D], ACT.Copy)\
                   .then_inc(h_rows_ready, 1)

            def softmax(i, h, g):
                act.wait_ge(max_ready, g + 1)
                at_least(act, turned_done, g - 1)
                for t in range(2):
                    op = act.activation(prob[h % 2][:, t, :], score[h % 2][0:R, t * EV:t * EV + SEQ], ACT.Exp,
                                        bias=neg_max[i][:, h, t:t + 1], accum_out=denom[i][:, h, t:t + 1])
                op.then_inc(prob_ready, 1)

            def probs_high(h, g):
                act.wait_ge(turned_done, g + 1)
                at_least(act, pv_done, g - 2)
                act.activation(probT_hi[h % 3][:, :, 0:SEQ], turned[h % 2][0:R, 0:2 * SEQ].rearrange("p (k s) -> p k s", k=2),
                               ACT.Copy).then_inc(hi_ready, 1)

            def denom_copy(n, i, group):
                act.wait_ge(rdenT_done, NG * n + group + 1)
                at_least(act, oT_ready, NG * n + group - 1)
                act.activation(rdenT[group % 2][:], out_b[(i + group) % 2][:, DEN:DEN + SEQ], ACT.Copy)\
                   .then_inc(rdenT_ready, 1)

            h_high(0)
            values_high(0, 0)
            copy_h(0)
            for r in range(ROUNDS - 1):
                high_parts(0, r)
            softmax(0, 0, 0)
            softmax(0, 1, 1)
            h_high(1)

            def body(n, k, odd, first, last):
                for h in range(HEADS):
                    g = n * HEADS + h
                    if h == 0:
                        high_parts(n, ROUNDS - 1)
                    if h >= 7 and not last:
                        high_parts(n + 1, h - 7)
                    if h == 2 and not first:
                        denom_copy(n - 1, 1 - odd, 2)
                    if h == 6:
                        denom_copy(n, odd, 0)
                    if h == 10:
                        denom_copy(n, odd, 1)
                    if h == 4 and not last:
                        values_high(n + 1, 1 - odd)
                    if h == 6 and not last:
                        copy_h(n + 1)
                    probs_high(h, g)
                    if h + 2 < HEADS:
                        softmax(odd, h + 2, g + 2)
                    elif not last:
                        softmax(1 - odd, h + 2 - HEADS, g + 2)
                    if h == HEADS - 1 and not beyond(n, 2):
                        h_high(n + 2)

            images(act, body)
            denom_copy(B - 1, (B - 1) % 2, 2)

        @block.vector
        def _(dve):
            dve.memset(zeros[:], 0.0).then_inc(zero_set, 1)
            for i in range(2):
                dve.memset(v_own[i].bitcast(F32).rearrange("p a b -> p (a b)"), 0.0).then_inc(zero_set, 1)
            for i in range(3):
                dve.memset(probT_hi[i].bitcast(F32)[:, :, SEQ:EV], 0.0).then_inc(zero_set, 1)
                dve.memset(probT_lo[i].bitcast(F32)[:, :, SEQ:EV], 0.0).then_inc(zero_set, 1)
            dve.memset(k_own.bitcast(F32).rearrange("p h s -> p (h s)"), 0.0).then_inc(zero_set, 1)
            dve.wait_ge(consts_in, CONSTS)
            dve.tensor_tensor(add_rows[:, :, 0:D], add_rows[:, :, 0:D], pos_rows[:], ALU.add).then_inc(add_step, 1)
            dve.wait_ge(add_step, 1)
            dve.tensor_copy(add_rows[:, :, D:W2], add_rows[:, :, P:D]).then_inc(add_ready, 1)
            dve.tensor_copy(wqkv[:, :, 0, :], raw_qkv[:]).then_inc(qkv_split, 1)
            dve.wait_ge(add_turned, 1)
            dve.tensor_copy(addT.rearrange("p k s -> p (k s)"), fb[:, 0:2 * SEQ]).then_inc(add_ready, 1)
            dve.wait_ge(qkv_split, 1)
            dve.tensor_tensor(wqkv[:, :, 1, :], raw_qkv[:], wqkv[:, :, 0, :].bitcast(F32), ALU.subtract)\
               .then_inc(qkv_split, 1)
            dve.wait_ge(add_ready, 2)
            dve.tensor_copy(hT[:, :, 0:1], addT[:, :, 0:1]).then_inc(cls_col, 1)
            dve.wait_ge(zero_set, 10)

            def add_position(m):
                dve.wait_ge(tok_done, m + 1)
                at_least(dve, h_turned, m)
                at_least(dve, hT_split, 2 * m)
                dve.tensor_tensor(hT[:, :, 1:SEQ], fb[:, 0:2 * NP].rearrange("p (k s) -> p k s", k=2),
                                  addT[:, :, 1:SEQ], ALU.add).then_inc(hT_ready, 1)

            def h_low(m):
                dve.wait_ge(hT_high_ready, 2 * m + 1)
                dve.tensor_tensor(hT_parts[:, 2, :], hT[:, 0, :], hT_parts[:, 0, :].bitcast(F32), ALU.subtract)\
                   .then_inc(hT_split, 1)
                dve.wait_ge(hT_high_ready, 2 * m + 2)
                dve.scalar_tensor_tensor(out=hT_parts[:, 1, :], in0=hT[:, 1, :], scalar=split[:, 5:6], in1=hT_high[:],
                                         op0=ALU.mult, op1=ALU.subtract).then_inc(hT_split, 1)

            def rope(m, t):
                dve.wait_ge(qk_done, 2 * m + 2 - t)
                at_least(dve, qk_ready, 4 * NG * m)
                b = (fa, fb)[t]
                src = b[0:R, 0:2 * D]
                heads = src.rearrange("p (h d) -> p h d", d=HD)
                dims = [list(d) for d in src.ap]
                swap = bass.AP(src.tensor, src.offset + HD // 2, [dims[0], [HD, 2 * HEADS], [-(HD // 2), 2], [1, HD // 2]])
                c = repeat(cos[:, t, :], 1, 2 * HEADS)
                s = repeat(sin[:, t, :].rearrange("p (a b) -> p a b", a=2), 1, 2 * HEADS)
                dve.tensor_tensor(rope_a[t].rearrange("p (h d) -> p h d", d=HD), heads, c, ALU.mult).then_inc(rope_step, 1)
                dve.tensor_tensor(rope_b[t].rearrange("p (h a b) -> p h a b", a=2, b=HD // 2), swap, s, ALU.mult)\
                   .then_inc(rope_step, 1)

            def values_low(m, i):
                dve.wait_ge(v_high, 2 * m + 2)
                for t in range(2):
                    own = v_own[i][:, t, :].rearrange("p (h w) -> p h w", w=DIAG)
                    src = fb[0:R, t * D:(t + 1) * D].rearrange("p (h d) -> p h d", d=HD)
                    op = dve.scalar_tensor_tensor(out=own[:, :, HD:SUB], in0=src, scalar=vmask[:, t:t + 1],
                                                  in1=own[:, :, 0:HD].bitcast(F32), op0=ALU.mult, op1=ALU.subtract)
                op.then_inc(v_ready, 1)

            def stack_queries(m, group):
                dve.wait_ge(high_ready, ROUNDS * m + 2 * group + 1)
                at_least(dve, score_done, (m - 1) * HEADS + G4 * (group + 1))
                dve.scalar_tensor_tensor(out=qT[:, 2 * group:2 * group + 2, :].rearrange("p c s -> p (c s)"),
                                         in0=fa[:, 0:2 * SEQ], scalar=split[:, 1:2],
                                         in1=high[0].rearrange("p c s -> p (c s)"),
                                         op0=ALU.mult, op1=ALU.subtract).then_inc(q_ready, 1)

            def stack_keys(m, group):
                dve.wait_ge(raw_ready, NG * m + group + 1)
                at_least(dve, score_done, (m - 1) * HEADS + G4 * (group + 1))
                for part in range(2):
                    rows = slice(part * P // 2, (part + 1) * P // 2)
                    h = group * G4 + part
                    op = dve.scalar_tensor_tensor(out=k_own[rows, h:h + 3:2, 0:SEQ], in0=raw[rows],
                                                  scalar=split[rows, 3:4], in1=high[1][rows],
                                                  op0=ALU.mult, op1=ALU.subtract)
                op.then_inc(k_ready, 1)

            def maxima(i, h, g):
                dve.wait_ge(score_done, g + 1)
                dve.tensor_reduce(neg_max[i][:, h, :],
                                  score[h % 2][0:R, 0:2 * EV].rearrange("p (t s) -> p t s", t=2)[:, :, 0:SEQ],
                                  AX_X, ALU.max, negate=True).then_inc(max_ready, 1)

            def probs_low(h, g):
                dve.wait_ge(hi_ready, g + 1)
                at_least(dve, pv_done, g - 2)
                dve.tensor_tensor(probT_lo[h % 3][:, :, 0:SEQ], turned[h % 2][0:R, 0:2 * SEQ].rearrange("p (k s) -> p k s", k=2),
                                  probT_hi[h % 3].bitcast(F32)[:, :, 0:SEQ], ALU.subtract).then_inc(probT_ready, 1)

            def denoms(n, i, group):
                c = NG * n + group
                dve.wait_ge(prob_ready, n * HEADS + (group + 1) * G4)
                dve.reciprocal(rden.rearrange("p h t -> p (h t)"),
                               denom[i][:, group * G4:(group + 1) * G4, :].rearrange("p h t -> p (h t)"))\
                   .then_inc(rden_ready, 1)
                dve.wait_ge(rden_ready, c + 1)
                at_least(dve, rdenT_done, c)
                dve.tensor_copy(rden_wide[:], repeat(rden.rearrange("p h t -> p t h"), 3, SUB)).then_inc(wide_ready, 1)

            def normalise_heads(n, i, group):
                c = NG * n + group
                dve.wait_ge(rdenT_ready, c + 1)
                if group == 0:
                    at_least(dve, proj_done, n)
                dve.tensor_tensor(oT[:, group, :], out_b[(i + group) % 2][:, 0:SEQ], rdenT[group % 2][:], ALU.mult)\
                   .then_inc(oT_ready, 1)

            def measure(n, i):
                dve.wait_ge(proj_done, n + 1)
                dve.wait_ge(res_ready, n + 1)
                at_least(dve, h1_ready, n)
                dve.tensor_tensor(res2[:], fa[0:R, 0:2 * D].rearrange("p (t d) -> p t d", t=2), res[i][:], ALU.add)\
                   .then_inc(ln_step, 1)
                dve.wait_ge(ln_step, n * LN + 1)
                for t in range(2):
                    op = dve.bn_stats(stats[:, t, :], res2[:, t, :])
                op.then_inc(ln_step, 1)
                hold(dve, dve_passed, ln_step, n * LN + 2)
                for t in range(2):
                    dve.bn_aggr(moments[:, t, :], stats[:, t, :]).then_inc(ln_step, 1)

            add_position(0)
            h_low(0)
            rope(0, 1)
            rope(0, 0)
            values_low(0, 0)
            for group in range(NG):
                stack_queries(0, group)
                if group < NG - 1:
                    stack_keys(0, group)
            add_position(1)
            maxima(0, 0, 0)
            maxima(0, 1, 1)

            def body(n, k, odd, first, last):
                for h in range(HEADS):
                    g = n * HEADS + h
                    if h == 11 and not last:
                        stack_queries(n + 1, 2)
                    if h == 0 and not last:
                        h_low(n + 1)
                    if h + 2 < HEADS:
                        maxima(odd, h + 2, g + 2)
                    elif not last:
                        maxima(1 - odd, h + 2 - HEADS, g + 2)
                    if h == 11 and not beyond(n, 2):
                        add_position(n + 2)
                    if h == 6 and not first:
                        measure(n - 1, 1 - odd)
                    if h in (2, 3) and not last:
                        rope(n + 1, 3 - h)
                    if h == 0:
                        stack_keys(n, 2)
                    if 7 <= h < 11 and not last:
                        (stack_queries, stack_keys)[(h - 7) % 2](n + 1, (h - 7) // 2)
                    probs_low(h, g)
                    if h == 2 and not first:
                        normalise_heads(n - 1, 1 - odd, 2)
                    if h == 6:
                        normalise_heads(n, odd, 0)
                    if h == 10:
                        normalise_heads(n, odd, 1)
                    if h == 4 and not last:
                        values_low(n + 1, 1 - odd)
                    if h % G4 == G4 - 1:
                        denoms(n, odd, h // G4)

            images(dve, body)
            normalise_heads(B - 1, (B - 1) % 2, 2)
            measure(B - 1, (B - 1) % 2)


def tables(S):
    inv_freq = 1.0 / ROPE_THETA ** (np.arange(0, HD, 2, dtype=np.float64) / HD)
    freqs = np.outer(np.arange(S.seq, dtype=np.float64), inv_freq)
    cos = np.cos(np.concatenate([freqs, freqs], axis=-1)).astype(np.float32)
    sin = np.sin(np.concatenate([-freqs, freqs], axis=-1)).astype(np.float32)
    tiles = [slice(0, S.rows), slice(S.second, S.seq)]
    low_q, low_k = (np.tile(np.repeat(np.array(x, np.float32), HD), P // (4 * HD)) for x in ((0, 0, 1, 1), (0, 1, 0, 1)))
    scale = HD ** -0.5
    low_x = np.repeat(np.array([0, 1], np.float32), P // 2)
    vmask = np.ones((S.rows, 2), np.float32)
    vmask[0, 1] = 0.0
    before = np.triu(np.ones((P, P), np.float32), 1)
    first_slot = np.arange(S.experts, dtype=np.float32) * CAP
    return {
        "ident": np.eye(P, dtype=np.float32),
        "cos": np.stack([cos[t] for t in tiles], axis=1),
        "sin": np.stack([sin[t] for t in tiles], axis=1),
        "split": np.stack([scale * (2 * low_q - 1), scale * low_q, 2 * low_k - 1, low_k, 2 * low_x - 1, low_x],
                          axis=1).astype(np.float32),
        "split_x": np.stack([2 * low_x - 1, low_x], axis=1).astype(np.float32),
        "vmask": vmask,
        "before": before,
        "slot_base": np.tile(BIG - first_slot, (P, 1)).astype(np.float32),
        "slot_limit": np.tile(BIG - first_slot - CAP, (P, 1)).astype(np.float32),
        "token_id": (np.arange(CHUNK // P)[None, :] * P + np.arange(P)[:, None]).astype(np.float32),
        "empty": (S.padded + np.arange(S.slots) % CAP).astype(np.int32).reshape(P, -1),
    }


def routing_phase(nc, S, wg, e_bias, wsg, wsu, wsd, t_ident, t_split, t_before, t_base, t_limit, t_token, hx, acc, slot_token):
    from contextlib import ExitStack

    HALF, D, E, NC, FT, SFF = S.half, S.dim, S.experts, S.chunks, S.ff_tile, S.sff
    T = CHUNK // P
    STEPS = 28

    with ExitStack() as ctx:
        def sb(name, shape, dt=F32):
            return ctx.enter_context(nc.sbuf_tensor(name, shape, dt))

        def bank(name):
            return ctx.enter_context(nc.psum_tensor(name, [P, 512], F32))

        def sem(name):
            return ctx.enter_context(nc.semaphore(name))

        ident = sb("b_ident", [P, P])
        before_f = sb("b_before_f", [P, P])
        before = sb("b_before", [P, P], BF16)
        ones = sb("b_ones", [P, P], BF16)
        base = sb("b_base", [P, E])
        limit = sb("b_limit", [P, E])
        bias = sb("b_bias", [P, E])
        split = sb("b_split", [P, 2])
        wg_rows = sb("b_wg_rows", [E, S.wide])
        raw = [sb("b_raw_gate", [P, 2, E]), sb("b_raw_g", [P, 2, S.shared]), sb("b_raw_u", [P, 2, S.shared])]
        wgT = sb("b_wgT", [P, 2, 2, E], F32R)
        w_g = sb("b_w_g", [P, 2, 2, S.shared], F32R)
        w_u = sb("b_w_u", [P, 2, 2, S.shared], F32R)
        w_d = sb("b_w_d", [FT, SFF, D])
        token_f = [sb(f"b_token_f{i}", [P, T]) for i in range(2)]
        token_i = [sb(f"b_token_i{i}", [P, T], I32) for i in range(2)]
        rows = [sb(f"b_rows{i}", [P, T, S.wide]) for i in range(2)]
        xT = sb("b_xT", [P, 3, CHUNK], F32R)
        high = sb("b_high", [P, CHUNK])
        sig = sb("b_sig", [P, T, E])
        choice = sb("b_choice", [P, T, E + 2])
        top = sb("b_top", [P, T, 8])
        replaced = sb("b_replaced", [P, T, E + 2])
        mask = sb("b_mask", [P, T, E], BF16)
        place = sb("b_place", [P, T, E])
        place_m = sb("b_place_m", [P, T, E])
        in_cap = sb("b_in_cap", [P, T, E])
        place_v = sb("b_place_v", [P, T, E])
        slots8 = sb("b_slots8", [P, T, 8])
        slot_i = [sb(f"b_slot_i{i}", [P, T, 8], I32) for i in range(2)]
        wsel = sb("b_wsel", [P, T, E])
        wsum = sb("b_wsum", [P, T])
        wden = sb("b_wden", [P, T])
        winv = sb("b_winv", [P, T])
        weight = [sb(f"b_weight{i}", [P, T, E]) for i in range(2)]
        silu_g = [sb(f"b_silu{i}", [FT, CHUNK]) for i in range(2)]
        inter = sb("b_inter", [FT, SFF, CHUNK])
        total = [sb(f"b_total{i}", [P, T, D]) for i in range(2)]

        t0, t1, gate_b, down_b = bank("b_t0"), bank("b_t1"), bank("b_gate"), bank("b_down")
        g_b = [bank("b_g0"), bank("b_g1")]
        u_b = [bank("b_u0"), bank("b_u1")]

        consts_in, setup = sem("b_consts_in"), sem("b_setup")
        wg_turned, wgT_ready = sem("b_wg_turned"), sem("b_wgT_ready")
        rows_in = [sem("b_rows_in0"), sem("b_rows_in1")]
        x_turned, xT0_ready, xT1_ready = sem("b_x_turned"), sem("b_xT0_ready"), sem("b_xT1_ready")
        gate_done, sig_ready = sem("b_gate_done"), sem("b_sig_ready")
        route_step, mask_ready, prefix_done = sem("b_route_step"), sem("b_mask_ready"), sem("b_prefix_done")
        slots_ready, weight_ready = sem("b_slots_ready"), sem("b_weight_ready")
        up_done, silu_ready, inter_ready = sem("b_up_done"), sem("b_silu_ready"), sem("b_inter_ready")
        down_done, total_ready = sem("b_down_done"), sem("b_total_ready")
        weight_out = [sem("b_weight_out0"), sem("b_weight_out1")]
        total_out = [sem("b_total_out0"), sem("b_total_out1")]
        scattered = [sem("b_scattered0"), sem("b_scattered1")]
        token_step = sem("b_token_step")

        SCATTERS = T * TOP_K * 16
        CONSTS = 17 * 16

        pool_passed, dve_passed = sem("b_pool_passed"), sem("b_dve_passed")
        block = ctx.enter_context(nc.Block())

        def chunks(eng, body):
            body(0, 0, 0, True, NC == 1)
            if NC == 1:
                return
            body(1, 0, 1, False, NC == 2)
            full = (NC - 3) // 2
            if full > 0:
                with eng.Fori(1, 1 + full) as k:
                    body(k * 2, k, 0, False, False)
                    body(k * 2 + 1, k, 1, False, False)
            for c in range(2 + 2 * max(full, 0), NC):
                body(c, c // 2, c % 2, False, c == NC - 1)

        def tile_rows(c, lo, width, handle):
            v = handle[bass.ds(c * CHUNK, CHUNK), lo:lo + width]
            return v.rearrange("(t p) d -> p t d", p=P)

        @block.sync
        def _(sp):
            for dst, src in ((ident[:], t_ident), (before_f[:], t_before), (base[:], t_base), (limit[:], t_limit),
                             (bias[:], e_bias.partition_broadcast(P)), (wg_rows[:, 0:D], wg), (wg_rows[:, D:S.wide], wg[:, P:D]), (split[:], t_split),
                             (raw[1][:, 0, :], wsg[0:P, :]), (raw[1][0:P // 2, 1, :], wsg[P:D, :]),
                             (raw[1][P // 2:P, 1, :], wsg[P:D, :]),
                             (raw[2][:, 0, :], wsu[0:P, :]), (raw[2][0:P // 2, 1, :], wsu[P:D, :]),
                             (raw[2][P // 2:P, 1, :], wsu[P:D, :]),
                             (w_d[:], wsd.rearrange("(j p) n -> p j n", p=FT)),
                             (token_f[0][:], t_token), (token_f[1][:], t_token)):
                sp.dma_start(dst, src).then_inc(consts_in, 16)

            def load(c, i):
                sp.dma_start(rows[i][:, :, 0:D], tile_rows(c, 0, D, hx)).then_inc(rows_in[i], 16)
                sp.dma_start(rows[i][:, :, D:S.wide], tile_rows(c, P, S.third, hx)).then_inc(rows_in[i], 16)

            load(0, 0)
            if NC > 1:
                load(1, 1)

            def body(c, k, odd, first, last):
                sp.wait_ge(weight_ready, c + 1)
                sp.dma_start(tile_rows(c, D, E, hx), weight[odd][:]).then_inc(weight_out[odd], 16)
                sp.wait_ge(total_ready, 2 * (c + 1))
                sp.dma_start(tile_rows(c, 0, D, acc), total[odd][:]).then_inc(total_out[odd], 16)
                if not (isinstance(c, int) and c + 2 >= NC):
                    load(c + 2, odd)

            chunks(sp, body)
            for i in range(2):
                n = (NC + 1 - i) // 2
                if n:
                    sp.wait_ge(weight_out[i], 16 * n)
                    sp.wait_ge(total_out[i], 16 * n)
                    sp.wait_ge(scattered[i], SCATTERS * n)

        @block.gpsimd
        def _(pool):
            pool.memset(ones[:], 1.0).then_inc(setup, 1)
            hold(pool, pool_passed, consts_in, CONSTS)
            pool.tensor_scalar(token_f[1][:], token_f[1][:], float(CHUNK), None, ALU.add).then_inc(token_step, 1)

            def body(c, k, odd, first, last):
                hold(pool, pool_passed, token_step, 2 * c + 1 if not first else 1)
                hold(pool, pool_passed, scattered[odd], k * SCATTERS)
                pool.tensor_copy(token_i[odd][:], token_f[odd][:]).then_inc(token_step, 1)
                hold(pool, pool_passed, token_step, 2 * c + 2)
                pool.tensor_scalar(token_f[odd][:], token_f[odd][:], float(2 * CHUNK), None, ALU.add)\
                    .then_inc(token_step, 1)
                hold(pool, pool_passed, slots_ready, c + 1)
                for t in range(T):
                    for j in range(TOP_K):
                        pool.indirect_dma_start(
                            slot_token, bass.IndirectOffsetOnAxis(ap=slot_i[odd][:, t, j:j + 1], axis=0),
                            token_i[odd][:, t:t + 1], None, bounds_check=S.slots - 1, oob_is_err=False,
                        ).then_inc(scattered[odd], 16)

            chunks(pool, body)

        @block.tensor
        def _(pe):
            pe.wait_ge(consts_in, CONSTS)
            for kh in range(2):
                mm = pe.transpose(gate_b[:, kh * P:kh * P + E], wg_rows[:, kh * P:(kh + 1) * P], ident[0:E, 0:E])
            mm.then_inc(wg_turned, 1)
            pe.wait_ge(setup, 2)
            pe.wait_ge(wgT_ready, 8)

            def turn(c, k, i):
                pe.wait_ge(rows_in[i], (k + 1) * 32)
                at_least(pe, route_step, (c - 1) * STEPS + 12)
                for kh in range(2):
                    for t in range(T):
                        mm = pe.transpose((t0, t1)[kh][:, t * P:(t + 1) * P], rows[i][:, t, kh * P:(kh + 1) * P],
                                          ident[:])
                mm.then_inc(x_turned, 1)

            def gate(c):
                pe.wait_ge(xT1_ready, 2 * (c + 1))
                at_least(pe, sig_ready, c)
                for t in range(T):
                    for n, (x, k, part) in enumerate(PRODUCTS):
                        mm = pe.matmul(gate_b[:, t * E:(t + 1) * E], xT[:, x, t * P:(t + 1) * P], wgT[:, k, part, :],
                                       start=(n == 0), stop=(n == len(PRODUCTS) - 1))
                mm.then_inc(gate_done, 1)

            def up(c, j):
                at_least(pe, inter_ready, c * SFF + j - 1)
                for w, b in ((w_g, g_b), (w_u, u_b)):
                    for n, (x, k, part) in enumerate(PRODUCTS):
                        mm = pe.matmul(b[j % 2][0:FT, :], w[:, k, part, j * FT:(j + 1) * FT], xT[:, x, :],
                                       start=(n == 0), stop=(n == len(PRODUCTS) - 1))
                mm.then_inc(up_done, 1)

            def prefix(c):
                pe.wait_ge(mask_ready, c + 1)
                for t in range(T):
                    for u in range(t + 1):
                        pe.matmul(t0[:, t * E:(t + 1) * E], before[:] if u == t else ones[:], mask[:, u, :],
                                  start=(u == 0), stop=(u == t))
                for t in range(T):
                    mm = pe.matmul(t1[:, 0:E], ones[:], mask[:, t, :], start=(t == 0), stop=(t == T - 1))
                mm.then_inc(prefix_done, 1)

            def down(c, q):
                at_least(pe, total_ready, 2 * c + q)
                for t in range(2):
                    for j in range(SFF):
                        if q == 0 and t == 0:
                            pe.wait_ge(inter_ready, c * SFF + j + 1)
                        s = (2 * q + t) * P
                        mm = pe.matmul(down_b[:, t * D:(t + 1) * D], inter[:, j, s:s + P], w_d[:, j, :],
                                       start=(j == 0), stop=(j == SFF - 1))
                mm.then_inc(down_done, 1)

            turn(0, 0, 0)
            gate(0)

            def body(c, k, odd, first, last):
                for j in range(SFF):
                    up(c, j)
                    if j == 1:
                        prefix(c)
                if not last:
                    turn(c + 1, k + odd, 1 - odd)
                down(c, 0)
                if not last:
                    gate(c + 1)
                down(c, 1)

            chunks(pe, body)

        @block.scalar
        def _(act):
            act.wait_ge(consts_in, CONSTS)

            def copy_x(c):
                act.wait_ge(x_turned, c + 1)
                act.activation(xT[:, 0, :], t0[:], ACT.Copy).then_inc(xT0_ready, 1)
                at_least(act, xT1_ready, 2 * c)
                act.activation(high.bitcast(F32R)[:], t1[:], ACT.Copy, scale=split[:, 0:1]).then_inc(xT0_ready, 1)

            def sigmoid(c):
                act.wait_ge(gate_done, c + 1)
                at_least(act, weight_ready, c)
                act.activation(sig.rearrange("p t e -> p (t e)"), gate_b[:, 0:T * E], ACT.Sigmoid).then_inc(sig_ready, 1)

            def silu(c, j):
                act.wait_ge(up_done, c * SFF + j + 1)
                at_least(act, inter_ready, c * SFF + j - 1)
                act.activation(silu_g[j % 2][:], g_b[j % 2][0:FT, :], ACT.Silu).then_inc(silu_ready, 1)

            copy_x(0)
            sigmoid(0)

            def body(c, k, odd, first, last):
                for j in range(SFF):
                    silu(c, j)
                if not last:
                    copy_x(c + 1)
                    sigmoid(c + 1)

            chunks(act, body)

        @block.vector
        def _(dve):
            dve.memset(choice[:, :, E:E + 2], SENTINEL).then_inc(setup, 1)
            dve.wait_ge(consts_in, CONSTS)
            dve.tensor_copy(before[:], before_f[:]).then_inc(wgT_ready, 1)
            dve.wait_ge(wg_turned, 1)
            dve.tensor_copy(raw[0][:], gate_b[:, 0:2 * P].rearrange("p (k e) -> p k e", k=2)[:, :, 0:E])\
               .then_inc(wgT_ready, 1)
            dve.wait_ge(wgT_ready, 2)
            for w, r in zip((wgT, w_g, w_u), raw):
                dve.tensor_copy(w[:, :, 0, :], r[:]).then_inc(wgT_ready, 1)
            dve.wait_ge(wgT_ready, 5)
            for w, r in zip((wgT, w_g, w_u), raw):
                dve.tensor_tensor(w[:, :, 1, :], r[:], w[:, :, 0, :].bitcast(F32), ALU.subtract).then_inc(wgT_ready, 1)

            def copy_x(c):
                dve.wait_ge(xT0_ready, 2 * c + 1)
                dve.tensor_tensor(xT[:, 2, :], t0[:], xT[:, 0, :].bitcast(F32), ALU.subtract).then_inc(xT1_ready, 1)
                dve.wait_ge(xT0_ready, 2 * c + 2)
                dve.scalar_tensor_tensor(out=xT[:, 1, :], in0=t1[:], scalar=split[:, 1:2], in1=high[:], op0=ALU.mult,
                                         op1=ALU.subtract).then_inc(xT1_ready, 1)

            def choose(c):
                z = c * STEPS
                dve.wait_ge(sig_ready, c + 1)
                dve.tensor_tensor(choice[:, :, 0:E], sig[:], repeat(bias[:], 1, T), ALU.add).then_inc(route_step, 1)
                hold(dve, dve_passed, route_step, z + 1)
                for t in range(T):
                    dve.max(top[:, t, :], choice[:, t, 0:E]).then_inc(route_step, 1)
                dve.wait_ge(route_step, z + 5)
                dve.memset(top[:, :, TOP_K:8], SENTINEL).then_inc(route_step, 1)
                hold(dve, dve_passed, route_step, z + 6)
                for t in range(T):
                    dve.match_replace(replaced[:, t, :], top[:, t, :], choice[:, t, :], TAKEN).then_inc(route_step, 1)
                dve.wait_ge(route_step, z + 10)
                at_least(dve, prefix_done, c)
                dve.tensor_scalar(mask[:], replaced[:, :, 0:E], TAKEN / 2, None, ALU.is_le).then_inc(mask_ready, 1)

            def queue_places(c):
                z = c * STEPS
                dve.wait_ge(prefix_done, c + 1)
                dve.tensor_tensor(place[:], repeat(base[:], 1, T), t0[:, 0:T * E].rearrange("p (t e) -> p t e", t=T),
                                  ALU.subtract).then_inc(route_step, 1)
                dve.wait_ge(route_step, z + 11)
                dve.tensor_tensor(base[:], base[:], t1[:, 0:E], ALU.subtract).then_inc(route_step, 1)
                dve.wait_ge(mask_ready, c + 1)
                dve.tensor_tensor(place_m[:], place[:], mask[:], ALU.mult).then_inc(route_step, 1)

            def drop_full(c):
                z = c * STEPS
                dve.wait_ge(route_step, z + 13)
                dve.tensor_tensor(in_cap[:], place_m[:], repeat(limit[:], 1, T), ALU.is_gt).then_inc(route_step, 1)
                dve.wait_ge(route_step, z + 14)
                dve.tensor_tensor(place_v[:], place_m[:], in_cap[:], ALU.mult).then_inc(route_step, 1)

            def six_slots(c, k, i):
                z = c * STEPS
                hold(dve, dve_passed, route_step, z + 15)
                for t in range(T):
                    dve.max(slots8[:, t, :], place_v[:, t, :]).then_inc(route_step, 1)
                dve.wait_ge(route_step, z + 19)
                at_least(dve, scattered[i], k * SCATTERS)
                dve.tensor_scalar(slot_i[i][:], slots8[:], -1.0, BIG, ALU.mult, ALU.add).then_inc(slots_ready, 1)

            def weights(c, k, i):
                z = c * STEPS
                for t in range(T):
                    dve.tensor_tensor_reduce(wsel[:, t, :], sig[:, t, :], mask[:, t, :], 1.0, 0.0, ALU.mult, ALU.add,
                                             wsum[:, t:t + 1]).then_inc(route_step, 1)
                dve.wait_ge(route_step, z + 23)
                dve.tensor_scalar(wden[:], wsum[:], 1e-20, None, ALU.add).then_inc(route_step, 1)
                dve.wait_ge(route_step, z + 24)
                dve.reciprocal(winv[:], wden[:]).then_inc(route_step, 1)
                dve.wait_ge(route_step, z + 25)
                at_least(dve, weight_out[i], k * 16)
                for t in range(T):
                    op = dve.tensor_scalar(weight[i][:, t, :], wsel[:, t, :], winv[:, t:t + 1], ROUTE_SCALE,
                                           ALU.mult, ALU.mult)
                    op.then_inc(weight_ready if t == T - 1 else route_step, 1)

            def gated(c, j):
                dve.wait_ge(silu_ready, c * SFF + j + 1)
                dve.tensor_tensor(inter[:, j, :], silu_g[j % 2][:], u_b[j % 2][0:FT, :], ALU.mult).then_inc(inter_ready, 1)

            def add_shared(c, k, i, q):
                if q == 0:
                    at_least(dve, total_out[i], k * 16)
                dve.wait_ge(down_done, 2 * c + q + 1)
                dve.tensor_tensor(total[i][:, 2 * q:2 * q + 2, :], down_b[:, 0:2 * D].rearrange("p (t d) -> p t d", t=2),
                                  rows[i][:, 2 * q:2 * q + 2, 0:D], ALU.add).then_inc(total_ready, 1)

            dve.wait_ge(setup, 2)
            copy_x(0)
            choose(0)

            def body(c, k, odd, first, last):
                for j in range(SFF):
                    gated(c, j)
                    if j == 2:
                        queue_places(c)
                    if j == 3:
                        drop_full(c)
                    if j == 4:
                        six_slots(c, k, odd)
                    if j == 5:
                        weights(c, k, odd)
                if not last:
                    copy_x(c + 1)
                add_shared(c, k, odd, 0)
                if not last:
                    choose(c + 1)
                add_shared(c, k, odd, 1)

            chunks(dve, body)


def experts_phase(nc, S, w_gate_up, w_down, t_ident, hx, acc, slot_token):
    from contextlib import ExitStack

    HALF, D, E, FT, FF = S.half, S.dim, S.experts, S.ff_tile, S.ff
    ST = CAP // 2

    with ExitStack() as ctx:
        def sb(name, shape, dt=F32):
            return ctx.enter_context(nc.sbuf_tensor(name, shape, dt))

        def bank(name):
            return ctx.enter_context(nc.psum_tensor(name, [P, 512], F32))

        def sem(name):
            return ctx.enter_context(nc.semaphore(name))

        ident = sb("c_ident", [P, P])
        w_gu = [sb(f"c_w_gu{i}", [HALF, 2, 2 * S.inner]) for i in range(2)]
        w_d = [sb(f"c_w_d{i}", [FT, FF, D]) for i in range(2)]
        token = [sb(f"c_token{i}", [ST, 2], I32) for i in range(4)]
        rows = [sb(f"c_rows{i}", [ST, 2, S.row]) for i in range(4)]
        xT = sb("c_xT", [HALF, 2 * CAP])
        silu_g = [sb(f"c_silu{i}", [FT, CAP]) for i in range(2)]
        inter = sb("c_inter", [FT, FF, CAP])
        y = [sb(f"c_y{i}", [ST, 2, D]) for i in range(2)]

        x_b = bank("c_x")
        gu_b = [bank(f"c_gu{i}") for i in range(4)]
        y_b = [bank("c_down0"), bank("c_down1")]

        ident_in = sem("c_ident_in")
        gu_in = [sem("c_gu_in0"), sem("c_gu_in1")]
        d_in = [sem("c_d_in0"), sem("c_d_in1")]
        token_in = [sem(f"c_token_in{i}") for i in range(4)]
        gathered = [sem(f"c_gathered{i}") for i in range(4)]
        x_turned, xT_ready = sem("c_x_turned"), sem("c_xT_ready")
        up_done, silu_ready, inter_ready = sem("c_up_done"), sem("c_silu_ready"), sem("c_inter_ready")
        down_done, y_ready = sem("c_down_done"), sem("c_y_ready")
        added = [sem(f"c_added{i}") for i in range(4)]

        pool_passed, dve_passed = sem("c_pool_passed"), sem("c_dve_passed")
        block = ctx.enter_context(nc.Block())

        def experts(eng, body):
            for i in range(4):
                body(i, 0, i, i == 0, E == i + 1)
            if E > 8:
                with eng.Fori(1, E // 4 - 1) as k:
                    for i in range(4):
                        body(k * 4 + i, k, i, False, False)
            k = E // 4 - 1
            for i in range(4):
                body(4 * k + i, k, i, False, i == 3)

        def beyond(e, ahead):
            return isinstance(e, int) and e + ahead >= E

        def wait_added(eng, k, i, back, passed=None):
            j = i - back
            if passed is None:
                at_least(eng, added[j % 4], 32 * (k + 1 + j // 4))
            else:
                hold(eng, passed, added[j % 4], 32 * (k + 1 + j // 4))

        @block.sync
        def _(sp):
            sp.dma_start(ident[:], t_ident).then_inc(ident_in, 16)

            def load_token(e, i):
                sp.dma_start(token[i][:], slot_token[bass.ds(e * CAP, CAP), :].rearrange("(p t) a -> p (t a)", t=2))\
                  .then_inc(token_in[i], 16)

            def load_weights(e, i):
                sp.dma_start(w_gu[i][:], w_gate_up[e].rearrange("(k p) n -> p k n", k=2)).then_inc(gu_in[i], 16)
                sp.dma_start(w_d[i][:], w_down[e].rearrange("(j p) n -> p j n", p=FT)).then_inc(d_in[i], 16)

            for e in range(3):
                load_token(e, e)
            load_weights(0, 0)
            load_weights(1, 1)

            def body(e, k, i, first, last):
                if not beyond(e, 3):
                    wait_added(sp, k, i, 1)
                    load_token(e + 3, (i + 3) % 4)
                if not beyond(e, 2):
                    sp.wait_ge(down_done, e + 1)
                    load_weights(e + 2, i % 2)

            experts(sp, body)
            for i in range(4):
                sp.wait_ge(added[i], 32 * (E // 4))

        @block.gpsimd
        def _(pool):
            def gather(e, k, i):
                hold(pool, pool_passed, token_in[i], 16 * (k + 1))
                hold(pool, pool_passed, y_ready, e - 3)
                for t in range(2):
                    pool.indirect_dma_start(rows[i][:, t, :], None, hx,
                                            bass.IndirectOffsetOnAxis(ap=token[i][:, t:t + 1], axis=0))\
                        .then_inc(gathered[i], 16)

            gather(0, 0, 0)
            gather(1, 0, 1)

            def body(e, k, i, first, last):
                if not beyond(e, 2):
                    gather(e + 2, k + (i + 2) // 4, (i + 2) % 4)
                hold(pool, pool_passed, y_ready, e + 1)
                wait_added(pool, k, i, 1, pool_passed)
                for t in range(2):
                    pool.indirect_dma_start(acc, bass.IndirectOffsetOnAxis(ap=token[i][:, t:t + 1], axis=0),
                                            y[i % 2][:, t, :], None, compute_op=ALU.add).then_inc(added[i], 16)

            experts(pool, body)

        @block.tensor
        def _(pe):
            pe.wait_ge(ident_in, 16)

            def turn(e, k, i):
                pe.wait_ge(gathered[i], 32 * (k + 1))
                for kh in range(2):
                    for t in range(2):
                        mm = pe.transpose(x_b[0:HALF, kh * CAP + t * ST:kh * CAP + (t + 1) * ST],
                                          rows[i][:, t, kh * HALF:(kh + 1) * HALF], ident[0:ST, 0:ST])
                mm.then_inc(x_turned, 1)

            turn(0, 0, 0)

            def body(e, k, i, first, last):
                k2 = k * 2 + i // 2
                pe.wait_ge(xT_ready, e + 1)
                pe.wait_ge(gu_in[i % 2], 16 * (k2 + 1))
                for j in range(FF):
                    at_least(pe, inter_ready, (e - 1) * FF + j + 1)
                    for w in range(2):
                        for kh in range(2):
                            c = w * S.inner + j * FT
                            mm = pe.matmul(gu_b[j][0:FT, w * CAP:(w + 1) * CAP], w_gu[i % 2][:, kh, c:c + FT],
                                           xT[:, kh * CAP:(kh + 1) * CAP], start=(kh == 0), stop=(kh == 1))
                    mm.then_inc(up_done, 1)
                if not last:
                    turn(e + 1, k + (i + 1) // 4, (i + 1) % 4)
                pe.wait_ge(d_in[i % 2], 16 * (k2 + 1))
                pe.wait_ge(inter_ready, (e + 1) * FF)
                at_least(pe, y_ready, e - 1)
                for t in range(2):
                    for j in range(FF):
                        mm = pe.matmul(y_b[i % 2][0:ST, t * D:(t + 1) * D], inter[:, j, t * ST:(t + 1) * ST],
                                       w_d[i % 2][:, j, :], start=(j == 0), stop=(j == FF - 1))
                mm.then_inc(down_done, 1)

            experts(pe, body)

        @block.scalar
        def _(act):
            def copy_x(e):
                act.wait_ge(x_turned, e + 1)
                act.activation(xT[:], x_b[0:HALF, 0:2 * CAP], ACT.Copy).then_inc(xT_ready, 1)

            copy_x(0)

            def body(e, k, i, first, last):
                for j in range(FF):
                    act.wait_ge(up_done, e * FF + j + 1)
                    at_least(act, inter_ready, e * FF + j - 1)
                    act.activation(silu_g[j % 2][:], gu_b[j][0:FT, 0:CAP], ACT.Silu).then_inc(silu_ready, 1)
                if not last:
                    copy_x(e + 1)

            experts(act, body)

        @block.vector
        def _(dve):
            def body(e, k, i, first, last):
                for j in range(FF):
                    dve.wait_ge(silu_ready, e * FF + j + 1)
                    at_least(dve, down_done, e)
                    dve.tensor_tensor(inter[:, j, :], silu_g[j % 2][:], gu_b[j][0:FT, CAP:2 * CAP], ALU.mult)\
                       .then_inc(inter_ready, 1)
                dve.wait_ge(down_done, e + 1)
                wait_added(dve, k, i, 2)
                for t in range(2):
                    op = dve.tensor_scalar(y[i % 2][:, t, :], y_b[i % 2][0:ST, t * D:(t + 1) * D],
                                           rows[i][:, t, bass.ds(e + D, 1)], None, ALU.mult)
                op.then_inc(y_ready, 1)

            experts(dve, body)


def final_phase(nc, S, acc, out):
    from contextlib import ExitStack

    D, B, J = S.dim, S.images, 14
    STEPS = S.seq // J
    REST = S.seq - STEPS * J

    with ExitStack() as ctx:
        def sb(name, shape, dt=F32):
            return ctx.enter_context(nc.sbuf_tensor(name, shape, dt))

        def sem(name):
            return ctx.enter_context(nc.semaphore(name))

        rows = [sb(f"d_rows{i}", [B, J, D]) for i in range(2)]
        norm = [sb(f"d_norm{i}", [B, J, D]) for i in range(2)]
        stats = sb("d_stats", [B, J, 6])
        moments = [sb(f"d_moments{i}", [B, J, 2]) for i in range(2)]
        rstd = [sb(f"d_rstd{i}", [B, J]) for i in range(2)]
        minus_half = sb("d_minus_half", [B, J])

        half_set = sem("d_half_set")
        rows_in = [sem("d_rows_in0"), sem("d_rows_in1")]
        out_done = [sem("d_out0"), sem("d_out1")]
        stats_ready, moments_ready, rstd_step = sem("d_stats_ready"), sem("d_moments_ready"), sem("d_rstd_step")
        norm_ready = sem("d_norm_ready")

        pool_passed, dve_passed = sem("d_pool_passed"), sem("d_dve_passed")
        block = ctx.enter_context(nc.Block())
        acc_v = acc[0:S.tokens, :].rearrange("(b s) d -> b s d", s=S.seq)

        def groups(eng, body):
            body(0, 0, 0, J)
            body(1, 0, 1, J)
            with eng.Fori(1, STEPS // 2 - 1) as k:
                body(k * 2, k, 0, J)
                body(k * 2 + 1, k, 1, J)
            k = STEPS // 2 - 1
            body(2 * k, k, 0, J)
            body(2 * k + 1, k, 1, J)
            body(STEPS, STEPS // 2, 0, REST)

        @block.sync
        def _(sp):
            def load(s, i, count):
                sp.dma_start(rows[i][:, 0:count, :], acc_v[:, bass.ds(s * J, count), :]).then_inc(rows_in[i], 16)

            load(0, 0, J)
            load(1, 1, J)

            def body(s, k, odd, count):
                sp.wait_ge(norm_ready, s + 1)
                sp.dma_start(out[:, bass.ds(s * J, count), :], norm[odd][:, 0:count, :]).then_inc(out_done[odd], 16)
                if not (isinstance(s, int) and s + 2 > STEPS):
                    load(s + 2, odd, REST if isinstance(s, int) and s + 2 == STEPS else J)

            groups(sp, body)
            sp.wait_ge(out_done[0], 16 * (STEPS // 2 + 1))
            sp.wait_ge(out_done[1], 16 * (STEPS // 2))

        @block.gpsimd
        def _(pool):
            pool.memset(minus_half[:], -0.5).then_inc(half_set, 1)
            hold(pool, pool_passed, half_set, 1)

            def body(s, k, odd, count):
                hold(pool, pool_passed, moments_ready, s + 1)
                hold(pool, pool_passed, norm_ready, s - 1)
                pool.tensor_scalar(rstd[odd][:, 0:count], moments[odd][:, 0:count, 1], LN_EPS, None, ALU.add)\
                    .then_inc(rstd_step, 1)
                hold(pool, pool_passed, rstd_step, 2 * s + 1)
                pool.tensor_tensor(rstd[odd][:, 0:count], rstd[odd][:, 0:count], minus_half[:, 0:count], ALU.pow)\
                    .then_inc(rstd_step, 1)

            groups(pool, body)

        @block.vector
        def _(dve):
            def measure(s, k, odd, count):
                dve.wait_ge(rows_in[odd], 16 * (k + 1))
                at_least(dve, moments_ready, s)
                for j in range(count):
                    op = dve.bn_stats(stats[:, j, :], rows[odd][:, j, :])
                op.then_inc(stats_ready, 1)
                hold(dve, dve_passed, stats_ready, s + 1)
                for j in range(count):
                    op = dve.bn_aggr(moments[odd][:, j, :], stats[:, j, :])
                op.then_inc(moments_ready, 1)

            def apply(s, k, odd, count):
                dve.wait_ge(rstd_step, 2 * s + 2)
                at_least(dve, out_done[odd], 16 * k)
                for j in range(count):
                    op = dve.tensor_scalar(norm[odd][:, j, :], rows[odd][:, j, :], moments[odd][:, j, 0:1],
                                           rstd[odd][:, j:j + 1], ALU.subtract, ALU.mult)
                op.then_inc(norm_ready, 1)

            def body(s, k, odd, count):
                measure(s, k, odd, count)
                apply(s, k, odd, count)

            groups(dve, body)


def vit_tower_moe_kernel(nc, S, x, tok_w, tok_b, pos, cls, w_qkv, w_proj, b_proj, wg, e_bias, w_gate_up, w_down,
                         wsg, wsu, wsd, t, out):
    hx = nc.dram_tensor("hx_scratch", [S.all_rows, S.row], F32, kind="Internal").ap()
    acc = nc.dram_tensor("acc_scratch", [S.all_rows, S.dim], F32, kind="Internal").ap()
    slot_token = nc.dram_tensor("slot_token_scratch", [S.slots, 1], I32, kind="Internal").ap()
    attention_phase(nc, S, x, tok_w, tok_b, pos, cls, w_qkv, w_proj, b_proj, t["ident"], t["cos"], t["sin"],
                    t["split"], t["vmask"], hx, acc, slot_token, t["empty"])
    routing_phase(nc, S, wg, e_bias, wsg, wsu, wsd, t["ident"], t["split_x"], t["before"], t["slot_base"], t["slot_limit"],
                  t["token_id"], hx, acc, slot_token)
    experts_phase(nc, S, w_gate_up, w_down, t["ident"], hx, acc, slot_token)
    final_phase(nc, S, acc, out)


_INS = ['x', 'L0_tok_W', 'L0_tok_b', 'L0_tok_pos_table', 'L0_tok_class_token', 'L0_attn_w_qkv', 'L0_attn_w_proj',
        'L0_attn_b_proj', 'L0_ffn_Wg', 'L0_ffn_e_bias', 'L0_ffn_W_gate_up', 'L0_ffn_W_down', 'L0_ffn_Wsg',
        'L0_ffn_Wsu', 'L0_ffn_Wsd']


def kernel(**inputs):
    import numpy as _np
    import concourse.bacc as _bacc
    from concourse import mybir as _mybir
    from concourse.bass_utils import run_bass_kernel_spmd as _run

    nc = _bacc.Bacc("TRN2", target_bir_lowering=False, num_devices=1)
    arrays, args = {}, []
    for name in _INS:
        a = _np.ascontiguousarray(inputs[name])
        arrays[f"in_{name}_dram"] = a
        args.append(nc.dram_tensor(f"in_{name}_dram", a.shape, _mybir.dt.from_np(a.dtype), kind="ExternalInput").ap())
    S = Shapes(inputs["x"], inputs["L0_tok_W"], inputs["L0_tok_pos_table"], inputs["L0_ffn_Wg"],
               inputs["L0_ffn_W_gate_up"], inputs["L0_ffn_Wsg"])
    consts = {}
    for name, a in tables(S).items():
        arrays[f"const_{name}_dram"] = a
        consts[name] = nc.dram_tensor(f"const_{name}_dram", a.shape, _mybir.dt.from_np(a.dtype),
                                      kind="ExternalInput").ap()
    out = nc.dram_tensor("out_0_dram", (S.images, S.seq, S.dim), F32, kind="ExternalOutput").ap()
    vit_tower_moe_kernel(nc, S, *args, consts, out)
    r = _run(nc, [arrays], core_ids=[0])
    return r.results[0]["out_0_dram"]
```

```python
import numpy as np

import concourse.bass as bass
from concourse import mybir

F32 = mybir.dt.float32
F32R = mybir.dt.float32r
BF16 = mybir.dt.bfloat16
I32 = mybir.dt.int32
ALU = mybir.AluOpType
ACT = mybir.ActivationFunctionType
AX_X = mybir.AxisListType.X

P = 128
PATCH = 16
HEADS = 12
HD = 16
TOP_K = 6
CAP = 192
ROUTE_SCALE = 2.5
LN_EPS = 1e-5
ROPE_THETA = 10000.0
BIG = 65536.0
SENTINEL = 3.0e38
TAKEN = -3.0e38
CHUNK = 512


PRODUCTS = [(0, 0, 0), (0, 0, 1), (2, 0, 0), (1, 1, 0), (1, 1, 1)]


class Shapes:

    def __init__(self, x, tok_w, pos, wg, w_gate_up, wsg):
        self.images, self.chans, self.height, self.width = x.shape
        self.gh, self.gw = self.height // PATCH, self.width // PATCH
        self.patches = self.gh * self.gw
        self.seq = pos.shape[0]
        self.dim = tok_w.shape[1]
        self.half = self.dim // 2
        self.half_heads = HEADS // 2
        self.rows = (self.seq + 1) // 2
        self.second = self.seq - self.rows
        self.tokens = self.images * self.seq
        self.chunks = -(-self.tokens // CHUNK)
        self.padded = self.chunks * CHUNK
        self.experts = wg.shape[0]
        self.slots = self.experts * CAP
        self.all_rows = self.padded + CAP
        self.inner = w_gate_up.shape[2] // 2
        self.shared = wsg.shape[1]
        self.ff_tile = 116
        self.ff = self.inner // self.ff_tile
        self.sff = self.shared // self.ff_tile
        self.third = self.dim - P
        self.wide = self.dim + self.third
        self.row = self.dim + self.experts
        self.even = self.seq + 1
        self.group = 4
        self.groups = HEADS // self.group


def repeat(ap, axis, count):
    dims = [list(d) for d in ap.ap]
    dims.insert(axis, [0, count])
    return bass.AP(ap.tensor, ap.offset, dims)


def at_least(eng, sem, value):
    if isinstance(value, int) and value <= 0:
        return
    eng.wait_ge(sem, value)


def hold(eng, passed, sem, value):
    if isinstance(value, int) and value <= 0:
        return
    eng.wait_ge(sem, value)
    eng.sem_inc(passed, 1)


def attention_phase(nc, S, x, tok_w, tok_b, pos, cls, w_qkv, w_proj, b_proj,
                    t_ident, t_cos, t_sin, t_split, t_vmask, hx, acc, slot_token, t_empty):
    from contextlib import ExitStack

    R, SEQ, SEC, NP = S.rows, S.seq, S.second, S.patches
    D, B, W2 = S.dim, S.images, S.wide
    KR = S.chans * PATCH
    PJ = PATCH // 2
    GW, GH = S.gw, S.gh
    EV, G4, NG = S.even, S.group, S.groups
    SUB = 2 * HD
    DIAG = P + SUB
    COPIES = 4
    PAIRS = HEADS // 2
    ROUNDS = 2 * NG
    DEN = P * 2
    LN = 6

    with ExitStack() as ctx:
        def sb(name, shape, dt=F32):
            return ctx.enter_context(nc.sbuf_tensor(name, shape, dt))

        def bank(name):
            return ctx.enter_context(nc.psum_tensor(name, [P, 512], F32))

        def sem(name):
            return ctx.enter_context(nc.semaphore(name))

        ident = sb("a_ident", [P, P])
        cos = sb("a_cos", [R, 2, HD])
        sin = sb("a_sin", [R, 2, HD])
        split = sb("a_split", [P, 6])
        vmask = sb("a_vmask", [R, 2])
        wt = sb("a_wt", [2 * KR, PJ, W2])
        raw_qkv = sb("a_raw_qkv", [P, 2, 3 * D])
        wqkv = sb("a_wqkv", [P, 2, 2, 3 * D], F32R)
        wp = sb("a_wp", [P, NG, D])
        bproj = sb("a_bproj", [R, D])
        pos_rows = sb("a_pos_rows", [R, 2, D])
        add_rows = sb("a_add_rows", [R, 2, W2])
        addT = sb("a_addT", [P, 2, SEQ])
        zeros = sb("a_zeros", [P, S.row])
        empty = sb("a_empty", [P, S.slots // P], I32)
        img = [sb(f"a_img{i}", [2 * KR, GH, S.width]) for i in range(2)]
        hT = sb("a_hT", [P, 2, SEQ])
        hT_high = sb("a_hT_high", [P, SEQ])
        hT_parts = sb("a_hT_parts", [P, 3, SEQ], F32R)
        rope_a = [sb(f"a_rope_a{i}", [R, 2 * D]) for i in range(2)]
        rope_b = [sb(f"a_rope_b{i}", [R, 2 * D]) for i in range(2)]
        qk = sb("a_qk", [R, 2, 2 * HEADS, COPIES * HD])
        high = [sb(f"a_high{i}", [P, 2, SEQ]) for i in range(2)]
        raw = sb("a_raw", [P, 2, SEQ])
        qT = sb("a_qT", [P, PAIRS, SEQ], F32R)
        k_own = sb("a_k_own", [P, HEADS, EV], F32R)
        v_own = [sb(f"a_v_own{i}", [R, 2, HEADS * DIAG], F32R) for i in range(2)]
        neg_max = [sb(f"a_neg_max{i}", [R, HEADS, 2]) for i in range(2)]
        denom = [sb(f"a_denom{i}", [R, HEADS, 2]) for i in range(2)]
        prob = [sb(f"a_prob{i}", [R, 2, SEQ]) for i in range(2)]
        probT_hi = [sb(f"a_probT_hi{i}", [R, 2, EV], F32R) for i in range(3)]
        probT_lo = [sb(f"a_probT_lo{i}", [R, 2, EV], F32R) for i in range(3)]
        rden = sb("a_rden", [R, G4, 2])
        rden_wide = sb("a_rden_wide", [R, 2, G4, SUB])
        rdenT = [sb(f"a_rdenT{i}", [P, SEQ]) for i in range(2)]
        oT = sb("a_oT", [P, NG, SEQ])
        h_rows = sb("a_h_rows", [R, 2, D])
        res = [sb(f"a_res{i}", [R, 2, D]) for i in range(2)]
        res2 = sb("a_res2", [R, 2, D])
        stats = sb("a_stats", [R, 2, 6])
        moments = sb("a_moments", [R, 2, 2])
        rstd = sb("a_rstd", [R, 2])
        minus_half = sb("a_minus_half", [R, 2])
        h1 = [sb(f"a_h1{i}", [R, 2, D]) for i in range(2)]

        score = [bank("a_score0"), bank("a_score1")]
        turned = [bank("a_turned0"), bank("a_turned1")]
        out_b = [bank("a_out0"), bank("a_out1")]
        fa, fb = bank("a_fa"), bank("a_fb")

        half_set = sem("a_half_set")
        consts_in, wp_in = sem("a_consts_in"), sem("a_wp_in")
        zero_set = sem("a_zero_set")
        scratch_set = sem("a_scratch_set")
        add_step = sem("a_add_step")
        add_ready, add_turned, cls_col = sem("a_add_ready"), sem("a_add_turned"), sem("a_cls_col")
        img_in = [sem("a_img_in0"), sem("a_img_in1")]
        tok_done = sem("a_tok_done")
        hT_ready, hT_high_ready, hT_split = sem("a_hT_ready"), sem("a_hT_high_ready"), sem("a_hT_split")
        qkv_split = sem("a_qkv_split")
        qk_done, rope_step, qk_ready = sem("a_qk_done"), sem("a_rope_step"), sem("a_qk_ready")
        v_done, v_high, v_ready = sem("a_v_done"), sem("a_v_high"), sem("a_v_ready")
        turn_qk, high_ready, raw_ready = sem("a_turn_qk"), sem("a_high_ready"), sem("a_raw_ready")
        q_ready, k_ready = sem("a_q_ready"), sem("a_k_ready")
        score_done, max_ready, prob_ready = sem("a_score_done"), sem("a_max_ready"), sem("a_prob_ready")
        turned_done, hi_ready, probT_ready, pv_done = (sem("a_turned_done"), sem("a_hi_ready"),
                                                       sem("a_probT_ready"), sem("a_pv_done"))
        rden_ready, wide_ready, rdenT_done, rdenT_ready = (sem("a_rden_ready"), sem("a_wide_ready"),
                                                           sem("a_rdenT_done"), sem("a_rdenT_ready"))
        oT_ready, proj_done = sem("a_oT_ready"), sem("a_proj_done")
        h_turned, h_rows_ready, res_ready = sem("a_h_turned"), sem("a_h_rows_ready"), sem("a_res_ready")
        ln_step, h1_ready = sem("a_ln_step"), sem("a_h1_ready")
        h1_out = [sem("a_h1_out0"), sem("a_h1_out1")]

        CONSTS = 18 * 16
        WP_DMAS = 2 * HEADS * 16
        IMG_DMAS = 2 * S.chans * 16

        x_rows = x.rearrange("b c (hp ph) w -> b c ph hp w", ph=PATCH)
        w_rows = tok_w.rearrange("(r g j) d -> g r j d", g=2, j=PJ)

        pool_passed, dve_passed = sem("a_pool_passed"), sem("a_dve_passed")
        block = ctx.enter_context(nc.Block())

        def images(eng, body):
            body(0, 0, 0, True, False)
            body(1, 0, 1, False, B == 2)
            if B > 4:
                with eng.Fori(1, B // 2 - 1) as k:
                    body(k * 2, k, 0, False, False)
                    body(k * 2 + 1, k, 1, False, False)
            if B > 2:
                k = B // 2 - 1
                body(2 * k, k, 0, False, False)
                body(2 * k + 1, k, 1, False, True)

        def beyond(n, ahead):
            return isinstance(n, int) and n + ahead >= B

        @block.sync
        def _(sp):
            for dst, src in ((ident[:], t_ident), (split[:], t_split),
                             (pos_rows[:, 0, :], pos[0:R, :]), (pos_rows[:, 1, :], pos[SEC:SEQ, :]),
                             (add_rows[:, 1, 0:D], tok_b.partition_broadcast(R)),
                             (add_rows[1:R, 0, 0:D], tok_b.partition_broadcast(R - 1)),
                             (add_rows[0:1, 0, 0:D], cls[0]),
                             (wt[0:KR, :, 0:D], w_rows[0]), (wt[KR:2 * KR, :, 0:D], w_rows[1]),
                             (wt[0:KR, :, D:W2], w_rows[0][:, :, P:D]), (wt[KR:2 * KR, :, D:W2], w_rows[1][:, :, P:D])):
                sp.dma_start(dst, src).then_inc(consts_in, 16)

            def load(n, i):
                for g in range(2):
                    for c in range(S.chans):
                        r = g * KR + c * PATCH
                        sp.dma_start(img[i][r:r + PATCH, :, 0:S.width - PJ * g],
                                     x_rows[n, c][:, :, PJ * g:S.width]).then_inc(img_in[i], 16)

            def store(n, i):
                sp.wait_ge(h1_ready, n + 1)
                sp.dma_start(hx[bass.ds(n * SEQ, R), 0:D], h1[i][:, 0, :]).then_inc(h1_out[i], 16)
                sp.dma_start(hx[bass.ds(n * SEQ + R, R - 1), 0:D], h1[i][1:R, 1, :]).then_inc(h1_out[i], 16)

            load(0, 0)
            load(1, 1)
            for h in range(HEADS):
                for part in range(2):
                    r = h % G4 * SUB + part * HD
                    sp.dma_start(wp[r:r + HD, h // G4, :], w_proj[h * HD:(h + 1) * HD, :]).then_inc(wp_in, 16)
            sp.wait_ge(wp_in, WP_DMAS)
            sp.dma_start(empty[:], t_empty).then_inc(scratch_set, 16)
            sp.wait_ge(scratch_set, 16)
            sp.dma_start(slot_token.rearrange("(p n) a -> p (n a)", p=P), empty[:]).then_inc(scratch_set, 16)
            sp.wait_ge(zero_set, 1)
            r, k = S.tokens, 2
            while r < S.all_rows:
                m = min(P, S.all_rows - r)
                sp.dma_start(hx[r:r + m, :], zeros[0:m, :]).then_inc(scratch_set, 16)
                r, k = r + m, k + 1
            sp.dma_start(acc[S.padded:S.padded + P, :], zeros[:, 0:D]).then_inc(scratch_set, 16)
            sp.dma_start(acc[S.padded + P:S.all_rows, :], zeros[0:CAP - P, 0:D]).then_inc(scratch_set, 16)
            sp.wait_ge(scratch_set, 16 * (k + 2))

            def body(n, k, odd, first, last):
                if not beyond(n, 2):
                    sp.wait_ge(tok_done, n + 1)
                    load(n + 2, odd)
                if not first:
                    store(n - 1, 1 - odd)

            images(sp, body)
            store(B - 1, (B - 1) % 2)
            for i in range(2):
                sp.wait_ge(h1_out[i], 32 * (B // 2))

        @block.gpsimd
        def _(pool):
            pool.memset(minus_half[:], -0.5).then_inc(half_set, 1)
            hold(pool, pool_passed, half_set, 1)
            hold(pool, pool_passed, consts_in, CONSTS)

            def rope_sum(m, group, t):
                hold(pool, pool_passed, rope_step, m * 4 + 4 - 2 * t)
                hold(pool, pool_passed, turn_qk, ROUNDS * m - ROUNDS + 2 * (group + 1))
                lo = group * G4
                a, b = (repeat(x.rearrange("p (s h d) -> p s h d", s=2, d=HD)[:, :, lo:lo + G4, :], 3, COPIES)
                        for x in (rope_a[t], rope_b[t]))
                out = qk[:, t, :, :].rearrange("p (s h) (c d) -> p s h c d", s=2, d=HD)[:, :, lo:lo + G4]
                for s in range(2):
                    pool.tensor_tensor(out[:, s], a[:, s], b[:, s], ALU.add).then_inc(qk_ready, 1)

            def rope_sums(m):
                for group in range(NG):
                    for t in (1, 0):
                        rope_sum(m, group, t)

            def stack_keys(m, group):
                hold(pool, pool_passed, raw_ready, NG * m + group + 1)
                hold(pool, pool_passed, score_done, (m - 1) * HEADS + G4 * (group + 1))
                if group == 0:
                    hold(pool, pool_passed, res_ready, m + 1)
                else:
                    hold(pool, pool_passed, k_ready, NG * m + group)
                for part in range(2):
                    rows = slice(part * P // 2, (part + 1) * P // 2)
                    h = group * G4 + part
                    op = pool.tensor_tensor(k_own[rows, h:h + 3:2, 0:SEQ], raw[rows], high[1][rows], ALU.subtract)
                op.then_inc(k_ready, 1)
                hold(pool, pool_passed, k_ready, NG * m + group + 1)

            def add_bias(m, i):
                hold(pool, pool_passed, h_rows_ready, m + 1)
                hold(pool, pool_passed, ln_step, (m - 2) * LN + 1)
                pool.tensor_tensor(res[i][:], h_rows[:], repeat(bproj[:], 1, 2), ALU.add).then_inc(res_ready, 1)

            def normalise(n, k_out, i):
                hold(pool, pool_passed, ln_step, n * LN + 4)
                pool.tensor_scalar(rstd[:], moments[:, :, 1], LN_EPS, None, ALU.add).then_inc(ln_step, 1)
                hold(pool, pool_passed, ln_step, n * LN + 5)
                pool.tensor_tensor(rstd[:], rstd[:], minus_half[:], ALU.pow).then_inc(ln_step, 1)
                hold(pool, pool_passed, ln_step, n * LN + 6)
                hold(pool, pool_passed, h1_out[i], k_out * 32)
                for t in range(2):
                    op = pool.tensor_scalar(h1[i][:, t, :], res2[:, t, :], moments[:, t, 0:1], rstd[:, t:t + 1],
                                            ALU.subtract, ALU.mult)
                op.then_inc(h1_ready, 1)

            def body(n, k, odd, first, last):
                stack_keys(n, 2)
                if not last:
                    rope_sums(n + 1)
                if not first:
                    normalise(n - 1, k - 1 + odd, 1 - odd)
                if not last:
                    add_bias(n + 1, 1 - odd)
                    stack_keys(n + 1, 0)
                    stack_keys(n + 1, 1)

            hold(pool, pool_passed, zero_set, 10)
            rope_sums(0)
            add_bias(0, 0)
            stack_keys(0, 0)
            stack_keys(0, 1)
            images(pool, body)
            normalise(B - 1, (B - 1) // 2, (B - 1) % 2)

        @block.tensor
        def _(pe):
            pe.wait_ge(consts_in, CONSTS)
            pe.wait_ge(add_ready, 1)
            for kh in range(2):
                for t in range(2):
                    mm = pe.transpose(fb[:, kh * SEQ + t * SEC:kh * SEQ + t * SEC + R],
                                      add_rows[:, t, kh * P:(kh + 1) * P], ident[0:R, 0:R])
            mm.then_inc(add_turned, 1)

            EMBED = [(f, j) for f in range(2) for j in range(PJ)]
            EMBED_CUTS = [0, 4, 7, 10, 13, 16]

            def embed(m, mk, i, lo, hi):
                if lo == 0:
                    pe.wait_ge(img_in[i], (mk + 1) * IMG_DMAS)
                    at_least(pe, h_rows_ready, m)
                for f, j in EMBED[lo:hi]:
                    mm = pe.matmul(fb[:, f * NP:(f + 1) * NP], wt[:, j, f * P:(f + 1) * P],
                                   img[i][:, :, j:j + PATCH * (GW - 1) + 1:PATCH], start=(j == 0), stop=(j == PJ - 1))
                if hi == len(EMBED):
                    mm.then_inc(tok_done, 1)

            def project_qk(m, t):
                pe.wait_ge(hT_split, 2 * (m + 1))
                if t == 0:
                    at_least(pe, raw_ready, NG * m)
                for n, (x, kt, part) in enumerate(PRODUCTS):
                    mm = pe.matmul((fa, fb)[t][0:R, 0:2 * D], hT_parts[:, x, t * SEC:t * SEC + R],
                                   wqkv[:, kt, part, 0:2 * D], start=(n == 0), stop=(n == len(PRODUCTS) - 1))
                mm.then_inc(qk_done, 1)

            def project_v(m):
                pe.wait_ge(rope_step, m * 4 + 2)
                for t in range(2):
                    for n, (x, kt, part) in enumerate(PRODUCTS):
                        mm = pe.matmul(fb[0:R, t * D:(t + 1) * D], hT_parts[:, x, t * SEC:t * SEC + R],
                                       wqkv[:, kt, part, 2 * D:3 * D], start=(n == 0), stop=(n == len(PRODUCTS) - 1))
                mm.then_inc(v_done, 1)

            def turn_h(m):
                pe.wait_ge(v_ready, m + 1)
                for t in range(2):
                    for kt, w in ((0, P), (1, D - P)):
                        mm = pe.transpose(fb[0:R, t * D + kt * P:t * D + kt * P + w],
                                          hT[0:w, kt, t * SEC:t * SEC + R], ident[0:w, 0:w])
                mm.then_inc(h_turned, 1)

            def turn(m, r):
                if r % 2 == 0:
                    pe.wait_ge(qk_ready, 4 * NG * m + 4 * (r // 2 + 1))
                if r == 0:
                    at_least(pe, ln_step, (m - 2) * LN + 1)
                elif r % 2 == 1:
                    pe.wait_ge(q_ready, NG * m + r // 2 + 1)
                else:
                    pe.wait_ge(raw_ready, NG * m + r // 2)
                for c in range(2):
                    h = r % 2 * HEADS + r // 2 * G4 + 2 * c
                    for t in range(2):
                        mm = pe.transpose(fa[:, c * SEQ + t * SEC:c * SEQ + t * SEC + R],
                                          qk[:, t, h:h + 2, :].rearrange("p h d -> p (h d)"), ident[0:R, 0:R])
                mm.then_inc(turn_qk, 1)

            def scores(n, h, g):
                if h % G4 == 0:
                    pe.wait_ge(q_ready, NG * n + h // G4 + 1)
                    pe.wait_ge(k_ready, NG * n + h // G4 + 1)
                at_least(pe, prob_ready, g - 1)
                for t in range(2):
                    mm = pe.matmul(score[h % 2][0:R, t * EV:(t + 1) * EV], qT[:, h // 2, t * SEC:t * SEC + R],
                                   k_own[:, h, :], start=True, stop=True)
                mm.then_inc(score_done, 1)

            def turn_probs(h, g):
                pe.wait_ge(prob_ready, g + 1)
                at_least(pe, probT_ready, g - 1)
                for kt in range(2):
                    for t in range(2):
                        mm = pe.transpose(turned[h % 2][0:R, kt * SEQ + t * SEC:kt * SEQ + t * SEC + R],
                                          prob[h % 2][:, t, kt * SEC:kt * SEC + R], ident[0:R, 0:R])
                mm.then_inc(turned_done, 1)

            def attend(n, i, h, g):
                pe.wait_ge(probT_ready, g + 1)
                group, j = h // G4, h % G4
                out = out_b[(i + group) % 2]
                if h == 0:
                    pe.wait_ge(v_ready, n + 1)
                if j == 0:
                    at_least(pe, oT_ready, NG * n + group - 1)
                last = 0
                for kt in range(2):
                    for part in (probT_hi, probT_lo):
                        last += 1
                        mm = pe.matmul(out[:, 0:EV], v_own[i][:, kt, h * DIAG - j * SUB:h * DIAG - j * SUB + P],
                                       part[h % 3][:, kt, :], start=(j == 0 and last == 1), stop=(j == G4 - 1 and last == 4))
                mm.then_inc(pv_done, 1)
                if j == G4 - 1:
                    pe.wait_ge(wide_ready, NG * n + group + 1)
                    for t in range(2):
                        mm = pe.transpose(out[:, DEN + t * SEC:DEN + t * SEC + R],
                                          rden_wide[:, t, :, :].rearrange("p h d -> p (h d)"), ident[0:R, 0:R])
                    mm.then_inc(rdenT_done, 1)

            def project_out(n, t):
                if t == 0:
                    if isinstance(n, int) and n == 0:
                        pe.wait_ge(wp_in, WP_DMAS)
                    pe.wait_ge(oT_ready, NG * (n + 1))
                    if not beyond(n, 2):
                        pe.wait_ge(rope_step, (n + 2) * 4 + 4)
                    elif n == B - 2:
                        pe.wait_ge(raw_ready, NG * B)
                    else:
                        pe.wait_ge(ln_step, (n - 1) * LN + 1)
                for group in range(NG):
                    mm = pe.matmul(fa[0:R, t * D:(t + 1) * D], oT[:, group, t * SEC:t * SEC + R], wp[:, group, :],
                                   start=(group == 0), stop=(group == NG - 1))
                if t == 1:
                    mm.then_inc(proj_done, 1)

            pe.wait_ge(cls_col, 1)
            pe.wait_ge(qkv_split, 2)
            embed(0, 0, 0, 0, len(EMBED))
            project_qk(0, 1)
            project_qk(0, 0)
            project_v(0)
            turn_h(0)
            embed(1, 0, 1, 0, len(EMBED))
            for r in range(ROUNDS - 1):
                turn(0, r)
            scores(0, 0, 0)
            scores(0, 1, 1)

            def body(n, k, odd, first, last):
                for h in range(HEADS):
                    g = n * HEADS + h
                    turn_probs(h, g)
                    if h + 2 < HEADS:
                        scores(n, h + 2, g + 2)
                    elif not last:
                        scores(n + 1, h + 2 - HEADS, g + 2)
                    if h >= 2:
                        attend(n, odd, h - 2, g - 2)
                    elif not first:
                        attend(n - 1, 1 - odd, h + HEADS - 2, g - 2)
                    if h in (1, 2) and not last:
                        project_qk(n + 1, 2 - h)
                    if h == 3 and not last:
                        project_v(n + 1)
                    if h in (4, 5) and not first:
                        project_out(n - 1, h - 4)
                    if h == 5 and not last:
                        turn_h(n + 1)
                    if 6 <= h < 11 and not beyond(n, 2):
                        embed(n + 2, k + 1, odd, EMBED_CUTS[h - 6], EMBED_CUTS[h - 5])
                    if 6 <= h < HEADS - 1 and not last:
                        turn(n + 1, h - 6)
                    if h == 0:
                        turn(n, ROUNDS - 1)

            images(pe, body)
            for h in (HEADS - 2, HEADS - 1):
                attend(B - 1, (B - 1) % 2, h, (B - 1) * HEADS + h)
            project_out(B - 1, 0)
            project_out(B - 1, 1)

        @block.scalar
        def _(act):
            for dst, src in ((raw_qkv[:, 0, :], w_qkv[0:P, :]), (raw_qkv[0:P // 2, 1, :], w_qkv[P:D, :]),
                             (raw_qkv[P // 2:P, 1, :], w_qkv[P:D, :]), (cos[:], t_cos), (sin[:], t_sin),
                             (vmask[:], t_vmask), (bproj[:], b_proj.partition_broadcast(R))):
                act.dma_start(dst, src).then_inc(consts_in, 16)
            act.wait_ge(consts_in, CONSTS)

            def high_parts(m, r):
                act.wait_ge(turn_qk, ROUNDS * m + r + 1)
                at_least(act, (q_ready, k_ready)[r % 2], NG * m + r // 2)
                act.activation(high[r % 2].bitcast(F32R).rearrange("p c s -> p (c s)"), fa[:, 0:2 * SEQ], ACT.Copy,
                               scale=split[:, 2 * (r % 2):2 * (r % 2) + 1]).then_inc(high_ready, 1)
                if r % 2 == 1:
                    act.activation(raw.rearrange("p c s -> p (c s)"), fa[:, 0:2 * SEQ], ACT.Copy,
                                   scale=split[:, 3:4]).then_inc(raw_ready, 1)

            def h_high(m):
                act.wait_ge(hT_ready, m + 1)
                at_least(act, v_done, m)
                act.activation(hT_parts[:, 0, :], hT[:, 0, :], ACT.Copy).then_inc(hT_high_ready, 1)
                act.activation(hT_high.bitcast(F32R)[:], hT[:, 1, :], ACT.Copy, scale=split[:, 4:5])\
                   .then_inc(hT_high_ready, 1)

            def values_high(m, i):
                act.wait_ge(v_done, m + 1)
                at_least(act, pv_done, (m - 1) * HEADS)
                if isinstance(m, int) and m < 2:
                    act.wait_ge(zero_set, 3)
                for t in range(2):
                    own = v_own[i][:, t, :].rearrange("p (h w) -> p h w", w=DIAG)
                    act.activation(own[:, :, 0:HD], fb[0:R, t * D:(t + 1) * D].rearrange("p (h d) -> p h d", d=HD),
                                   ACT.Copy, scale=vmask[:, t:t + 1]).then_inc(v_high, 1)

            def copy_h(m):
                act.wait_ge(h_turned, m + 1)
                at_least(act, res_ready, m)
                act.activation(h_rows.rearrange("p t d -> p (t d)"), fb[0:R, 0:2 * D], ACT.Copy)\
                   .then_inc(h_rows_ready, 1)

            def softmax(i, h, g):
                act.wait_ge(max_ready, g + 1)
                at_least(act, turned_done, g - 1)
                for t in range(2):
                    op = act.activation(prob[h % 2][:, t, :], score[h % 2][0:R, t * EV:t * EV + SEQ], ACT.Exp,
                                        bias=neg_max[i][:, h, t:t + 1], accum_out=denom[i][:, h, t:t + 1])
                op.then_inc(prob_ready, 1)

            def probs_high(h, g):
                act.wait_ge(turned_done, g + 1)
                at_least(act, pv_done, g - 2)
                act.activation(probT_hi[h % 3][:, :, 0:SEQ], turned[h % 2][0:R, 0:2 * SEQ].rearrange("p (k s) -> p k s", k=2),
                               ACT.Copy).then_inc(hi_ready, 1)

            def denom_copy(n, i, group):
                act.wait_ge(rdenT_done, NG * n + group + 1)
                at_least(act, oT_ready, NG * n + group - 1)
                act.activation(rdenT[group % 2][:], out_b[(i + group) % 2][:, DEN:DEN + SEQ], ACT.Copy)\
                   .then_inc(rdenT_ready, 1)

            h_high(0)
            values_high(0, 0)
            copy_h(0)
            for r in range(ROUNDS - 1):
                high_parts(0, r)
            softmax(0, 0, 0)
            softmax(0, 1, 1)
            h_high(1)

            def body(n, k, odd, first, last):
                for h in range(HEADS):
                    g = n * HEADS + h
                    if h >= 7 and not last:
                        high_parts(n + 1, h - 7)
                    if h == 2 and not first:
                        denom_copy(n - 1, 1 - odd, 2)
                    if h == 6:
                        denom_copy(n, odd, 0)
                    if h == 10:
                        denom_copy(n, odd, 1)
                    if h == 4 and not last:
                        values_high(n + 1, 1 - odd)
                    if h == 6 and not last:
                        copy_h(n + 1)
                    probs_high(h, g)
                    if h == 0:
                        high_parts(n, ROUNDS - 1)
                    if h + 2 < HEADS:
                        softmax(odd, h + 2, g + 2)
                    elif not last:
                        softmax(1 - odd, h + 2 - HEADS, g + 2)
                    if h == HEADS - 1 and not beyond(n, 2):
                        h_high(n + 2)

            images(act, body)
            denom_copy(B - 1, (B - 1) % 2, 2)

        @block.vector
        def _(dve):
            dve.memset(zeros[:], 0.0).then_inc(zero_set, 1)
            for i in range(2):
                dve.memset(v_own[i].bitcast(F32).rearrange("p a b -> p (a b)"), 0.0).then_inc(zero_set, 1)
            for i in range(3):
                dve.memset(probT_hi[i].bitcast(F32)[:, :, SEQ:EV], 0.0).then_inc(zero_set, 1)
                dve.memset(probT_lo[i].bitcast(F32)[:, :, SEQ:EV], 0.0).then_inc(zero_set, 1)
            dve.memset(k_own.bitcast(F32).rearrange("p h s -> p (h s)"), 0.0).then_inc(zero_set, 1)
            dve.wait_ge(consts_in, CONSTS)
            dve.tensor_tensor(add_rows[:, :, 0:D], add_rows[:, :, 0:D], pos_rows[:], ALU.add).then_inc(add_step, 1)
            dve.wait_ge(add_step, 1)
            dve.tensor_copy(add_rows[:, :, D:W2], add_rows[:, :, P:D]).then_inc(add_ready, 1)
            dve.tensor_copy(wqkv[:, :, 0, :], raw_qkv[:]).then_inc(qkv_split, 1)
            dve.wait_ge(add_turned, 1)
            dve.tensor_copy(addT.rearrange("p k s -> p (k s)"), fb[:, 0:2 * SEQ]).then_inc(add_ready, 1)
            dve.wait_ge(qkv_split, 1)
            dve.tensor_tensor(wqkv[:, :, 1, :], raw_qkv[:], wqkv[:, :, 0, :].bitcast(F32), ALU.subtract)\
               .then_inc(qkv_split, 1)
            dve.wait_ge(add_ready, 2)
            dve.tensor_copy(hT[:, :, 0:1], addT[:, :, 0:1]).then_inc(cls_col, 1)
            dve.wait_ge(zero_set, 10)

            def add_position(m):
                dve.wait_ge(tok_done, m + 1)
                at_least(dve, h_turned, m)
                at_least(dve, hT_split, 2 * m)
                dve.tensor_tensor(hT[:, :, 1:SEQ], fb[:, 0:2 * NP].rearrange("p (k s) -> p k s", k=2),
                                  addT[:, :, 1:SEQ], ALU.add).then_inc(hT_ready, 1)

            def h_low(m):
                dve.wait_ge(hT_high_ready, 2 * m + 1)
                dve.tensor_tensor(hT_parts[:, 2, :], hT[:, 0, :], hT_parts[:, 0, :].bitcast(F32), ALU.subtract)\
                   .then_inc(hT_split, 1)
                dve.wait_ge(hT_high_ready, 2 * m + 2)
                dve.scalar_tensor_tensor(out=hT_parts[:, 1, :], in0=hT[:, 1, :], scalar=split[:, 5:6], in1=hT_high[:],
                                         op0=ALU.mult, op1=ALU.subtract).then_inc(hT_split, 1)

            def rope(m, t):
                dve.wait_ge(qk_done, 2 * m + 2 - t)
                at_least(dve, qk_ready, 4 * NG * m)
                b = (fa, fb)[t]
                src = b[0:R, 0:2 * D]
                heads = src.rearrange("p (h d) -> p h d", d=HD)
                dims = [list(d) for d in src.ap]
                swap = bass.AP(src.tensor, src.offset + HD // 2, [dims[0], [HD, 2 * HEADS], [-(HD // 2), 2], [1, HD // 2]])
                c = repeat(cos[:, t, :], 1, 2 * HEADS)
                s = repeat(sin[:, t, :].rearrange("p (a b) -> p a b", a=2), 1, 2 * HEADS)
                dve.tensor_tensor(rope_a[t].rearrange("p (h d) -> p h d", d=HD), heads, c, ALU.mult).then_inc(rope_step, 1)
                dve.tensor_tensor(rope_b[t].rearrange("p (h a b) -> p h a b", a=2, b=HD // 2), swap, s, ALU.mult)\
                   .then_inc(rope_step, 1)

            def values_low(m, i):
                dve.wait_ge(v_high, 2 * m + 2)
                for t in range(2):
                    own = v_own[i][:, t, :].rearrange("p (h w) -> p h w", w=DIAG)
                    src = fb[0:R, t * D:(t + 1) * D].rearrange("p (h d) -> p h d", d=HD)
                    op = dve.scalar_tensor_tensor(out=own[:, :, HD:SUB], in0=src, scalar=vmask[:, t:t + 1],
                                                  in1=own[:, :, 0:HD].bitcast(F32), op0=ALU.mult, op1=ALU.subtract)
                op.then_inc(v_ready, 1)

            def stack_queries(m, group):
                dve.wait_ge(high_ready, ROUNDS * m + 2 * group + 1)
                at_least(dve, score_done, (m - 1) * HEADS + G4 * (group + 1))
                dve.scalar_tensor_tensor(out=qT[:, 2 * group:2 * group + 2, :].rearrange("p c s -> p (c s)"),
                                         in0=fa[:, 0:2 * SEQ], scalar=split[:, 1:2],
                                         in1=high[0].rearrange("p c s -> p (c s)"),
                                         op0=ALU.mult, op1=ALU.subtract).then_inc(q_ready, 1)

            def maxima(i, h, g):
                dve.wait_ge(score_done, g + 1)
                dve.tensor_reduce(neg_max[i][:, h, :],
                                  score[h % 2][0:R, 0:2 * EV].rearrange("p (t s) -> p t s", t=2)[:, :, 0:SEQ],
                                  AX_X, ALU.max, negate=True).then_inc(max_ready, 1)

            def probs_low(h, g):
                dve.wait_ge(hi_ready, g + 1)
                at_least(dve, pv_done, g - 2)
                dve.tensor_tensor(probT_lo[h % 3][:, :, 0:SEQ], turned[h % 2][0:R, 0:2 * SEQ].rearrange("p (k s) -> p k s", k=2),
                                  probT_hi[h % 3].bitcast(F32)[:, :, 0:SEQ], ALU.subtract).then_inc(probT_ready, 1)

            def denoms(n, i, group):
                c = NG * n + group
                dve.wait_ge(prob_ready, n * HEADS + (group + 1) * G4)
                dve.reciprocal(rden.rearrange("p h t -> p (h t)"),
                               denom[i][:, group * G4:(group + 1) * G4, :].rearrange("p h t -> p (h t)"))\
                   .then_inc(rden_ready, 1)
                dve.wait_ge(rden_ready, c + 1)
                at_least(dve, rdenT_done, c)
                dve.tensor_copy(rden_wide[:], repeat(rden.rearrange("p h t -> p t h"), 3, SUB)).then_inc(wide_ready, 1)

            def normalise_heads(n, i, group):
                c = NG * n + group
                dve.wait_ge(rdenT_ready, c + 1)
                if group == 0:
                    at_least(dve, proj_done, n)
                dve.tensor_tensor(oT[:, group, :], out_b[(i + group) % 2][:, 0:SEQ], rdenT[group % 2][:], ALU.mult)\
                   .then_inc(oT_ready, 1)

            def measure(n, i):
                dve.wait_ge(proj_done, n + 1)
                dve.wait_ge(res_ready, n + 1)
                at_least(dve, h1_ready, n)
                dve.tensor_tensor(res2[:], fa[0:R, 0:2 * D].rearrange("p (t d) -> p t d", t=2), res[i][:], ALU.add)\
                   .then_inc(ln_step, 1)
                dve.wait_ge(ln_step, n * LN + 1)
                for t in range(2):
                    op = dve.bn_stats(stats[:, t, :], res2[:, t, :])
                op.then_inc(ln_step, 1)
                hold(dve, dve_passed, ln_step, n * LN + 2)
                for t in range(2):
                    dve.bn_aggr(moments[:, t, :], stats[:, t, :]).then_inc(ln_step, 1)

            add_position(0)
            h_low(0)
            rope(0, 1)
            rope(0, 0)
            values_low(0, 0)
            for group in range(NG):
                stack_queries(0, group)
            add_position(1)
            maxima(0, 0, 0)
            maxima(0, 1, 1)

            def body(n, k, odd, first, last):
                for h in range(HEADS):
                    g = n * HEADS + h
                    if h == 0 and not last:
                        h_low(n + 1)
                    if h + 2 < HEADS:
                        maxima(odd, h + 2, g + 2)
                    elif not last:
                        maxima(1 - odd, h + 2 - HEADS, g + 2)
                    if h == 6 and not first:
                        measure(n - 1, 1 - odd)
                    if h in (2, 3) and not last:
                        rope(n + 1, 3 - h)
                    if h in (7, 9, 11) and not last:
                        stack_queries(n + 1, (h - 7) // 2)
                    if h == 11 and not beyond(n, 2):
                        add_position(n + 2)
                    probs_low(h, g)
                    if h == 2 and not first:
                        normalise_heads(n - 1, 1 - odd, 2)
                    if h == 6:
                        normalise_heads(n, odd, 0)
                    if h == 10:
                        normalise_heads(n, odd, 1)
                    if h == 4 and not last:
                        values_low(n + 1, 1 - odd)
                    if h % G4 == G4 - 1:
                        denoms(n, odd, h // G4)

            images(dve, body)
            normalise_heads(B - 1, (B - 1) % 2, 2)
            measure(B - 1, (B - 1) % 2)


def tables(S):
    inv_freq = 1.0 / ROPE_THETA ** (np.arange(0, HD, 2, dtype=np.float64) / HD)
    freqs = np.outer(np.arange(S.seq, dtype=np.float64), inv_freq)
    cos = np.cos(np.concatenate([freqs, freqs], axis=-1)).astype(np.float32)
    sin = np.sin(np.concatenate([-freqs, freqs], axis=-1)).astype(np.float32)
    tiles = [slice(0, S.rows), slice(S.second, S.seq)]
    low_q, low_k = (np.tile(np.repeat(np.array(x, np.float32), HD), P // (4 * HD)) for x in ((0, 0, 1, 1), (0, 1, 0, 1)))
    scale = HD ** -0.5
    low_x = np.repeat(np.array([0, 1], np.float32), P // 2)
    vmask = np.ones((S.rows, 2), np.float32)
    vmask[0, 1] = 0.0
    before = np.triu(np.ones((P, P), np.float32), 1)
    first_slot = np.arange(S.experts, dtype=np.float32) * CAP
    return {
        "ident": np.eye(P, dtype=np.float32),
        "cos": np.stack([cos[t] for t in tiles], axis=1),
        "sin": np.stack([sin[t] for t in tiles], axis=1),
        "split": np.stack([scale * (2 * low_q - 1), scale * low_q, 2 * low_k - 1, low_k, 2 * low_x - 1, low_x],
                          axis=1).astype(np.float32),
        "split_x": np.stack([2 * low_x - 1, low_x], axis=1).astype(np.float32),
        "vmask": vmask,
        "before": before,
        "slot_base": np.tile(BIG - first_slot, (P, 1)).astype(np.float32),
        "slot_limit": np.tile(BIG - first_slot - CAP, (P, 1)).astype(np.float32),
        "token_id": (np.arange(CHUNK // P)[None, :] * P + np.arange(P)[:, None]).astype(np.float32),
        "empty": (S.padded + np.arange(S.slots) % CAP).astype(np.int32).reshape(P, -1),
    }


def routing_phase(nc, S, wg, e_bias, wsg, wsu, wsd, t_ident, t_split, t_before, t_base, t_limit, t_token, hx, acc, slot_token):
    from contextlib import ExitStack

    HALF, D, E, NC, FT, SFF = S.half, S.dim, S.experts, S.chunks, S.ff_tile, S.sff
    T = CHUNK // P
    STEPS = 28

    with ExitStack() as ctx:
        def sb(name, shape, dt=F32):
            return ctx.enter_context(nc.sbuf_tensor(name, shape, dt))

        def bank(name):
            return ctx.enter_context(nc.psum_tensor(name, [P, 512], F32))

        def sem(name):
            return ctx.enter_context(nc.semaphore(name))

        ident = sb("b_ident", [P, P])
        before_f = sb("b_before_f", [P, P])
        before = sb("b_before", [P, P], BF16)
        ones = sb("b_ones", [P, P], BF16)
        base = sb("b_base", [P, E])
        limit = sb("b_limit", [P, E])
        bias = sb("b_bias", [P, E])
        split = sb("b_split", [P, 2])
        wg_rows = sb("b_wg_rows", [E, S.wide])
        raw = [sb("b_raw_gate", [P, 2, E]), sb("b_raw_g", [P, 2, S.shared]), sb("b_raw_u", [P, 2, S.shared])]
        wgT = sb("b_wgT", [P, 2, 2, E], F32R)
        w_g = sb("b_w_g", [P, 2, 2, S.shared], F32R)
        w_u = sb("b_w_u", [P, 2, 2, S.shared], F32R)
        w_d = sb("b_w_d", [FT, SFF, D])
        token_f = [sb(f"b_token_f{i}", [P, T]) for i in range(2)]
        token_i = [sb(f"b_token_i{i}", [P, T], I32) for i in range(2)]
        rows = [sb(f"b_rows{i}", [P, T, S.wide]) for i in range(2)]
        xT = sb("b_xT", [P, 3, CHUNK], F32R)
        high = sb("b_high", [P, CHUNK])
        sig = sb("b_sig", [P, T, E])
        choice = sb("b_choice", [P, T, E + 2])
        top = sb("b_top", [P, T, 8])
        replaced = sb("b_replaced", [P, T, E + 2])
        mask = sb("b_mask", [P, T, E], BF16)
        place = sb("b_place", [P, T, E])
        place_m = sb("b_place_m", [P, T, E])
        in_cap = sb("b_in_cap", [P, T, E])
        place_v = sb("b_place_v", [P, T, E])
        slots8 = sb("b_slots8", [P, T, 8])
        slot_i = [sb(f"b_slot_i{i}", [P, T, 8], I32) for i in range(2)]
        wsel = sb("b_wsel", [P, T, E])
        wsum = sb("b_wsum", [P, T])
        wden = sb("b_wden", [P, T])
        winv = sb("b_winv", [P, T])
        weight = [sb(f"b_weight{i}", [P, T, E]) for i in range(2)]
        silu_g = [sb(f"b_silu{i}", [FT, CHUNK]) for i in range(2)]
        inter = sb("b_inter", [FT, SFF, CHUNK])
        total = [sb(f"b_total{i}", [P, T, D]) for i in range(2)]

        t0, t1, gate_b, down_b = bank("b_t0"), bank("b_t1"), bank("b_gate"), bank("b_down")
        g_b = [bank("b_g0"), bank("b_g1")]
        u_b = [bank("b_u0"), bank("b_u1")]

        gate_in, up_in, consts_in, setup = sem("b_gate_in"), sem("b_up_in"), sem("b_consts_in"), sem("b_setup")
        w_split, before_ready = sem("b_w_split"), sem("b_before_ready")
        wg_turned, wgT_ready = sem("b_wg_turned"), sem("b_wgT_ready")
        rows_in = [sem("b_rows_in0"), sem("b_rows_in1")]
        x_turned, xT0_ready, xT1_ready = sem("b_x_turned"), sem("b_xT0_ready"), sem("b_xT1_ready")
        gate_done, sig_ready = sem("b_gate_done"), sem("b_sig_ready")
        route_step, mask_ready, prefix_done = sem("b_route_step"), sem("b_mask_ready"), sem("b_prefix_done")
        slots_ready, weight_ready = sem("b_slots_ready"), sem("b_weight_ready")
        up_done, silu_ready, inter_ready = sem("b_up_done"), sem("b_silu_ready"), sem("b_inter_ready")
        down_done, total_ready = sem("b_down_done"), sem("b_total_ready")
        weight_out = [sem("b_weight_out0"), sem("b_weight_out1")]
        total_out = [sem("b_total_out0"), sem("b_total_out1")]
        scattered = [sem("b_scattered0"), sem("b_scattered1")]
        token_step = sem("b_token_step")

        SCATTERS = T * TOP_K * 16
        CONSTS = 8 * 16

        pool_passed, dve_passed = sem("b_pool_passed"), sem("b_dve_passed")
        block = ctx.enter_context(nc.Block())

        def chunks(eng, body):
            body(0, 0, 0, True, NC == 1)
            if NC == 1:
                return
            body(1, 0, 1, False, NC == 2)
            full = (NC - 3) // 2
            if full > 0:
                with eng.Fori(1, 1 + full) as k:
                    body(k * 2, k, 0, False, False)
                    body(k * 2 + 1, k, 1, False, False)
            for c in range(2 + 2 * max(full, 0), NC):
                body(c, c // 2, c % 2, False, c == NC - 1)

        def tile_rows(c, lo, width, handle):
            v = handle[bass.ds(c * CHUNK, CHUNK), lo:lo + width]
            return v.rearrange("(t p) d -> p t d", p=P)

        @block.sync
        def _(sp):
            for dst, src in ((wg_rows[:, 0:D], wg), (wg_rows[:, D:S.wide], wg[:, P:D]), (ident[:], t_ident)):
                sp.dma_start(dst, src).then_inc(gate_in, 16)

            def load(c, i):
                sp.dma_start(rows[i][:, :, 0:D], tile_rows(c, 0, D, hx)).then_inc(rows_in[i], 16)
                sp.dma_start(rows[i][:, :, D:S.wide], tile_rows(c, P, S.third, hx)).then_inc(rows_in[i], 16)

            load(0, 0)
            for dst, src in ((split[:], t_split), (bias[:], e_bias.partition_broadcast(P)), (before_f[:], t_before),
                             (base[:], t_base), (limit[:], t_limit),
                             (token_f[0][:], t_token), (token_f[1][:], t_token)):
                sp.dma_start(dst, src).then_inc(consts_in, 16)
            if NC > 1:
                load(1, 1)
            sp.dma_start(w_d[:], wsd.rearrange("(j p) n -> p j n", p=FT)).then_inc(consts_in, 16)

            def body(c, k, odd, first, last):
                sp.wait_ge(weight_ready, c + 1)
                sp.dma_start(tile_rows(c, D, E, hx), weight[odd][:]).then_inc(weight_out[odd], 16)
                sp.wait_ge(total_ready, 2 * (c + 1))
                sp.dma_start(tile_rows(c, 0, D, acc), total[odd][:]).then_inc(total_out[odd], 16)
                if not (isinstance(c, int) and c + 2 >= NC):
                    load(c + 2, odd)

            chunks(sp, body)
            for i in range(2):
                n = (NC + 1 - i) // 2
                if n:
                    sp.wait_ge(weight_out[i], 16 * n)
                    sp.wait_ge(total_out[i], 16 * n)
                    sp.wait_ge(scattered[i], SCATTERS * n)

        @block.gpsimd
        def _(pool):
            pool.memset(ones[:], 1.0).then_inc(setup, 1)
            hold(pool, pool_passed, consts_in, CONSTS)
            pool.tensor_scalar(token_f[1][:], token_f[1][:], float(CHUNK), None, ALU.add).then_inc(token_step, 1)

            def body(c, k, odd, first, last):
                hold(pool, pool_passed, token_step, 2 * c + 1 if not first else 1)
                hold(pool, pool_passed, scattered[odd], k * SCATTERS)
                pool.tensor_copy(token_i[odd][:], token_f[odd][:]).then_inc(token_step, 1)
                hold(pool, pool_passed, token_step, 2 * c + 2)
                pool.tensor_scalar(token_f[odd][:], token_f[odd][:], float(2 * CHUNK), None, ALU.add)\
                    .then_inc(token_step, 1)
                hold(pool, pool_passed, slots_ready, c + 1)
                for t in range(T):
                    for j in range(TOP_K):
                        pool.indirect_dma_start(
                            slot_token, bass.IndirectOffsetOnAxis(ap=slot_i[odd][:, t, j:j + 1], axis=0),
                            token_i[odd][:, t:t + 1], None, bounds_check=S.slots - 1, oob_is_err=False,
                        ).then_inc(scattered[odd], 16)

            chunks(pool, body)

        @block.tensor
        def _(pe):
            pe.wait_ge(gate_in, 48)
            for kh in range(2):
                mm = pe.transpose(gate_b[:, kh * P:kh * P + E], wg_rows[:, kh * P:(kh + 1) * P], ident[0:E, 0:E])
            mm.then_inc(wg_turned, 1)
            pe.wait_ge(setup, 2)

            def turn(c, k, i):
                pe.wait_ge(rows_in[i], (k + 1) * 32)
                at_least(pe, route_step, (c - 1) * STEPS + 12)
                for kh in range(2):
                    for t in range(T):
                        mm = pe.transpose((t0, t1)[kh][:, t * P:(t + 1) * P], rows[i][:, t, kh * P:(kh + 1) * P],
                                          ident[:])
                mm.then_inc(x_turned, 1)

            def gate(c):
                if isinstance(c, int) and c == 0:
                    pe.wait_ge(wgT_ready, 3)
                pe.wait_ge(xT1_ready, 2 * (c + 1))
                at_least(pe, sig_ready, c)
                for t in range(T):
                    for n, (x, k, part) in enumerate(PRODUCTS):
                        mm = pe.matmul(gate_b[:, t * E:(t + 1) * E], xT[:, x, t * P:(t + 1) * P], wgT[:, k, part, :],
                                       start=(n == 0), stop=(n == len(PRODUCTS) - 1))
                mm.then_inc(gate_done, 1)

            def up(c, j):
                at_least(pe, inter_ready, c * SFF + j - 1)
                for w, b in ((w_g, g_b), (w_u, u_b)):
                    for n, (x, k, part) in enumerate(PRODUCTS):
                        mm = pe.matmul(b[j % 2][0:FT, :], w[:, k, part, j * FT:(j + 1) * FT], xT[:, x, :],
                                       start=(n == 0), stop=(n == len(PRODUCTS) - 1))
                mm.then_inc(up_done, 1)

            def prefix(c):
                pe.wait_ge(mask_ready, c + 1)
                for t in range(T):
                    for u in range(t + 1):
                        pe.matmul(t0[:, t * E:(t + 1) * E], before[:] if u == t else ones[:], mask[:, u, :],
                                  start=(u == 0), stop=(u == t))
                for t in range(T):
                    mm = pe.matmul(t1[:, 0:E], ones[:], mask[:, t, :], start=(t == 0), stop=(t == T - 1))
                mm.then_inc(prefix_done, 1)

            def down(c, q):
                at_least(pe, total_ready, 2 * c + q)
                for t in range(2):
                    for j in range(SFF):
                        if q == 0 and t == 0:
                            pe.wait_ge(inter_ready, c * SFF + j + 1)
                        s = (2 * q + t) * P
                        mm = pe.matmul(down_b[:, t * D:(t + 1) * D], inter[:, j, s:s + P], w_d[:, j, :],
                                       start=(j == 0), stop=(j == SFF - 1))
                mm.then_inc(down_done, 1)

            turn(0, 0, 0)
            gate(0)
            pe.wait_ge(w_split, 4)
            pe.wait_ge(consts_in, CONSTS)

            def body(c, k, odd, first, last):
                for j in range(SFF):
                    up(c, j)
                    if j == 1:
                        prefix(c)
                if not last:
                    turn(c + 1, k + odd, 1 - odd)
                down(c, 0)
                if not last:
                    gate(c + 1)
                down(c, 1)

            chunks(pe, body)

        @block.scalar
        def _(act):
            for w, src in ((1, wsg), (2, wsu)):
                for dst, rows_in in ((raw[w][:, 0, :], src[0:P, :]), (raw[w][0:P // 2, 1, :], src[P:D, :]),
                                     (raw[w][P // 2:P, 1, :], src[P:D, :])):
                    act.dma_start(dst, rows_in).then_inc(up_in, 16)
            act.wait_ge(consts_in, CONSTS)

            def copy_x(c):
                act.wait_ge(x_turned, c + 1)
                act.activation(xT[:, 0, :], t0[:], ACT.Copy).then_inc(xT0_ready, 1)
                at_least(act, xT1_ready, 2 * c)
                act.activation(high.bitcast(F32R)[:], t1[:], ACT.Copy, scale=split[:, 0:1]).then_inc(xT0_ready, 1)

            def sigmoid(c):
                act.wait_ge(gate_done, c + 1)
                at_least(act, weight_ready, c)
                act.activation(sig.rearrange("p t e -> p (t e)"), gate_b[:, 0:T * E], ACT.Sigmoid).then_inc(sig_ready, 1)

            def silu(c, j):
                act.wait_ge(up_done, c * SFF + j + 1)
                at_least(act, inter_ready, c * SFF + j - 1)
                act.activation(silu_g[j % 2][:], g_b[j % 2][0:FT, :], ACT.Silu).then_inc(silu_ready, 1)

            copy_x(0)
            act.wait_ge(up_in, 96)
            for w, src in ((w_g, raw[1]), (w_u, raw[2])):
                act.activation(w[:, :, 0, :], src[:], ACT.Copy).then_inc(w_split, 1)
            sigmoid(0)

            def body(c, k, odd, first, last):
                for j in range(SFF):
                    silu(c, j)
                if not last:
                    copy_x(c + 1)
                    sigmoid(c + 1)

            chunks(act, body)

        @block.vector
        def _(dve):
            dve.memset(choice[:, :, E:E + 2], SENTINEL).then_inc(setup, 1)
            dve.wait_ge(wg_turned, 1)
            dve.tensor_copy(raw[0][:], gate_b[:, 0:2 * P].rearrange("p (k e) -> p k e", k=2)[:, :, 0:E])\
               .then_inc(wgT_ready, 1)
            dve.wait_ge(wgT_ready, 1)
            dve.tensor_copy(wgT[:, :, 0, :], raw[0][:]).then_inc(wgT_ready, 1)
            dve.wait_ge(wgT_ready, 2)
            dve.tensor_tensor(wgT[:, :, 1, :], raw[0][:], wgT[:, :, 0, :].bitcast(F32), ALU.subtract)\
               .then_inc(wgT_ready, 1)
            dve.wait_ge(consts_in, CONSTS)
            dve.tensor_copy(before[:], before_f[:]).then_inc(before_ready, 1)

            def copy_x(c):
                dve.wait_ge(xT0_ready, 2 * c + 1)
                dve.tensor_tensor(xT[:, 2, :], t0[:], xT[:, 0, :].bitcast(F32), ALU.subtract).then_inc(xT1_ready, 1)
                dve.wait_ge(xT0_ready, 2 * c + 2)
                dve.scalar_tensor_tensor(out=xT[:, 1, :], in0=t1[:], scalar=split[:, 1:2], in1=high[:], op0=ALU.mult,
                                         op1=ALU.subtract).then_inc(xT1_ready, 1)

            def choose(c):
                z = c * STEPS
                dve.wait_ge(sig_ready, c + 1)
                dve.tensor_tensor(choice[:, :, 0:E], sig[:], repeat(bias[:], 1, T), ALU.add).then_inc(route_step, 1)
                hold(dve, dve_passed, route_step, z + 1)
                for t in range(T):
                    dve.max(top[:, t, :], choice[:, t, 0:E]).then_inc(route_step, 1)
                dve.wait_ge(route_step, z + 5)
                dve.memset(top[:, :, TOP_K:8], SENTINEL).then_inc(route_step, 1)
                hold(dve, dve_passed, route_step, z + 6)
                for t in range(T):
                    dve.match_replace(replaced[:, t, :], top[:, t, :], choice[:, t, :], TAKEN).then_inc(route_step, 1)
                dve.wait_ge(route_step, z + 10)
                at_least(dve, prefix_done, c)
                dve.tensor_scalar(mask[:], replaced[:, :, 0:E], TAKEN / 2, None, ALU.is_le).then_inc(mask_ready, 1)

            def queue_places(c):
                z = c * STEPS
                dve.wait_ge(prefix_done, c + 1)
                dve.tensor_tensor(place[:], repeat(base[:], 1, T), t0[:, 0:T * E].rearrange("p (t e) -> p t e", t=T),
                                  ALU.subtract).then_inc(route_step, 1)
                dve.wait_ge(route_step, z + 11)
                dve.tensor_tensor(base[:], base[:], t1[:, 0:E], ALU.subtract).then_inc(route_step, 1)
                dve.wait_ge(mask_ready, c + 1)
                dve.tensor_tensor(place_m[:], place[:], mask[:], ALU.mult).then_inc(route_step, 1)

            def drop_full(c):
                z = c * STEPS
                dve.wait_ge(route_step, z + 13)
                dve.tensor_tensor(in_cap[:], place_m[:], repeat(limit[:], 1, T), ALU.is_gt).then_inc(route_step, 1)
                dve.wait_ge(route_step, z + 14)
                dve.tensor_tensor(place_v[:], place_m[:], in_cap[:], ALU.mult).then_inc(route_step, 1)

            def six_slots(c, k, i):
                z = c * STEPS
                hold(dve, dve_passed, route_step, z + 15)
                for t in range(T):
                    dve.max(slots8[:, t, :], place_v[:, t, :]).then_inc(route_step, 1)
                dve.wait_ge(route_step, z + 19)
                at_least(dve, scattered[i], k * SCATTERS)
                dve.tensor_scalar(slot_i[i][:], slots8[:], -1.0, BIG, ALU.mult, ALU.add).then_inc(slots_ready, 1)

            def weights(c, k, i):
                z = c * STEPS
                for t in range(T):
                    dve.tensor_tensor_reduce(wsel[:, t, :], sig[:, t, :], mask[:, t, :], 1.0, 0.0, ALU.mult, ALU.add,
                                             wsum[:, t:t + 1]).then_inc(route_step, 1)
                dve.wait_ge(route_step, z + 23)
                dve.tensor_scalar(wden[:], wsum[:], 1e-20, None, ALU.add).then_inc(route_step, 1)
                dve.wait_ge(route_step, z + 24)
                dve.reciprocal(winv[:], wden[:]).then_inc(route_step, 1)
                dve.wait_ge(route_step, z + 25)
                at_least(dve, weight_out[i], k * 16)
                for t in range(T):
                    op = dve.tensor_scalar(weight[i][:, t, :], wsel[:, t, :], winv[:, t:t + 1], ROUTE_SCALE,
                                           ALU.mult, ALU.mult)
                    op.then_inc(weight_ready if t == T - 1 else route_step, 1)

            def gated(c, j):
                dve.wait_ge(silu_ready, c * SFF + j + 1)
                dve.tensor_tensor(inter[:, j, :], silu_g[j % 2][:], u_b[j % 2][0:FT, :], ALU.mult).then_inc(inter_ready, 1)

            def add_shared(c, k, i, q):
                if q == 0:
                    at_least(dve, total_out[i], k * 16)
                dve.wait_ge(down_done, 2 * c + q + 1)
                dve.tensor_tensor(total[i][:, 2 * q:2 * q + 2, :], down_b[:, 0:2 * D].rearrange("p (t d) -> p t d", t=2),
                                  rows[i][:, 2 * q:2 * q + 2, 0:D], ALU.add).then_inc(total_ready, 1)

            dve.wait_ge(setup, 2)
            copy_x(0)
            for w, (parts, src) in enumerate(((w_g, raw[1]), (w_u, raw[2]))):
                dve.wait_ge(w_split, 2)
                dve.tensor_tensor(parts[:, :, 1, :], src[:], parts[:, :, 0, :].bitcast(F32), ALU.subtract)\
                   .then_inc(w_split, 1)
            choose(0)

            def body(c, k, odd, first, last):
                for j in range(SFF):
                    gated(c, j)
                    if j == 2:
                        queue_places(c)
                    if j == 3:
                        drop_full(c)
                    if j == 4:
                        six_slots(c, k, odd)
                    if j == 5:
                        weights(c, k, odd)
                if not last:
                    copy_x(c + 1)
                add_shared(c, k, odd, 0)
                if not last:
                    choose(c + 1)
                add_shared(c, k, odd, 1)

            chunks(dve, body)


def experts_phase(nc, S, w_gate_up, w_down, t_ident, t_split, hx, acc, slot_token):
    from contextlib import ExitStack

    D, E, FT, FF, H = S.dim, S.experts, S.ff_tile, S.ff, S.third
    ST = CAP // 2

    with ExitStack() as ctx:
        def sb(name, shape, dt=F32):
            return ctx.enter_context(nc.sbuf_tensor(name, shape, dt))

        def bank(name):
            return ctx.enter_context(nc.psum_tensor(name, [P, 512], F32))

        def sem(name):
            return ctx.enter_context(nc.semaphore(name))

        ident = sb("c_ident", [P, P])
        split = sb("c_split", [P, 2])
        raw = [sb(f"c_raw{i}", [P, 2, 2 * S.inner]) for i in range(2)]
        w_gu = [sb(f"c_w_gu{i}", [P, 2, 2, 2 * S.inner], F32R) for i in range(2)]
        w_d = [sb(f"c_w_d{i}", [FT, FF, D]) for i in range(2)]
        token = [sb(f"c_token{i}", [ST, 2], I32) for i in range(4)]
        rows = [sb(f"c_rows{i}", [ST, 2, S.row]) for i in range(4)]
        rest = sb("c_rest", [ST, 2, 2, H])
        xT = sb("c_xT", [P, 3, CAP], F32R)
        high = sb("c_high", [P, CAP])
        silu_g = [sb(f"c_silu{i}", [FT, CAP]) for i in range(2)]
        inter = sb("c_inter", [FT, FF, CAP])
        y = [sb(f"c_y{i}", [ST, 2, D]) for i in range(2)]

        x_b = bank("c_x")
        gu_b = [bank(f"c_gu{i}") for i in range(4)]
        y_b = [bank("c_down0"), bank("c_down1")]

        ident_in = sem("c_ident_in")
        gu_in = [sem("c_gu_in0"), sem("c_gu_in1")]
        d_in = [sem("c_d_in0"), sem("c_d_in1")]
        token_in = [sem(f"c_token_in{i}") for i in range(4)]
        gathered = [sem(f"c_gathered{i}") for i in range(4)]
        rest_ready, x_turned, x_high, xT_ready = (sem("c_rest_ready"), sem("c_x_turned"), sem("c_x_high"),
                                                  sem("c_xT_ready"))
        w_high, w_low = sem("c_w_high"), sem("c_w_low")
        up_done, silu_ready, inter_ready = sem("c_up_done"), sem("c_silu_ready"), sem("c_inter_ready")
        down_done, y_ready = sem("c_down_done"), sem("c_y_ready")
        added = [sem(f"c_added{i}") for i in range(4)]

        pool_passed, dve_passed = sem("c_pool_passed"), sem("c_dve_passed")
        block = ctx.enter_context(nc.Block())

        def experts(eng, body):
            for i in range(4):
                body(i, 0, i, i == 0, E == i + 1)
            if E > 8:
                with eng.Fori(1, E // 4 - 1) as k:
                    for i in range(4):
                        body(k * 4 + i, k, i, False, False)
            k = E // 4 - 1
            for i in range(4):
                body(4 * k + i, k, i, False, i == 3)

        def beyond(e, ahead):
            return isinstance(e, int) and e + ahead >= E

        def wait_added(eng, k, i, back, passed=None):
            j = i - back
            if passed is None:
                at_least(eng, added[j % 4], 32 * (k + 1 + j // 4))
            else:
                hold(eng, passed, added[j % 4], 32 * (k + 1 + j // 4))

        @block.sync
        def _(sp):
            sp.dma_start(ident[:], t_ident).then_inc(ident_in, 16)
            sp.dma_start(split[:], t_split).then_inc(ident_in, 16)

            def load_token(e, i):
                sp.dma_start(token[i][:], slot_token[bass.ds(e * CAP, CAP), :].rearrange("(p t) a -> p (t a)", t=2))\
                  .then_inc(token_in[i], 16)

            def load_up(e, i):
                sp.dma_start(raw[i][:, 0, :], w_gate_up[e][0:P, :]).then_inc(gu_in[i], 16)
                sp.dma_start(raw[i][0:H, 1, :], w_gate_up[e][P:D, :]).then_inc(gu_in[i], 16)

            def load_down(e, i):
                sp.dma_start(w_d[i][:], w_down[e].rearrange("(j p) n -> p j n", p=FT)).then_inc(d_in[i], 16)

            for e in range(3):
                load_token(e, e)
            for e in range(2):
                load_up(e, e)
                load_down(e, e)

            def body(e, k, i, first, last):
                if not beyond(e, 2):
                    sp.wait_ge(w_low, 3 * (e + 1))
                    load_up(e + 2, i % 2)
                if not beyond(e, 3):
                    wait_added(sp, k, i, 1)
                    load_token(e + 3, (i + 3) % 4)
                if not beyond(e, 2):
                    sp.wait_ge(down_done, e + 1)
                    load_down(e + 2, i % 2)

            experts(sp, body)
            for i in range(4):
                sp.wait_ge(added[i], 32 * (E // 4))

        @block.gpsimd
        def _(pool):
            def gather(e, k, i):
                hold(pool, pool_passed, token_in[i], 16 * (k + 1))
                hold(pool, pool_passed, y_ready, e - 3)
                for t in range(2):
                    pool.indirect_dma_start(rows[i][:, t, :], None, hx,
                                            bass.IndirectOffsetOnAxis(ap=token[i][:, t:t + 1], axis=0))\
                        .then_inc(gathered[i], 16)

            gather(0, 0, 0)
            gather(1, 0, 1)

            def body(e, k, i, first, last):
                if not beyond(e, 2):
                    gather(e + 2, k + (i + 2) // 4, (i + 2) % 4)
                hold(pool, pool_passed, y_ready, e + 1)
                wait_added(pool, k, i, 1, pool_passed)
                for t in range(2):
                    pool.indirect_dma_start(acc, bass.IndirectOffsetOnAxis(ap=token[i][:, t:t + 1], axis=0),
                                            y[i % 2][:, t, :], None, compute_op=ALU.add).then_inc(added[i], 16)

            experts(pool, body)

        @block.tensor
        def _(pe):
            pe.wait_ge(ident_in, 32)

            def turn(e, k, i):
                pe.wait_ge(gathered[i], 32 * (k + 1))
                pe.wait_ge(rest_ready, e + 1)
                for t in range(2):
                    pe.transpose(x_b[:, t * ST:(t + 1) * ST], rows[i][:, t, 0:P], ident[0:ST, 0:ST])
                    mm = pe.transpose(x_b[:, CAP + t * ST:CAP + (t + 1) * ST],
                                      rest[:, t, :, :].rearrange("p a d -> p (a d)"), ident[0:ST, 0:ST])
                mm.then_inc(x_turned, 1)

            turn(0, 0, 0)

            def body(e, k, i, first, last):
                k2 = k * 2 + i // 2
                pe.wait_ge(xT_ready, 2 * (e + 1))
                pe.wait_ge(w_low, 3 * (e + 1))
                for j in range(FF):
                    at_least(pe, inter_ready, (e - 1) * FF + j + 1)
                    for w in range(2):
                        c = w * S.inner + j * FT
                        for n, (x, kt, part) in enumerate(PRODUCTS):
                            mm = pe.matmul(gu_b[j][0:FT, w * CAP:(w + 1) * CAP], w_gu[i % 2][:, kt, part, c:c + FT],
                                           xT[:, x, :], start=(n == 0), stop=(n == len(PRODUCTS) - 1))
                    mm.then_inc(up_done, 1)
                if not last:
                    turn(e + 1, k + (i + 1) // 4, (i + 1) % 4)
                pe.wait_ge(d_in[i % 2], 16 * (k2 + 1))
                at_least(pe, y_ready, e - 1)
                for t in range(2):
                    for j in range(FF):
                        if t == 0:
                            pe.wait_ge(inter_ready, e * FF + j + 1)
                        mm = pe.matmul(y_b[i % 2][0:ST, t * D:(t + 1) * D], inter[:, j, t * ST:(t + 1) * ST],
                                       w_d[i % 2][:, j, :], start=(j == 0), stop=(j == FF - 1))
                mm.then_inc(down_done, 1)

            experts(pe, body)

        @block.scalar
        def _(act):
            act.wait_ge(ident_in, 32)

            def split_high(e, k2, i, piece):
                if piece == 0:
                    act.wait_ge(gu_in[i], 32 * (k2 + 1))
                    at_least(act, up_done, (e - 1) * FF)
                out, src = ((w_gu[i][:, 0, 0, :], raw[i][:, 0, :]), (w_gu[i][0:H, 1, 0, :], raw[i][0:H, 1, :]),
                            (w_gu[i][H:2 * H, 1, 0, :], raw[i][0:H, 1, :]))[piece]
                act.activation(out, src, ACT.Copy).then_inc(w_high, 1)

            def copy_x(e):
                act.wait_ge(x_turned, e + 1)
                act.activation(xT[:, 0, :], x_b[:, 0:CAP], ACT.Copy).then_inc(x_high, 1)
                at_least(act, xT_ready, 2 * e)
                act.activation(high.bitcast(F32R)[:], x_b[:, CAP:2 * CAP], ACT.Copy, scale=split[:, 0:1])\
                   .then_inc(x_high, 1)

            for piece in range(3):
                split_high(0, 0, 0, piece)
            copy_x(0)

            def body(e, k, i, first, last):
                for j in range(FF):
                    if j < 3 and not last:
                        split_high(e + 1, k * 2 + (i + 1) // 2, (i + 1) % 2, j)
                    act.wait_ge(up_done, e * FF + j + 1)
                    at_least(act, inter_ready, e * FF + j - 1)
                    act.activation(silu_g[j % 2][:], gu_b[j][0:FT, 0:CAP], ACT.Silu).then_inc(silu_ready, 1)
                if not last:
                    copy_x(e + 1)

            experts(act, body)

        @block.vector
        def _(dve):
            dve.wait_ge(ident_in, 32)

            def split_low(e, i, piece):
                dve.wait_ge(w_high, 3 * e + piece + 1)
                rows_out = (slice(0, P), slice(0, H), slice(H, 2 * H))[piece]
                rows_in = slice(0, P) if piece == 0 else slice(0, H)
                kt = min(piece, 1)
                dve.tensor_tensor(w_gu[i][rows_out, kt, 1, :], raw[i][rows_in, kt, :],
                                  w_gu[i][rows_in, kt, 0, :].bitcast(F32), ALU.subtract).then_inc(w_low, 1)

            def repeat_rest(e, k, i):
                dve.wait_ge(gathered[i], 32 * (k + 1))
                at_least(dve, x_turned, e)
                dve.tensor_copy(rest[:], repeat(rows[i][:, :, P:D], 2, 2)).then_inc(rest_ready, 1)

            def copy_x(e):
                dve.wait_ge(x_high, 2 * e + 2)
                dve.tensor_tensor(xT[:, 2, :], x_b[:, 0:CAP], xT[:, 0, :].bitcast(F32), ALU.subtract)\
                   .then_inc(xT_ready, 1)
                dve.scalar_tensor_tensor(out=xT[:, 1, :], in0=x_b[:, CAP:2 * CAP], scalar=split[:, 1:2], in1=high[:],
                                         op0=ALU.mult, op1=ALU.subtract).then_inc(xT_ready, 1)

            repeat_rest(0, 0, 0)
            for piece in range(3):
                split_low(0, 0, piece)
            copy_x(0)

            def body(e, k, i, first, last):
                for j in range(FF):
                    if j == 0 and not last:
                        repeat_rest(e + 1, k + (i + 1) // 4, (i + 1) % 4)
                    dve.wait_ge(silu_ready, e * FF + j + 1)
                    at_least(dve, down_done, e)
                    dve.tensor_tensor(inter[:, j, :], silu_g[j % 2][:], gu_b[j][0:FT, CAP:2 * CAP], ALU.mult)\
                       .then_inc(inter_ready, 1)
                    if j in (0, 1) and not last:
                        split_low(e + 1, (i + 1) % 2, j)
                if not last:
                    copy_x(e + 1)
                    split_low(e + 1, (i + 1) % 2, 2)
                dve.wait_ge(down_done, e + 1)
                wait_added(dve, k, i, 2)
                for t in range(2):
                    op = dve.tensor_scalar(y[i % 2][:, t, :], y_b[i % 2][0:ST, t * D:(t + 1) * D],
                                           rows[i][:, t, bass.ds(e + D, 1)], None, ALU.mult)
                op.then_inc(y_ready, 1)

            experts(dve, body)


def final_phase(nc, S, acc, out):
    from contextlib import ExitStack

    D, B, J = S.dim, S.images, 8
    STEPS = S.seq // J
    REST = S.seq - STEPS * J
    BUFS = 4
    SHARE = 2

    with ExitStack() as ctx:
        def sb(name, shape, dt=F32):
            return ctx.enter_context(nc.sbuf_tensor(name, shape, dt))

        def sem(name):
            return ctx.enter_context(nc.semaphore(name))

        rows = [sb(f"d_rows{i}", [B, J, D]) for i in range(BUFS)]
        norm = [sb(f"d_norm{i}", [B, J, D]) for i in range(BUFS)]
        stats = [sb(f"d_stats{i}", [B, J, 6]) for i in range(2)]
        moments = [sb(f"d_moments{i}", [B, J, 2]) for i in range(BUFS)]
        rstd = [sb(f"d_rstd{i}", [B, J]) for i in range(BUFS)]
        shift = [sb(f"d_shift{i}", [B, J]) for i in range(BUFS)]
        minus_half = sb("d_minus_half", [B, J])

        half_set = sem("d_half_set")
        rows_in = [sem(f"d_rows_in{i}") for i in range(BUFS)]
        out_done = [sem(f"d_out{i}") for i in range(BUFS)]
        stats_ready, moments_ready, rstd_step = sem("d_stats_ready"), sem("d_moments_ready"), sem("d_rstd_step")
        dve_norm, act_norm = sem("d_dve_norm"), sem("d_act_norm")

        pool_passed, dve_passed = sem("d_pool_passed"), sem("d_dve_passed")
        block = ctx.enter_context(nc.Block())
        acc_v = acc[0:S.tokens, :].rearrange("(b s) d -> b s d", s=S.seq)

        def groups(eng, body):
            for i in range(BUFS):
                body(i, 0, i, J)
            with eng.Fori(1, STEPS // BUFS - 1) as k:
                for i in range(BUFS):
                    body(k * BUFS + i, k, i, J)
            for s in range((STEPS // BUFS - 1) * BUFS, STEPS + 1):
                body(s, s // BUFS, s % BUFS, REST if s == STEPS else J)

        @block.sync
        def _(sp):
            def load(s, i, count):
                sp.dma_start(rows[i][:, 0:count, :], acc_v[:, bass.ds(s * J, count), :]).then_inc(rows_in[i], 16)

            for s in range(3):
                load(s, s, J)

            def body(s, k, i, count):
                if not (isinstance(s, int) and s + 3 > STEPS):
                    at_least(sp, dve_norm, s)
                    at_least(sp, act_norm, s)
                    load(s + 3, (i + 3) % BUFS, REST if isinstance(s, int) and s + 3 == STEPS else J)
                sp.wait_ge(dve_norm, s + 1)
                sp.wait_ge(act_norm, s + 1)
                sp.dma_start(out[:, bass.ds(s * J, count), :], norm[i][:, 0:count, :]).then_inc(out_done[i], 16)

            groups(sp, body)
            for i in range(BUFS):
                sp.wait_ge(out_done[i], 16 * ((STEPS + BUFS - i) // BUFS))

        @block.gpsimd
        def _(pool):
            pool.memset(minus_half[:], -0.5).then_inc(half_set, 1)
            hold(pool, pool_passed, half_set, 1)

            def body(s, k, i, count):
                hold(pool, pool_passed, moments_ready, s + 1)
                hold(pool, pool_passed, act_norm, s - 3)
                hold(pool, pool_passed, dve_norm, s - 3)
                pool.tensor_scalar(rstd[i][:, 0:count], moments[i][:, 0:count, 1], LN_EPS, None, ALU.add)\
                    .then_inc(rstd_step, 1)
                pool.tensor_scalar(shift[i][:, 0:count], moments[i][:, 0:count, 0], -1.0, None, ALU.mult)\
                    .then_inc(rstd_step, 1)
                hold(pool, pool_passed, rstd_step, 4 * s + 2)
                pool.tensor_tensor(rstd[i][:, 0:count], rstd[i][:, 0:count], minus_half[:, 0:count], ALU.pow)\
                    .then_inc(rstd_step, 1)
                hold(pool, pool_passed, rstd_step, 4 * s + 3)
                pool.tensor_tensor(shift[i][:, 0:count], shift[i][:, 0:count], rstd[i][:, 0:count], ALU.mult)\
                    .then_inc(rstd_step, 1)

            groups(pool, body)

        @block.scalar
        def _(act):
            def body(s, k, i, count):
                act.wait_ge(rstd_step, 4 * s + 4)
                at_least(act, out_done[i], 16 * k)
                for j in range(SHARE, count):
                    op = act.activation(norm[i][:, j, :], rows[i][:, j, :], ACT.Identity, bias=shift[i][:, j:j + 1],
                                        scale=rstd[i][:, j:j + 1])
                op.then_inc(act_norm, 1)

            groups(act, body)

        @block.vector
        def _(dve):
            def measure(s, k, i, count):
                dve.wait_ge(rows_in[i], 16 * (k + 1))
                at_least(dve, moments_ready, s - 1)
                for j in range(count):
                    op = dve.bn_stats(stats[i % 2][:, j, :], rows[i][:, j, :])
                op.then_inc(stats_ready, 1)
                hold(dve, dve_passed, stats_ready, s + 1)
                hold(dve, dve_passed, rstd_step, 4 * (s - 3))
                for j in range(count):
                    op = dve.bn_aggr(moments[i][:, j, :], stats[i % 2][:, j, :])
                op.then_inc(moments_ready, 1)

            def apply(s, k, i, count):
                dve.wait_ge(rstd_step, 4 * s + 4)
                at_least(dve, out_done[i], 16 * k)
                for j in range(SHARE):
                    op = dve.tensor_scalar(norm[i][:, j, :], rows[i][:, j, :], moments[i][:, j, 0:1],
                                           rstd[i][:, j:j + 1], ALU.subtract, ALU.mult)
                op.then_inc(dve_norm, 1)

            def body(s, k, i, count):
                if not (isinstance(s, int) and s == STEPS):
                    measure(s + 1, k + (i + 1) // BUFS, (i + 1) % BUFS,
                            REST if isinstance(s, int) and s + 1 == STEPS else J)
                apply(s, k, i, count)

            measure(0, 0, 0, J)
            groups(dve, body)


def vit_tower_moe_kernel(nc, S, x, tok_w, tok_b, pos, cls, w_qkv, w_proj, b_proj, wg, e_bias, w_gate_up, w_down,
                         wsg, wsu, wsd, t, out):
    hx = nc.dram_tensor("hx_scratch", [S.all_rows, S.row], F32, kind="Internal").ap()
    acc = nc.dram_tensor("acc_scratch", [S.all_rows, S.dim], F32, kind="Internal").ap()
    slot_token = nc.dram_tensor("slot_token_scratch", [S.slots, 1], I32, kind="Internal").ap()
    attention_phase(nc, S, x, tok_w, tok_b, pos, cls, w_qkv, w_proj, b_proj, t["ident"], t["cos"], t["sin"],
                    t["split"], t["vmask"], hx, acc, slot_token, t["empty"])
    routing_phase(nc, S, wg, e_bias, wsg, wsu, wsd, t["ident"], t["split_x"], t["before"], t["slot_base"], t["slot_limit"],
                  t["token_id"], hx, acc, slot_token)
    experts_phase(nc, S, w_gate_up, w_down, t["ident"], t["split_x"], hx, acc, slot_token)
    final_phase(nc, S, acc, out)


_INS = ['x', 'L0_tok_W', 'L0_tok_b', 'L0_tok_pos_table', 'L0_tok_class_token', 'L0_attn_w_qkv', 'L0_attn_w_proj',
        'L0_attn_b_proj', 'L0_ffn_Wg', 'L0_ffn_e_bias', 'L0_ffn_W_gate_up', 'L0_ffn_W_down', 'L0_ffn_Wsg',
        'L0_ffn_Wsu', 'L0_ffn_Wsd']


def kernel(**inputs):
    import numpy as _np
    import concourse.bacc as _bacc
    from concourse import mybir as _mybir
    from concourse.bass_utils import run_bass_kernel_spmd as _run

    nc = _bacc.Bacc("TRN2", target_bir_lowering=False, num_devices=1)
    arrays, args = {}, []
    for name in _INS:
        a = _np.ascontiguousarray(inputs[name])
        arrays[f"in_{name}_dram"] = a
        args.append(nc.dram_tensor(f"in_{name}_dram", a.shape, _mybir.dt.from_np(a.dtype), kind="ExternalInput").ap())
    S = Shapes(inputs["x"], inputs["L0_tok_W"], inputs["L0_tok_pos_table"], inputs["L0_ffn_Wg"],
               inputs["L0_ffn_W_gate_up"], inputs["L0_ffn_Wsg"])
    consts = {}
    for name, a in tables(S).items():
        arrays[f"const_{name}_dram"] = a
        consts[name] = nc.dram_tensor(f"const_{name}_dram", a.shape, _mybir.dt.from_np(a.dtype),
                                      kind="ExternalInput").ap()
    out = nc.dram_tensor("out_0_dram", (S.images, S.seq, S.dim), F32, kind="ExternalOutput").ap()
    vit_tower_moe_kernel(nc, S, *args, consts, out)
    r = _run(nc, [arrays], core_ids=[0])
    return r.results[0]["out_0_dram"]
```
